# Optimizing a Trainium2 kernel written in Bass

```python
import numpy as np
import jax
import jax.numpy as jnp

def _softmax(x, axis=-1):
    return jax.nn.softmax(x, axis=axis)

def _gelu(x):
    return jax.nn.gelu(x, approximate=True)

def _silu(x):
    return jax.nn.silu(x)

def _sigmoid(x):
    return jax.nn.sigmoid(x)

def _layernorm(x, axis=-1, eps=1e-05):
    m = jnp.mean(x, axis=axis, keepdims=True)
    v = jnp.var(x, axis=axis, keepdims=True)
    return (x - m) / jnp.sqrt(v + eps)

def _scatter_add(tgt, idx, src, axis=0):
    return tgt.at[idx].add(src)

def _segment_sum(src, seg, n):
    return jax.ops.segment_sum(src, seg, n)
kernel_name = 'mk_xattn_ffn_d2_seqx_r8_a045a7'

def setup_inputs(seed: int=0):
    np.random.seed(seed)
    _w = jnp.asarray

    def _rec_inputs():
        import jax
        import jax.numpy as jnp
        _rk = jax.random.key(seed)
        x = -0.0005207 + 1.001 * jax.random.normal(jax.random.fold_in(_rk, 1), (4, 256, 512), jnp.float32)
        _lenS = 256 - jax.random.randint(jax.random.fold_in(_rk, 7), (4,), 0, max(1, 256 // 4) + 1, jnp.int32)
        _lenS2 = 1601 - jax.random.randint(jax.random.fold_in(_rk, 8), (4,), 0, max(1, 1601 // 4) + 1, jnp.int32)
        _ctx_4096P = jax.random.normal(jax.random.fold_in(_rk, 11), (4, 16, 512), jnp.float32)
        _ctx_4096c = jax.random.dirichlet(jax.random.fold_in(_rk, 511), 0.3 * jnp.ones((16,), jnp.float32), (4, 1601))
        _ctx_4096t = jnp.einsum('bsk,bkd->bsd', _ctx_4096c, _ctx_4096P)
        _ctx_4096t = _ctx_4096t * jax.lax.rsqrt(jnp.mean(jnp.square(_ctx_4096t)) + 1e-12) * 0.953939
        ctx_4096 = -0.00010331 + 0.999899 * (_ctx_4096t + 0.3 * jax.random.normal(jax.random.fold_in(_rk, 611), (4, 1601, 512), jnp.float32))
        return (x, ctx_4096)
    x, ctx_4096 = _rec_inputs()

    def _L0_xattn_setup():
        import jax, jax.numpy as jnp
        import numpy as np
        import math
        HIDDEN = 512
        N_HEADS = 32
        HEAD_DIM = 128
        N_KV_HEADS = 4
        N_GROUPS = N_HEADS // N_KV_HEADS
        key = jax.random.key(seed)
        ks = jax.random.split(key, 6)
        B, NL, S = (8, 64, 512)
        latents = jax.random.normal(ks[0], (B, NL, HIDDEN), dtype=jnp.float32)
        context = jax.random.normal(ks[1], (B, S, HIDDEN), dtype=jnp.float32)
        scale = 1.0 / math.sqrt(HIDDEN)
        Wq = jax.random.normal(ks[2], (HIDDEN, N_HEADS * HEAD_DIM), dtype=jnp.float32) * scale
        Wk = jax.random.normal(ks[3], (HIDDEN, N_KV_HEADS * HEAD_DIM), dtype=jnp.float32) * scale
        Wv = jax.random.normal(ks[4], (HIDDEN, N_KV_HEADS * HEAD_DIM), dtype=jnp.float32) * scale
        Wo = jax.random.normal(ks[5], (N_HEADS * HEAD_DIM, HIDDEN), dtype=jnp.float32) * scale
        return {'latents': latents, 'context': context, 'Wq': Wq, 'Wk': Wk, 'Wv': Wv, 'Wo': Wo}
    _L0_xattn_all = _L0_xattn_setup()
    _L0_xattn_in = {k: v for k, v in _L0_xattn_all.items() if k in ('Wq', 'Wk', 'Wv', 'Wo')}
    del _L0_xattn_all

    def _L0_ffn_setup():
        import jax, jax.numpy as jnp
        import numpy as np
        B, S, D = (4, 256, 512)
        NUM_EXPERTS, TOP_K = (3, 2)

        def _expert_outputs(h, w1, b1, w2, b2):
            pre = jnp.einsum('bsd,edf->ebsf', h, w1) + b1[:, None, None, :]
            act = jnp.stack([jnp.tanh(pre[0]), jax.nn.gelu(pre[1], approximate=False), jax.nn.silu(pre[2])])
            return jnp.einsum('ebsf,efd->ebsd', act, w2) + b2[:, None, None, :]
        key = jax.random.key(seed)
        ks = jax.random.split(key, 8)
        scale_in = 1.0 / np.sqrt(D)
        scale_gate = 1.0 / np.sqrt(D + 1)
        return {'h': jax.random.normal(ks[0], (B, S, D), dtype=jnp.float32), 'gate_w': jax.random.uniform(ks[1], (D + 1, NUM_EXPERTS), minval=-scale_gate, maxval=scale_gate, dtype=jnp.float32), 'gate_b': jnp.zeros((NUM_EXPERTS,), dtype=jnp.float32), 'w1': jax.random.uniform(ks[2], (NUM_EXPERTS, D, D), minval=-scale_in, maxval=scale_in, dtype=jnp.float32), 'b1': jnp.zeros((NUM_EXPERTS, D), dtype=jnp.float32), 'w2': jax.random.uniform(ks[3], (NUM_EXPERTS, D, D), minval=-scale_in, maxval=scale_in, dtype=jnp.float32), 'b2': jnp.zeros((NUM_EXPERTS, D), dtype=jnp.float32)}
    _L0_ffn_all = _L0_ffn_setup()
    _L0_ffn_in = {k: v for k, v in _L0_ffn_all.items() if k in ('gate_w', 'gate_b', 'w1', 'b1', 'w2', 'b2')}
    del _L0_ffn_all

    def _L1_xattn_setup():
        import jax, jax.numpy as jnp
        import numpy as np
        EPS = 1e-06

        def rmsnorm(x, w):
            xf = x.astype(jnp.float32)
            var = jnp.mean(xf * xf, axis=-1, keepdims=True)
            return (xf * jax.lax.rsqrt(var + EPS)).astype(x.dtype) * w
        key = jax.random.key(seed)
        ks = jax.random.split(key, 6)
        B, T, S, Dt, Df = (4, 128, 72, 512, 512)
        text = jax.random.normal(ks[0], (B, T, Dt), dtype=jnp.float32)
        features = jax.random.normal(ks[1], (B, S, Df), dtype=jnp.float32)
        lim_q = float(np.sqrt(6.0 / (Dt + Df)))
        lim_k = float(np.sqrt(6.0 / (Df + Df)))
        Wq_w = jax.random.uniform(ks[2], (Df, Dt), minval=-lim_q, maxval=lim_q, dtype=jnp.float32)
        Wk_w = jax.random.uniform(ks[3], (Df, Df), minval=-lim_k, maxval=lim_k, dtype=jnp.float32)
        bq = 1.0 / np.sqrt(Dt)
        bk = 1.0 / np.sqrt(Df)
        Wq_b = jax.random.uniform(ks[4], (Df,), minval=-bq, maxval=bq, dtype=jnp.float32)
        Wk_b = jax.random.uniform(ks[5], (Df,), minval=-bk, maxval=bk, dtype=jnp.float32)
        fn_w = jnp.ones((Df,), dtype=jnp.float32)
        qn_w = jnp.ones((Df,), dtype=jnp.float32)
        kn_w = jnp.ones((Df,), dtype=jnp.float32)
        return {'text': text, 'features': features, 'Wq_w': Wq_w, 'Wq_b': Wq_b, 'Wk_w': Wk_w, 'Wk_b': Wk_b, 'fn_w': fn_w, 'qn_w': qn_w, 'kn_w': kn_w}
    _L1_xattn_all = _L1_xattn_setup()
    _L1_xattn_in = {k: v for k, v in _L1_xattn_all.items() if k in ('Wq_w', 'Wq_b', 'Wk_w', 'Wk_b', 'fn_w', 'qn_w', 'kn_w')}
    del _L1_xattn_all

    def _L1_ffn_setup():
        import jax, jax.numpy as jnp
        import numpy as np
        HIDDEN = 512
        MOE_INTER = 128
        SHARED_INTER = 512
        NUM_EXPERTS = 16
        TOP_K = 2

        def _moe_forward(x, gate_w, w_gate_up, w_down, shared_w_gate_up, shared_w_down):
            orig_shape = x.shape
            x2 = x.reshape(-1, orig_shape[-1])
            gu_s = x2 @ shared_w_gate_up.T
            g_s, u_s = jnp.split(gu_s, 2, axis=-1)
            shared_out = jax.nn.silu(g_s) * u_s @ shared_w_down.T
            logits = x2 @ gate_w.T
            probs = jax.nn.softmax(logits, axis=-1)
            topk_vals, topk_idx = jax.lax.top_k(probs, TOP_K)
            topk_vals = topk_vals / jnp.sum(topk_vals, axis=-1, keepdims=True)
            combine = jnp.sum(jax.nn.one_hot(topk_idx, NUM_EXPERTS, dtype=x2.dtype) * topk_vals[..., None], axis=1)
            gu = jnp.einsum('th,eih->eti', x2, w_gate_up)
            g, u = jnp.split(gu, 2, axis=-1)
            act = jax.nn.silu(g) * u
            out_e = jnp.einsum('eti,ehi->eth', act, w_down)
            moe_out = jnp.einsum('eth,te->th', out_e, combine)
            return (moe_out + shared_out).reshape(orig_shape)
        key = jax.random.key(seed)
        ks = jax.random.split(key, 6)
        s = 0.02
        hidden_states = jax.random.normal(ks[0], (2, 256, HIDDEN), dtype=jnp.float32)
        gate_w = jax.random.normal(ks[1], (NUM_EXPERTS, HIDDEN), dtype=jnp.float32) * s
        w_gate_up = jax.random.normal(ks[2], (NUM_EXPERTS, 2 * MOE_INTER, HIDDEN), dtype=jnp.float32) * s
        w_down = jax.random.normal(ks[3], (NUM_EXPERTS, HIDDEN, MOE_INTER), dtype=jnp.float32) * s
        shared_w_gate_up = jax.random.normal(ks[4], (2 * SHARED_INTER, HIDDEN), dtype=jnp.float32) * s
        shared_w_down = jax.random.normal(ks[5], (HIDDEN, SHARED_INTER), dtype=jnp.float32) * s
        return {'hidden_states': hidden_states, 'gate_w': gate_w, 'w_gate_up': w_gate_up, 'w_down': w_down, 'shared_w_gate_up': shared_w_gate_up, 'shared_w_down': shared_w_down}
    _L1_ffn_all = _L1_ffn_setup()
    _L1_ffn_in = {k: v for k, v in _L1_ffn_all.items() if k in ('gate_w', 'w_gate_up', 'w_down', 'shared_w_gate_up', 'shared_w_down')}
    del _L1_ffn_all
    return {'x': x, 'ctx_4096': ctx_4096, 'L0_xattn_Wq': _L0_xattn_in['Wq'], 'L0_xattn_Wk': _L0_xattn_in['Wk'], 'L0_xattn_Wv': _L0_xattn_in['Wv'], 'L0_xattn_Wo': _L0_xattn_in['Wo'], 'L0_ffn_gate_w': _L0_ffn_in['gate_w'], 'L0_ffn_gate_b': _L0_ffn_in['gate_b'], 'L0_ffn_w1': _L0_ffn_in['w1'], 'L0_ffn_b1': _L0_ffn_in['b1'], 'L0_ffn_w2': _L0_ffn_in['w2'], 'L0_ffn_b2': _L0_ffn_in['b2'], 'L1_xattn_Wq_w': _L1_xattn_in['Wq_w'], 'L1_xattn_Wq_b': _L1_xattn_in['Wq_b'], 'L1_xattn_Wk_w': _L1_xattn_in['Wk_w'], 'L1_xattn_Wk_b': _L1_xattn_in['Wk_b'], 'L1_xattn_fn_w': _L1_xattn_in['fn_w'], 'L1_xattn_qn_w': _L1_xattn_in['qn_w'], 'L1_xattn_kn_w': _L1_xattn_in['kn_w'], 'L1_ffn_gate_w': _L1_ffn_in['gate_w'], 'L1_ffn_w_gate_up': _L1_ffn_in['w_gate_up'], 'L1_ffn_w_down': _L1_ffn_in['w_down'], 'L1_ffn_shared_w_gate_up': _L1_ffn_in['shared_w_gate_up'], 'L1_ffn_shared_w_down': _L1_ffn_in['shared_w_down']}

def reference(x, ctx_4096, L0_xattn_Wq, L0_xattn_Wk, L0_xattn_Wv, L0_xattn_Wo, L0_ffn_gate_w, L0_ffn_gate_b, L0_ffn_w1, L0_ffn_b1, L0_ffn_w2, L0_ffn_b2, L1_xattn_Wq_w, L1_xattn_Wq_b, L1_xattn_Wk_w, L1_xattn_Wk_b, L1_xattn_fn_w, L1_xattn_qn_w, L1_xattn_kn_w, L1_ffn_gate_w, L1_ffn_w_gate_up, L1_ffn_w_down, L1_ffn_shared_w_gate_up, L1_ffn_shared_w_down):
    import jax
    import jax.numpy as jnp

    def _L0_xattn_ref(latents, context, Wq, Wk, Wv, Wo):
        import jax, jax.numpy as jnp
        import numpy as np
        import math
        HIDDEN = 512
        N_HEADS = 32
        HEAD_DIM = 128
        N_KV_HEADS = 4
        N_GROUPS = N_HEADS // N_KV_HEADS
        b, q_len, _ = latents.shape
        kv_len = q_len + context.shape[1]
        hidden_states = jnp.concatenate([context, latents], axis=1)
        q = (latents @ Wq).reshape(b, q_len, N_KV_HEADS, N_GROUPS, HEAD_DIM)
        k = (hidden_states @ Wk).reshape(b, kv_len, N_KV_HEADS, HEAD_DIM)
        v = (hidden_states @ Wv).reshape(b, kv_len, N_KV_HEADS, HEAD_DIM)
        scale = 1.0 / math.sqrt(HEAD_DIM)
        scores = jnp.einsum('bqhgd,bkhd->bhgqk', q, k) * scale
        attn = jax.nn.softmax(scores.astype(jnp.float32), axis=-1).astype(q.dtype)
        out = jnp.einsum('bhgqk,bkhd->bqhgd', attn, v)
        out = out.reshape(b, q_len, N_HEADS * HEAD_DIM)
        return out @ Wo

    def _L0_ffn_ref(h, gate_w, gate_b, w1, b1, w2, b2):
        import jax, jax.numpy as jnp
        import numpy as np
        B, S, D = (4, 256, 512)
        NUM_EXPERTS, TOP_K = (3, 2)

        def _expert_outputs(h, w1, b1, w2, b2):
            pre = jnp.einsum('bsd,edf->ebsf', h, w1) + b1[:, None, None, :]
            act = jnp.stack([jnp.tanh(pre[0]), jax.nn.gelu(pre[1], approximate=False), jax.nn.silu(pre[2])])
            return jnp.einsum('ebsf,efd->ebsd', act, w2) + b2[:, None, None, :]
        b, s, d = h.shape
        vision_len = int(s * 0.3)
        text_strength = jnp.mean(jnp.abs(h[:, vision_len:, :]), axis=(1, 2), keepdims=True)
        vision_strength = jnp.mean(jnp.abs(h[:, :vision_len, :]), axis=(1, 2), keepdims=True)
        modality_ratio = text_strength / (vision_strength + 1e-08)
        modality_ratio = jnp.broadcast_to(modality_ratio, (b, s, 1))
        router_input = jnp.concatenate([h, modality_ratio], axis=-1)
        gate_logits = router_input @ gate_w + gate_b
        gate_scores = jax.nn.softmax(gate_logits, axis=-1)
        top_val, top_idx = jax.lax.top_k(gate_scores, TOP_K)
        top_val = top_val / (jnp.sum(top_val, axis=-1, keepdims=True) + 1e-08)
        expert_out = _expert_outputs(h, w1, b1, w2, b2)
        moe_out = jnp.zeros_like(h)
        batch_idx = jnp.arange(b)
        for i in range(TOP_K):
            j = top_idx[:, 0, i]
            out_i = expert_out[j, batch_idx]
            moe_out = moe_out + top_val[..., i:i + 1] * out_i
        return moe_out

    def _L1_xattn_ref(text, features, Wq_w, Wq_b, Wk_w, Wk_b, fn_w, qn_w, kn_w):
        import jax, jax.numpy as jnp
        import numpy as np
        EPS = 1e-06

        def rmsnorm(x, w):
            xf = x.astype(jnp.float32)
            var = jnp.mean(xf * xf, axis=-1, keepdims=True)
            return (xf * jax.lax.rsqrt(var + EPS)).astype(x.dtype) * w
        features_n = rmsnorm(features, fn_w)
        Q = jnp.einsum('btd,fd->btf', text, Wq_w) + Wq_b
        K = jnp.einsum('bsd,fd->bsf', features_n, Wk_w) + Wk_b
        Q = rmsnorm(Q, qn_w)
        K = rmsnorm(K, kn_w)
        scale = 1.0 / jnp.sqrt(jnp.asarray(K.shape[-1], dtype=Q.dtype))
        scores = jnp.einsum('btf,bsf->bts', Q, K) * scale
        attn = jax.nn.softmax(scores, axis=-1)
        attended = jnp.einsum('bts,bsf->btf', attn, features_n)
        return attended

    def _L1_ffn_ref(hidden_states, gate_w, w_gate_up, w_down, shared_w_gate_up, shared_w_down):
        import jax, jax.numpy as jnp
        import numpy as np
        HIDDEN = 512
        MOE_INTER = 128
        SHARED_INTER = 512
        NUM_EXPERTS = 16
        TOP_K = 2

        def _moe_forward(x, gate_w, w_gate_up, w_down, shared_w_gate_up, shared_w_down):
            orig_shape = x.shape
            x2 = x.reshape(-1, orig_shape[-1])
            gu_s = x2 @ shared_w_gate_up.T
            g_s, u_s = jnp.split(gu_s, 2, axis=-1)
            shared_out = jax.nn.silu(g_s) * u_s @ shared_w_down.T
            logits = x2 @ gate_w.T
            probs = jax.nn.softmax(logits, axis=-1)
            topk_vals, topk_idx = jax.lax.top_k(probs, TOP_K)
            topk_vals = topk_vals / jnp.sum(topk_vals, axis=-1, keepdims=True)
            combine = jnp.sum(jax.nn.one_hot(topk_idx, NUM_EXPERTS, dtype=x2.dtype) * topk_vals[..., None], axis=1)
            gu = jnp.einsum('th,eih->eti', x2, w_gate_up)
            g, u = jnp.split(gu, 2, axis=-1)
            act = jax.nn.silu(g) * u
            out_e = jnp.einsum('eti,ehi->eth', act, w_down)
            moe_out = jnp.einsum('eth,te->th', out_e, combine)
            return (moe_out + shared_out).reshape(orig_shape)
        return _moe_forward(hidden_states, gate_w, w_gate_up, w_down, shared_w_gate_up, shared_w_down)
    x = x + _L0_xattn_ref(_layernorm(x, axis=-1), ctx_4096, L0_xattn_Wq, L0_xattn_Wk, L0_xattn_Wv, L0_xattn_Wo)
    x = x + _L0_ffn_ref(_layernorm(x, axis=-1), L0_ffn_gate_w, L0_ffn_gate_b, L0_ffn_w1, L0_ffn_b1, L0_ffn_w2, L0_ffn_b2)
    x = x + _L1_xattn_ref(_layernorm(x, axis=-1), ctx_4096, L1_xattn_Wq_w, L1_xattn_Wq_b, L1_xattn_Wk_w, L1_xattn_Wk_b, L1_xattn_fn_w, L1_xattn_qn_w, L1_xattn_kn_w)
    x = x + _L1_ffn_ref(_layernorm(x, axis=-1), L1_ffn_gate_w, L1_ffn_w_gate_up, L1_ffn_w_down, L1_ffn_shared_w_gate_up, L1_ffn_shared_w_down)
    return x

_drawn_inputs = setup_inputs


def setup_inputs(seed=0):
    import zlib

    import numpy as np

    out = dict(_drawn_inputs(seed))
    spreads = {'L0_ffn_gate_b': (0.0, 0.8),
     'L0_ffn_b1': (0.0, 0.486),
     'L0_ffn_b2': (0.0, 0.1),
     'L1_xattn_fn_w': (1.0, 0.2),
     'L1_xattn_qn_w': (1.0, 0.6),
     'L1_xattn_kn_w': (1.0, 0.6)}
    factors = {'L1_xattn_Wq_b': 8.0,
     'L1_xattn_Wk_b': 8.0,
     'L1_ffn_gate_w': 5.84,
     'L1_ffn_w_gate_up': 5.677,
     'L1_ffn_w_down': 5.559,
     'L1_ffn_shared_w_gate_up': 5.704,
     'L1_ffn_shared_w_down': 5.748}
    for name, (base, spread) in spreads.items():
        noise = np.random.default_rng([zlib.crc32(name.encode()), seed]).standard_normal(out[name].shape)
        drawn = base * np.exp(spread * noise) if base else spread * noise
        out[name] = jnp.asarray(drawn.astype(out[name].dtype))
    for name, factor in factors.items():
        out[name] = (out[name] * factor).astype(out[name].dtype)
    return out
```

```python
import math
from contextlib import ExitStack

import concourse.bass as bass
from concourse import mybir

F32 = mybir.dt.float32
F32R = mybir.dt.float32r
ALU = mybir.AluOpType
ACT = mybir.ActivationFunctionType
AX = mybir.AxisListType
P = 128


def new_semaphore(nc, held, name):
    held.append(nc.alloc_semaphore(name=name))
    return held[-1]


def release(nc, held):
    nc.clear_and_free_semaphores(list(held))
    nc.all_engine_barrier()
    held.clear()


def norm_block(nc, held, x_res, xn, eps, name, load_from=None, constants=None):
    tiles = x_res.shape[1]
    with ExitStack() as ctx:
        sb = lambda n, s, d=F32: ctx.enter_context(nc.sbuf_tensor(f"{name}_{n}", s, d))
        sem = lambda n: new_semaphore(nc, held, f"{name}_{n}")
        stats = sb("stats", [P, tiles, 6])
        mean_var = sb("mean_var", [P, tiles, 2])
        var_eps = sb("var_eps", [P, tiles])
        deviation = sb("deviation", [P, tiles])
        inverse = sb("inverse", [P, tiles])
        x_loaded = [sem(f"x_loaded{t}") for t in range(tiles)] if load_from is not None else None
        zeroed, constants_ready = sem("zeroed"), sem("constants_ready")
        stats_done, mean_done, var_done = sem("stats_done"), sem("mean_done"), sem("var_done")
        deviation_done, inverse_done, normed = sem("deviation_done"), sem("inverse_done"), sem("normed")
        block = ctx.enter_context(nc.Block())

        if load_from is not None:
            rows = load_from.rearrange("b (t p) d -> (b t) p d", p=P)

            @block.sync
            def _(sp):
                for t in range(tiles):
                    sp.dma_start(x_res[:, t, :], rows[t]).then_inc(x_loaded[t], 16)

            @block.gpsimd
            def _(pool):
                ident, ones = constants
                pool.memset(ident[:, :], 0.0).then_inc(zeroed, 1)
                pool.memset(ones[:, :], 1.0).then_inc(constants_ready, 1)
                pool.wait_ge(zeroed, 1)
                pool.affine_select(out=ident[:, :], in_=ident[:, :], compare_op=ALU.not_equal, fill=1.0,
                                   base=0, pattern=[[-1, P]], channel_multiplier=1).then_inc(constants_ready, 1)

        @block.vector
        def _(dve):
            for t in range(tiles):
                if x_loaded:
                    dve.wait_ge(x_loaded[t], 16)
                dve.bn_stats(stats[:, t, :], x_res[:, t, :]).then_inc(stats_done, 1)
            for t in range(tiles):
                dve.wait_ge(stats_done, t + 1)
                dve.bn_aggr(mean_var[:, t, :], stats[:, t, :]).then_inc(mean_done, 1)
            dve.wait_ge(mean_done, tiles)
            dve.tensor_scalar(var_eps[:, :], mean_var[:, :, 1], eps, None, ALU.add).then_inc(var_done, 1)
            dve.wait_ge(deviation_done, 1)
            dve.reciprocal(inverse[:, :], deviation[:, :]).then_inc(inverse_done, 1)
            dve.wait_ge(inverse_done, 1)
            for t in range(tiles):
                dve.tensor_scalar(xn[:, t, :], x_res[:, t, :], mean_var[:, t, 0:1], inverse[:, t:t + 1],
                                  ALU.subtract, ALU.mult).then_inc(normed, 1)

        @block.scalar
        def _(act):
            act.wait_ge(var_done, 1)
            act.activation(deviation[:, :], var_eps[:, :], ACT.Sqrt).then_inc(deviation_done, 1)


def grouped_attention_block(nc, held, ctx_in, wq, wk, wv, wo, x_res, xn, ident, ones):
    B, CTX, D = ctx_in.shape
    TOK = x_res.shape[1] * P // B
    QT = TOK // P
    DC = D // P
    HD = P
    KVH = wk.shape[1] // HD
    HPG = wq.shape[1] // HD // KVH
    KEYS = TOK + CTX
    WIDTH = KEYS + KEYS % 2
    KT = -(-KEYS // P)
    LAST = KEYS - (KT - 1) * P
    PAIRS = -(-KT // 2)
    BANK = 512
    CHUNKS = [(c, min(BANK, WIDTH - c)) for c in range(0, WIDTH, BANK)]
    HALVES = [(0, 2 * BANK), (2 * BANK, KEYS)]
    LAT = TOK // P
    STAGES = 3
    SCALE = 1.0 / math.sqrt(HD)
    VG = -(-KT // 4)
    VPIECES = [(4 * q, 4, P) for q in range(VG - 1)] + [(4 * (VG - 1), KT - 1 - 4 * (VG - 1), P), (KT - 1, 1, LAST)]
    rows_of = lambda k: LAST if k == KT - 1 else P
    assert QT == 2 and len(CHUNKS) == 4 and HPG == 8 and KT % STAGES == 0 and KT - 1 - 4 * (VG - 1) > 0

    with ExitStack() as ctx:
        sb = lambda n, s, d=F32: ctx.enter_context(nc.sbuf_tensor(f"a_{n}", s, d))
        sem = lambda n: new_semaphore(nc, held, f"a_{n}")
        stage = [sb(f"stage{i}", [P, D]) for i in range(STAGES)]
        hid_hi, hid_lo = sb("hid_hi", [P, DC, WIDTH], F32R), sb("hid_lo", [P, DC, WIDTH], F32R)
        k_hi, k_lo = sb("k_hi", [P, WIDTH], F32R), sb("k_lo", [P, WIDTH], F32R)
        v_hi, v_lo = sb("v_hi", [P, KT, HD], F32R), sb("v_lo", [P, KT, HD], F32R)
        probs = [[sb(f"probs{a}{j}", [P, WIDTH]) for j in range(QT)] for a in range(2)]
        v_t = probs[0][0]
        pt_hi, pt_lo = sb("pt_hi", [P, 2, 2, TOK], F32R), sb("pt_lo", [P, 2, 2, TOK], F32R)
        q_hi, q_lo = [sb(f"q_hi{a}", [P, TOK], F32R) for a in range(2)], [sb(f"q_lo{a}", [P, TOK], F32R) for a in range(2)]
        wkv_raw = sb("wkv_raw", [P, 2, DC, HD])
        wkv_hi, wkv_lo = sb("wkv_hi", [P, 2, DC, HD], F32R), sb("wkv_lo", [P, 2, DC, HD], F32R)
        wq_raw, wo_raw = sb("wq_raw", [P, DC, HD]), sb("wo_raw", [P, D])
        wq_hi = [sb(f"wq_hi{a}", [P, DC, HD], F32R) for a in range(2)]
        wq_lo = [sb(f"wq_lo{a}", [P, DC, HD], F32R) for a in range(2)]
        wo_hi = [sb(f"wo_hi{a}", [P, D], F32R) for a in range(2)]
        wo_lo = [sb(f"wo_lo{a}", [P, D], F32R) for a in range(2)]
        o_f, o_hi, o_lo = sb("o_f", [P, TOK]), sb("o_hi", [P, TOK], F32R), sb("o_lo", [P, TOK], F32R)
        diag, inv_wide = sb("diag", [P, TOK]), sb("inv_wide", [P, TOK])
        half_max, neg_max = sb("half_max", [P, 2]), sb("neg_max", [P, QT])
        half_sum, row_sum, row_inv = sb("half_sum", [P, 2, QT, 2]), sb("row_sum", [P, QT]), sb("row_inv", [P, QT])

        ps_s = ctx.enter_context(nc.psum_tensor("a_ps_s", [P, 4, BANK], F32))
        ps_t = ctx.enter_context(nc.psum_tensor("a_ps_t", [P, 2, BANK], F32))
        ps_o = ctx.enter_context(nc.psum_tensor("a_ps_o", [P, BANK], F32))
        ps_m = ctx.enter_context(nc.psum_tensor("a_ps_m", [P, BANK], F32))
        s_flat = ps_s[:, :, :].rearrange("p c n -> p (c n)")

        pad_zeroed = sem("pad_zeroed")
        stage_loaded = [sem(f"stage_loaded{i}") for i in range(STAGES)]
        stage_copied, hid_ps, hid_hi_done, hid_done = sem("stage_copied"), sem("hid_ps"), sem("hid_hi_done"), sem("hid_done")
        wkv_loaded, wkv_hi_done, wkv_ready = sem("wkv_loaded"), sem("wkv_hi_done"), sem("wkv_ready")
        wq_loaded, wq_hi_done, wq_ready = sem("wq_loaded"), sem("wq_hi_done"), sem("wq_ready")
        wo_loaded, wo_hi_done, wo_ready = sem("wo_loaded"), sem("wo_hi_done"), sem("wo_ready")
        kv_ps, k_hi_done, k_done, vt_done = sem("kv_ps"), sem("k_hi_done"), sem("k_done"), sem("vt_done")
        v_ps, v_hi_done, v_done = sem("v_ps"), sem("v_hi_done"), sem("v_done")
        q_ps, q_hi_done, q_done = sem("q_ps"), sem("q_hi_done"), sem("q_done")
        s_ps, max_done, neg_max_done, probs_done = sem("s_ps"), sem("max_done"), sem("neg_max_done"), sem("probs_done")
        sum_done, inv_done, diag_done, inv_ps = sem("sum_done"), sem("inv_done"), sem("diag_done"), sem("inv_ps")
        pt_ps, pt_hi_done, pt_done, pv_ps = sem("pt_ps"), sem("pt_hi_done"), sem("pt_done"), sem("pv_ps")
        o_f_done, o_hi_done, o_done = sem("o_f_done"), sem("o_hi_done"), sem("o_done")
        wo_ps, wo_added, inv_copied = sem("wo_ps"), sem("wo_added"), sem("inv_copied")
        block = ctx.enter_context(nc.Block())

        wk_v = wk.rearrange("(c p) n -> p c n", p=P)
        wv_v = wv.rearrange("(c p) n -> p c n", p=P)
        wq_v = wq.rearrange("(c p) n -> p c n", p=P)

        @block.sync
        def _(sp):
            def load_wq(u, head):
                sp.wait_ge(wq_ready, u)
                sp.dma_start(wq_raw[:, :, :], wq_v[:, :, bass.ds(head * HD, HD)]).then_inc(wq_loaded, 16)

            def load_wo(u, head):
                sp.wait_ge(wo_ready, u)
                sp.dma_start(wo_raw[:, :], wo[bass.ds(head * HD, HD), :]).then_inc(wo_loaded, 16)

            with sp.Fori(0, B) as b:
                for r in range(LAT, KT):
                    if r >= STAGES:
                        sp.wait_ge(hid_ps, KT * b + r - STAGES + 1)
                    else:
                        sp.wait_ge(hid_ps, KT * b)
                    n = rows_of(r)
                    sp.dma_start(stage[r % STAGES][0:n, :], ctx_in[b, (r - LAT) * P:(r - LAT) * P + n, :]
                                 ).then_inc(stage_loaded[r % STAGES], 16)
                with sp.Fori(0, KVH) as g:
                    sp.wait_ge(wkv_ready, KVH * b + g)
                    sp.dma_start(wkv_raw[:, 0, :, :], wk_v[:, :, bass.ds(g * HD, HD)]).then_inc(wkv_loaded, 16)
                    sp.dma_start(wkv_raw[:, 1, :, :], wv_v[:, :, bass.ds(g * HD, HD)]).then_inc(wkv_loaded, 16)
                    u0 = (b * KVH + g) * HPG
                    load_wq(u0, g * HPG)
                    with sp.Fori(0, HPG - 1) as h:
                        load_wq(u0 + h + 1, g * HPG + h + 1)
                        load_wo(u0 + h, g * HPG + h)
                    load_wo(u0 + HPG - 1, g * HPG + HPG - 1)

        @block.gpsimd
        def _(pool):
            pool.memset(hid_hi[:, :, KEYS:WIDTH].bitcast(F32), 0.0).then_inc(pad_zeroed, 1)
            pool.memset(hid_lo[:, :, KEYS:WIDTH].bitcast(F32), 0.0).then_inc(pad_zeroed, 1)

            def split(hi, lo, raw, hi_done, ready, n):
                pool.tensor_tensor(hi, raw, ones[:, 0:1].to_broadcast(raw.shape), ALU.mult).then_inc(hi_done, 1)
                pool.wait_ge(hi_done, n + 1)
                pool.tensor_tensor(lo, raw, hi.bitcast(F32), ALU.subtract).then_inc(ready, 1)

            def flat(w):
                return w[:].rearrange("p c n -> p (c n)" if len(w.shape) == 3 else "p a c n -> p (a c n)")

            def split_wq(u, a, free):
                pool.wait_ge(wq_loaded, 16 * (u + 1))
                pool.wait_ge(q_ps, free)
                split(flat(wq_hi[a]), flat(wq_lo[a]), flat(wq_raw), wq_hi_done, wq_ready, u)

            def split_wo(u, a, free):
                pool.wait_ge(wo_loaded, 16 * (u + 1))
                pool.wait_ge(wo_ps, QT * free)
                split(wo_hi[a][:, :], wo_lo[a][:, :], wo_raw[:, :], wo_hi_done, wo_ready, u)

            with pool.Fori(0, B) as b:
                for r in range(LAT):
                    pool.wait_ge(hid_ps, KT * b)
                    pool.tensor_tensor(stage[r][:, :], xn[:, bass.ds(QT * b + r, 1), :].rearrange("p a d -> p (a d)"),
                                       ones[:, 0:1].to_broadcast([P, D]), ALU.mult).then_inc(stage_copied, 1)
                with pool.Fori(0, KVH) as g:
                    G = b * KVH + g
                    pool.wait_ge(wkv_loaded, 32 * (G + 1))
                    pool.wait_ge(kv_ps, 8 * G)
                    split(flat(wkv_hi), flat(wkv_lo), flat(wkv_raw), wkv_hi_done, wkv_ready, G)
                    u0 = G * HPG
                    split_wq(u0, 0, u0)
                    split_wq(u0 + 1, 1, u0)
                    split_wo(u0, 0, u0)
                    split_wq(u0 + 2, 0, u0 + 1)
                    split_wo(u0 + 1, 1, u0)
                    with pool.Fori(0, HPG // 2 - 2) as i:
                        for a in range(2):
                            u = u0 + 2 * i + 2 + a
                            split_wq(u + 1, 1 - a, u)
                            split_wo(u, a, u - 1)
                    split_wq(u0 + 7, 1, u0 + 6)
                    split_wo(u0 + 6, 0, u0 + 5)
                    split_wo(u0 + 7, 1, u0 + 6)

        @block.tensor
        def _(pe):
            def three(out, w_hi, w_lo, m_hi, m_lo, first, last):
                pe.matmul(out, w_hi, m_hi, start=first, stop=False)
                pe.matmul(out, w_hi, m_lo, start=False, stop=False)
                return pe.matmul(out, w_lo, m_hi, start=False, stop=last)

            def project(out, w_hi, w_lo, c0, n):
                for c in range(DC):
                    mm = three(out, w_hi[:, c, :], w_lo[:, c, :], hid_hi[:, c, c0:c0 + n], hid_lo[:, c, c0:c0 + n],
                               c == 0, c == DC - 1)
                return mm

            def queries(u, a):
                pe.wait_ge(wq_ready, u + 1)
                project(ps_m[:, 0:TOK], wq_hi[a], wq_lo[a], 0, TOK).then_inc(q_ps, 1)

            def scores(u, a, j, first):
                if j == 0:
                    pe.wait_ge(q_done, u + 1)
                for half in range(2):
                    if not first:
                        pe.wait_ge(probs_done, 4 * u + 2 * j + half - 1)
                    for c in (2 * half, 2 * half + 1):
                        c0, n = CHUNKS[c]
                        mm = three(ps_s[:, c, 0:n], q_hi[a][:, P * j:P * j + P], q_lo[a][:, P * j:P * j + P],
                                   k_hi[:, c0:c0 + n], k_lo[:, c0:c0 + n], True, True)
                    mm.then_inc(s_ps, 1)

            def transpose_probs(v, a, p, first):
                if p == 0:
                    pe.wait_ge(probs_done, 4 * (v + 1))
                if not (first and p < 2):
                    pe.wait_ge(pt_done, PAIRS * v + p - 1)
                for k in range(2 * p, min(2 * p + 2, KT)):
                    n = rows_of(k)
                    for j in range(QT):
                        at = (k % 2) * TOK + j * P
                        tr = pe.transpose(ps_t[0:n, p % 2, at:at + P], probs[a][j][:, k * P:k * P + n], ident[:, :])
                tr.then_inc(pt_ps, 1)

            def weigh_values(v, p):
                pe.wait_ge(pt_done, PAIRS * v + p + 1)
                if p == 0:
                    pe.wait_ge(o_f_done, v)
                for k in range(2 * p, min(2 * p + 2, KT)):
                    n = rows_of(k)
                    mm = three(ps_o[:, 0:TOK], v_hi[0:n, k, :], v_lo[0:n, k, :], pt_hi[0:n, p % 2, k % 2, :],
                               pt_lo[0:n, p % 2, k % 2, :], k == 0, k == KT - 1)
                mm.then_inc(pv_ps, 1)

            def spread_inverse(v):
                pe.wait_ge(diag_done, QT * (v + 1))
                pe.matmul(ps_m[:, 0:TOK], ones[:, :], diag[:, :], start=True, stop=True).then_inc(inv_ps, 1)

            def output(w, a, j):
                if j == 0:
                    pe.wait_ge(o_done, w + 1)
                    pe.wait_ge(wo_ready, w + 1)
                else:
                    pe.wait_ge(wo_added, QT * w + 1)
                three(ps_m[:, :], o_hi[:, P * j:P * j + P], o_lo[:, P * j:P * j + P], wo_hi[a][:, :], wo_lo[a][:, :],
                      True, True).then_inc(wo_ps, 1)

            def step(u, a, qk, pv, out, ahead, first_pv=False):
                v = u - 1
                if pv:
                    transpose_probs(v, 1 - a, 0, first_pv)
                    transpose_probs(v, 1 - a, 1, first_pv)
                if qk:
                    scores(u, a, 0, not pv)
                if out:
                    output(u - 2, a, 0)
                if pv:
                    weigh_values(v, 0)
                    transpose_probs(v, 1 - a, 2, False)
                    weigh_values(v, 1)
                    transpose_probs(v, 1 - a, 3, False)
                if qk:
                    scores(u, a, 1, False)
                if out:
                    output(u - 2, a, 1)
                if pv:
                    weigh_values(v, 2)
                    transpose_probs(v, 1 - a, 4, False)
                    weigh_values(v, 3)
                if ahead:
                    if out:
                        pe.wait_ge(wo_added, QT * (u - 1))
                    queries(u + 1, 1 - a)
                if pv:
                    transpose_probs(v, 1 - a, 5, False)
                    weigh_values(v, 4)
                    transpose_probs(v, 1 - a, 6, False)
                    weigh_values(v, 5)
                    transpose_probs(v, 1 - a, 7, False)
                    weigh_values(v, 6)
                    if ahead:
                        pe.wait_ge(q_done, u + 2)
                    elif out:
                        pe.wait_ge(wo_added, QT * (u - 1))
                    spread_inverse(v)
                    weigh_values(v, 7)

            with pe.Fori(0, B) as b:
                pe.wait_ge(probs_done, 4 * HPG * KVH * b)
                for r in range(KT):
                    i, n = r % STAGES, rows_of(r)
                    if r < LAT:
                        pe.wait_ge(stage_copied, LAT * b + r + 1)
                    else:
                        loads = [q for q in range(LAT, KT) if q % STAGES == i]
                        pe.wait_ge(stage_loaded[i], 16 * (len(loads) * b + loads.index(r) + 1))
                    if r >= 4:
                        pe.wait_ge(hid_done, KT * b + r - 3)
                    for c in range(DC):
                        tr = pe.transpose(ps_s[:, r % 4, c * P:c * P + n], stage[i][0:n, c * P:(c + 1) * P],
                                          ident[0:n, 0:n])
                    tr.then_inc(hid_ps, 1)
                with pe.Fori(0, KVH) as g:
                    G = b * KVH + g
                    u0 = G * HPG
                    pe.wait_ge(pad_zeroed, 2)
                    pe.wait_ge(hid_done, KT * (b + 1))
                    pe.wait_ge(wkv_ready, G + 1)
                    pe.wait_ge(probs_done, 4 * u0)
                    for kv in range(2):
                        for c, (c0, n) in enumerate(CHUNKS):
                            if kv:
                                pe.wait_ge(k_done, 4 * G + c + 1)
                            project(ps_s[:, c, 0:n], wkv_hi[:, kv], wkv_lo[:, kv], c0, n).then_inc(kv_ps, 1)
                    pe.wait_ge(wo_added, QT * u0)
                    queries(u0, 0)
                    pe.wait_ge(pt_done, PAIRS * u0)
                    for q in range(VG):
                        pe.wait_ge(vt_done, 4 * G + q + 1)
                        if q >= 2:
                            pe.wait_ge(v_done, len(VPIECES) * G + q - 1)
                        for k in range(4 * q, min(4 * q + 4, KT)):
                            n = rows_of(k)
                            tr = pe.transpose(ps_t[0:n, q % 2, (k % 4) * P:(k % 4 + 1) * P], v_t[:, k * P:k * P + n],
                                              ident[:, :])
                        tr.then_inc(v_ps, 1)
                    step(u0, 0, True, False, False, True)
                    pe.wait_ge(v_done, len(VPIECES) * (G + 1))
                    step(u0 + 1, 1, True, True, False, True, first_pv=True)
                    with pe.Fori(0, HPG // 2 - 2) as i:
                        step(u0 + 2 * i + 2, 0, True, True, True, True)
                        step(u0 + 2 * i + 3, 1, True, True, True, True)
                    step(u0 + 6, 0, True, True, True, True)
                    step(u0 + 7, 1, True, True, True, False)
                    step(u0 + 8, 0, False, True, True, False)
                    output(u0 + 7, 1, 0)
                    output(u0 + 7, 1, 1)

        @block.scalar
        def _(act):
            def probs_hi(v, p):
                act.wait_ge(pt_ps, PAIRS * v + p + 1)
                full = 2 if 2 * p + 2 < KT else 1
                n = P if full == 2 else LAST
                if p >= 2:
                    act.wait_ge(pv_ps, PAIRS * v + p - 1)
                else:
                    act.wait_ge(pv_ps, PAIRS * v)
                act.activation(pt_hi[0:n, p % 2, 0:full, :],
                               ps_t[0:n, p % 2, 0:full * TOK].rearrange("p (k q) -> p k q", k=full),
                               ACT.Copy).then_inc(pt_hi_done, 1)

            def exponentials(u, a, j, half):
                act.wait_ge(neg_max_done, QT * u + j + 1)
                lo, hi = HALVES[half]
                act.activation(probs[a][j][:, lo:hi], s_flat[:, lo:hi], ACT.Exp, bias=neg_max[:, j:j + 1], scale=SCALE,
                               accum_out=half_sum[:, a, j, half:half + 1]).then_inc(probs_done, 1)

            def queries_hi(u, a):
                act.wait_ge(q_ps, u + 1)
                act.activation(q_hi[a][:, :], ps_m[:, 0:TOK], ACT.Copy).then_inc(q_hi_done, 1)

            def inverse_out(v):
                act.wait_ge(inv_ps, v + 1)
                act.wait_ge(o_f_done, v)
                act.activation(inv_wide[:, :], ps_m[:, 0:TOK], ACT.Copy).then_inc(inv_copied, 1)

            def output_hi(w):
                act.wait_ge(o_f_done, w + 1)
                act.activation(o_hi[:, :], o_f[:, :], ACT.Copy).then_inc(o_hi_done, 1)

            def step(u, a, qk, pv, out, ahead):
                v = u - 1
                if pv:
                    probs_hi(v, 0)
                    probs_hi(v, 1)
                if out:
                    output_hi(u - 2)
                if qk:
                    exponentials(u, a, 0, 0)
                    exponentials(u, a, 0, 1)
                if pv:
                    probs_hi(v, 2)
                    probs_hi(v, 3)
                if qk:
                    exponentials(u, a, 1, 0)
                if pv:
                    probs_hi(v, 4)
                if qk:
                    exponentials(u, a, 1, 1)
                if ahead:
                    queries_hi(u + 1, 1 - a)
                if pv:
                    probs_hi(v, 5)
                    probs_hi(v, 6)
                    probs_hi(v, 7)
                    inverse_out(v)

            with act.Fori(0, B) as b:
                for r in range(KT):
                    n = rows_of(r)
                    act.wait_ge(hid_ps, KT * b + r + 1)
                    act.activation(hid_hi[:, :, r * P:r * P + n],
                                   ps_s[:, r % 4, :].rearrange("p (c n) -> p c n", c=DC)[:, :, 0:n],
                                   ACT.Copy).then_inc(hid_hi_done, 1)
                with act.Fori(0, KVH) as g:
                    G = b * KVH + g
                    u0 = G * HPG
                    for c, (c0, n) in enumerate(CHUNKS):
                        act.wait_ge(kv_ps, 8 * G + c + 1)
                        act.activation(k_hi[:, c0:c0 + n], ps_s[:, c, 0:n], ACT.Copy).then_inc(k_hi_done, 1)
                    for c, (c0, n) in enumerate(CHUNKS):
                        act.wait_ge(kv_ps, 8 * G + 4 + c + 1)
                        act.activation(v_t[:, c0:c0 + n], ps_s[:, c, 0:n], ACT.Copy).then_inc(vt_done, 1)
                    queries_hi(u0, 0)
                    for i, (k, m, n) in enumerate(VPIECES):
                        act.wait_ge(v_ps, VG * G + min(i, VG - 1) + 1)
                        act.activation(v_hi[0:n, k:k + m, :],
                                       ps_t[0:n, k // 4 % 2, (k % 4) * P:(k % 4 + m) * P].rearrange("p (k d) -> p k d", k=m),
                                       ACT.Copy).then_inc(v_hi_done, 1)
                    step(u0, 0, True, False, False, True)
                    step(u0 + 1, 1, True, True, False, True)
                    with act.Fori(0, HPG // 2 - 2) as i:
                        step(u0 + 2 * i + 2, 0, True, True, True, True)
                        step(u0 + 2 * i + 3, 1, True, True, True, True)
                    step(u0 + 6, 0, True, True, True, True)
                    step(u0 + 7, 1, True, True, True, False)
                    step(u0 + 8, 0, False, True, True, False)
                    output_hi(u0 + 7)

        @block.vector
        def _(dve):
            def probs_lo(v, p):
                full = 2 if 2 * p + 2 < KT else 1
                n = P if full == 2 else LAST
                dve.wait_ge(pt_hi_done, PAIRS * v + p + 1)
                dve.tensor_tensor(pt_lo[0:n, p % 2, 0:full, :],
                                  ps_t[0:n, p % 2, 0:full * TOK].rearrange("p (k q) -> p k q", k=full),
                                  pt_hi[0:n, p % 2, 0:full, :].bitcast(F32), ALU.subtract).then_inc(pt_done, 1)

            def maxima(u, j):
                for half, (lo, hi) in enumerate(HALVES):
                    dve.wait_ge(s_ps, 4 * u + 2 * j + half + 1)
                    dve.reduce_max(half_max[:, half:half + 1], s_flat[:, lo:hi], AX.X).then_inc(max_done, 1)
                dve.wait_ge(max_done, 4 * u + 2 * j + 2)
                dve.tensor_scalar(neg_max[:, j:j + 1], half_max[:, 0:1], half_max[:, 1:2], -SCALE, ALU.max,
                                  ALU.mult).then_inc(neg_max_done, 1)

            def queries_lo(u, a):
                dve.wait_ge(q_hi_done, u + 1)
                dve.tensor_tensor(q_lo[a][:, :], ps_m[:, 0:TOK], q_hi[a][:, :].bitcast(F32), ALU.subtract).then_inc(q_done, 1)

            def inverse_sums(v, a):
                dve.wait_ge(probs_done, 4 * (v + 1))
                dve.tensor_tensor(row_sum[:, :], half_sum[:, a, :, 0], half_sum[:, a, :, 1], ALU.add).then_inc(sum_done, 1)
                dve.wait_ge(sum_done, v + 1)
                dve.reciprocal(row_inv[:, :], row_sum[:, :]).then_inc(inv_done, 1)
                dve.wait_ge(inv_done, v + 1)
                for j in range(QT):
                    dve.tensor_scalar(diag[:, P * j:P * j + P], ident[:, :], row_inv[:, j:j + 1], None,
                                      ALU.mult).then_inc(diag_done, 1)

            def normalise(w):
                dve.wait_ge(pv_ps, PAIRS * (w + 1))
                dve.wait_ge(inv_copied, w + 1)
                dve.tensor_tensor(o_f[:, :], ps_o[:, 0:TOK], inv_wide[:, :], ALU.mult).then_inc(o_f_done, 1)

            def output_lo(w):
                dve.wait_ge(o_hi_done, w + 1)
                dve.tensor_tensor(o_lo[:, :], o_f[:, :], o_hi[:, :].bitcast(F32), ALU.subtract).then_inc(o_done, 1)

            def add_output(w, j, tile):
                x_tile = x_res[:, bass.ds(tile, 1), :].rearrange("p a d -> p (a d)")
                dve.wait_ge(wo_ps, QT * w + j + 1)
                dve.wait_ge(wo_added, QT * w + j)
                dve.tensor_tensor(x_tile, ps_m[:, :], x_tile, ALU.add).then_inc(wo_added, 1)

            def step(u, a, tile, qk, pv, out, ahead):
                v = u - 1
                if out:
                    normalise(u - 2)
                if pv:
                    inverse_sums(v, 1 - a)
                    probs_lo(v, 0)
                    probs_lo(v, 1)
                if out:
                    output_lo(u - 2)
                if qk:
                    maxima(u, 0)
                if out:
                    add_output(u - 2, 0, tile)
                if pv:
                    probs_lo(v, 2)
                    probs_lo(v, 3)
                if qk:
                    maxima(u, 1)
                if out:
                    add_output(u - 2, 1, tile + 1)
                if pv:
                    probs_lo(v, 4)
                if ahead:
                    queries_lo(u + 1, 1 - a)
                if pv:
                    probs_lo(v, 5)
                    probs_lo(v, 6)
                    probs_lo(v, 7)

            with dve.Fori(0, B) as b:
                for r in range(KT):
                    n = rows_of(r)
                    dve.wait_ge(hid_hi_done, KT * b + r + 1)
                    dve.tensor_tensor(hid_lo[:, :, r * P:r * P + n],
                                      ps_s[:, r % 4, :].rearrange("p (c n) -> p c n", c=DC)[:, :, 0:n],
                                      hid_hi[:, :, r * P:r * P + n].bitcast(F32), ALU.subtract).then_inc(hid_done, 1)
                with dve.Fori(0, KVH) as g:
                    G = b * KVH + g
                    u0 = G * HPG
                    tile = QT * b
                    for c, (c0, n) in enumerate(CHUNKS):
                        dve.wait_ge(k_hi_done, 4 * G + c + 1)
                        dve.tensor_tensor(k_lo[:, c0:c0 + n], ps_s[:, c, 0:n], k_hi[:, c0:c0 + n].bitcast(F32),
                                          ALU.subtract).then_inc(k_done, 1)
                    queries_lo(u0, 0)
                    for i, (k, m, n) in enumerate(VPIECES):
                        dve.wait_ge(v_hi_done, len(VPIECES) * G + (i + 1 if i < VG - 1 else VG + 1))
                        dve.tensor_tensor(v_lo[0:n, k:k + m, :],
                                          ps_t[0:n, k // 4 % 2, (k % 4) * P:(k % 4 + m) * P].rearrange("p (k d) -> p k d", k=m),
                                          v_hi[0:n, k:k + m, :].bitcast(F32), ALU.subtract).then_inc(v_done, 1)
                    step(u0, 0, tile, True, False, False, True)
                    step(u0 + 1, 1, tile, True, True, False, True)
                    with dve.Fori(0, HPG // 2 - 2) as i:
                        step(u0 + 2 * i + 2, 0, tile, True, True, True, True)
                        step(u0 + 2 * i + 3, 1, tile, True, True, True, True)
                    step(u0 + 6, 0, tile, True, True, True, True)
                    step(u0 + 7, 1, tile, True, True, True, False)
                    step(u0 + 8, 0, tile, False, True, True, False)
                    normalise(u0 + 7)
                    output_lo(u0 + 7)
                    add_output(u0 + 7, 0, tile)
                    add_output(u0 + 7, 1, tile + 1)


class Chain:

    def __init__(self, engine, semaphore):
        self.engine, self.semaphore, self.count = engine, semaphore, 0

    def link(self, instruction):
        self.count += 1
        instruction.then_inc(self.semaphore, 1)
        self.engine.wait_ge(self.semaphore, self.count)


def wide(x, n):
    return x.unsqueeze(2).to_broadcast([x.shape[0], x.shape[1], n])


def softmax_rows(dve, chain, scores, logits, row, row2, exp_wait, max_done):
    E = logits.shape[2]
    chain.link(dve.reduce_max(row, logits, AX.X))
    dve.tensor_tensor(scores, logits, wide(row, E), ALU.subtract).then_inc(max_done, 1)
    dve.wait_ge(exp_wait, 1)
    chain.link(dve.reduce_sum(row, scores, AX.X))
    chain.link(dve.reciprocal(row2, row))
    chain.link(dve.tensor_tensor(scores, scores, wide(row2, E), ALU.mult))


def top_two(dve, chain, scores, ramp, hit, first, second, rest, row, best, runner):
    E, tiles = scores.shape[2], scores.shape[1]
    ramps = ramp.unsqueeze(1).to_broadcast([P, tiles, E])
    for values, value, one_hot in ((scores, best, first), (rest, runner, second)):
        chain.link(dve.reduce_max(value, values, AX.X))
        chain.link(dve.tensor_tensor(hit, values, wide(value, E), ALU.is_equal))
        chain.link(dve.tensor_tensor(hit, hit, ramps, ALU.mult))
        chain.link(dve.reduce_max(row, hit, AX.X))
        chain.link(dve.tensor_tensor(one_hot, hit, wide(row, E), ALU.is_equal))
        if values is scores:
            chain.link(dve.scalar_tensor_tensor(rest, first, -4.0, scores, ALU.mult, ALU.add))


def gated_experts_block(nc, held, gate_w, gate_b, w1, b1, w2, b2, x_res, xn, ident, ones, batches):
    TILES, D = x_res.shape[1], x_res.shape[2]
    E, _, F = w1.shape
    DC, FC = D // P, F // P
    TPB = TILES // batches
    VISION = int(TPB * P * 0.3)
    EW = E + E % 2
    BANK = 512
    TC = TILES * P // BANK
    TPC = BANK // P
    STEPS = TC * FC
    PIECES = DC + FC
    FUNCTIONS = (ACT.Tanh, ACT.Gelu, ACT.Silu)
    assert E == len(FUNCTIONS) and TPB == 2 and VISION <= P and PIECES == STEPS and D == BANK and F == BANK

    with ExitStack() as ctx:
        sb = lambda n, s, d=F32: ctx.enter_context(nc.sbuf_tensor(f"b_{n}", s, d))
        sem = lambda n: new_semaphore(nc, held, f"b_{n}")
        xt_hi, xt_lo = sb("xt_hi", [P, DC, TILES * P], F32R), sb("xt_lo", [P, DC, TILES * P], F32R)
        w1_raw, w2_raw = sb("w1_raw", [P, DC, F]), sb("w2_raw", [P, FC, D])
        w1_hi = [sb(f"w1_hi{a}", [P, DC, F], F32R) for a in range(2)]
        w1_lo = [sb(f"w1_lo{a}", [P, DC, F], F32R) for a in range(2)]
        w2_hi = [sb(f"w2_hi{a}", [P, FC, D], F32R) for a in range(2)]
        w2_lo = [sb(f"w2_lo{a}", [P, FC, D], F32R) for a in range(2)]
        hidden = [sb(f"hidden{i}", [P, BANK]) for i in range(2)]
        act_hi, act_lo = sb("act_hi", [P, FC, TILES * P], F32R), sb("act_lo", [P, FC, TILES * P], F32R)
        b1_rows, b1_cols = sb("b1_rows", [E * FC, P]), sb("b1_cols", [P, E, FC])
        b2_raw, b2_hi, b2_lo = sb("b2_raw", [1, E, D]), sb("b2_hi", [1, E, D], F32R), sb("b2_lo", [1, E, D], F32R)
        one_r = sb("one_r", [1, P], F32R)
        gate_raw, gate_hi, gate_lo = sb("gate_raw", [P, DC, EW]), sb("gate_hi", [P, DC, EW], F32R), sb("gate_lo", [P, DC, EW], F32R)
        gate_rows = sb("gate_rows", [P, 2, E])
        vision, text = sb("vision", [P, P]), sb("text", [P, P])
        ramp = sb("ramp", [P, E])
        magnitudes, magnitude = sb("magnitudes", [P, D]), sb("magnitude", [P, TILES])
        strength, ratio = sb("strength", [P, batches]), sb("ratio", [P, batches])
        logits, scores = sb("logits", [P, TILES, E]), sb("scores", [P, TILES, E])
        hit, first, second, rest = (sb(n, [P, TILES, E]) for n in ("hit", "first", "second", "rest"))
        row, row2, best, runner = (sb(n, [P, TILES]) for n in ("row", "row2", "best", "runner"))
        chosen = sb("chosen", [1, batches, 2, E])
        part, share = sb("part", [P, TILES, E]), sb("share", [P, TILES, E])

        ps_t = ctx.enter_context(nc.psum_tensor("b_ps_t", [P, 2, BANK], F32))
        ps_h = ctx.enter_context(nc.psum_tensor("b_ps_h", [P, 2, BANK], F32))
        ps_y = ctx.enter_context(nc.psum_tensor("b_ps_y", [P, 2, BANK], F32))
        ps_r = ctx.enter_context(nc.psum_tensor("b_ps_r", [P, BANK], F32))
        ps_c = ctx.enter_context(nc.psum_tensor("b_ps_c", [P, BANK], F32))
        strengths = ps_c[:, 0:2 * batches].rearrange("p (k b) -> p k b", k=2)
        choices = ps_c[:, 0:batches * 2 * E].rearrange("p (b i e) -> p b i e", b=batches, i=2)

        small_loaded, gate_loaded = sem("small_loaded"), sem("gate_loaded")
        w1_loaded, w2_loaded = sem("w1_loaded"), sem("w2_loaded")
        masks_set, masks_done, pads_set = sem("masks_set"), sem("masks_done"), sem("pads_set")
        magnitude_done, strength_ps, gate_hi_done, gate_done = sem("magnitude_done"), sem("strength_ps"), sem("gate_hi_done"), sem("gate_done")
        b1_ps, b1_done = sem("b1_ps"), sem("b1_done")
        b2_hi_done, b2_done = sem("b2_hi_done"), sem("b2_done")
        xt_ps, xt_hi_done, xt_done, logits_ps = sem("xt_ps"), sem("xt_hi_done"), sem("xt_done"), sem("logits_ps")
        centred, exp_done, chosen_done, choices_ps = sem("centred"), sem("exp_done"), sem("chosen_done"), sem("choices_ps")
        w_hi_done, w_done = sem("w_hi_done"), sem("w_done")
        h_ps, hidden_done, act_hi_done, act_done = sem("h_ps"), sem("hidden_done"), sem("act_hi_done"), sem("act_done")
        y_ps, added, router = sem("y_ps"), sem("added"), sem("router")
        block = ctx.enter_context(nc.Block())

        @block.sync
        def _(sp):
            for e in range(E):
                if e:
                    sp.wait_ge(w_done, PIECES * e)
                sp.dma_start(w1_raw[:, :, :], w1[e].rearrange("(c p) f -> p c f", p=P)).then_inc(w1_loaded, 16)
                sp.dma_start(w2_raw[:, :, :], w2[e].rearrange("(c p) d -> p c d", p=P)).then_inc(w2_loaded, 16)
                if e == 0:
                    sp.dma_start(gate_raw[:, :, 0:E], gate_w[0:D, :].rearrange("(c p) e -> p c e", p=P)).then_inc(gate_loaded, 16)
                    sp.dma_start(gate_rows[:, 0, :], gate_w[D, :].partition_broadcast(P)).then_inc(small_loaded, 16)
                    sp.dma_start(gate_rows[:, 1, :], gate_b.partition_broadcast(P)).then_inc(small_loaded, 16)
                    sp.dma_start(b1_rows[:, :], b1.rearrange("e (c p) -> (e c) p", p=P)).then_inc(small_loaded, 16)
                    sp.dma_start(b2_raw[:, :, :], b2.rearrange("(a e) d -> a e d", a=1)).then_inc(small_loaded, 16)

        @block.gpsimd
        def _(pool):
            pool.memset(gate_raw[:, :, E:EW], 0.0).then_inc(pads_set, 1)
            pool.memset(one_r[:, :].bitcast(F32), 1.0).then_inc(pads_set, 1)
            pool.iota(ramp[:, :], pattern=[[-1, E]], base=E, channel_multiplier=0,
                      allow_small_or_imprecise_dtypes=True).then_inc(pads_set, 1)
            pool.memset(vision[:, :], 1.0).then_inc(masks_set, 1)
            pool.memset(text[:, :], 1.0).then_inc(masks_set, 1)
            pool.wait_ge(masks_set, 2)
            pool.affine_select(out=vision[:, :], in_=vision[:, :], compare_op=ALU.is_ge, fill=0.0,
                               base=VISION - 1, pattern=[[0, P]], channel_multiplier=-1).then_inc(masks_done, 1)
            pool.affine_select(out=text[:, :], in_=text[:, :], compare_op=ALU.is_ge, fill=0.0,
                               base=-VISION, pattern=[[0, P]], channel_multiplier=1).then_inc(masks_done, 1)

        @block.tensor
        def _(pe):
            def three(out, w_hi, w_lo, m_hi, m_lo, first, last):
                pe.matmul(out, w_hi, m_hi, start=first, stop=False)
                pe.matmul(out, w_hi, m_lo, start=False, stop=False)
                return pe.matmul(out, w_lo, m_hi, start=False, stop=last)

            for t in range(TILES):
                if t >= 2:
                    pe.wait_ge(xt_done, t - 1)
                for c in range(DC):
                    tr = pe.transpose(ps_t[:, t % 2, c * P:(c + 1) * P], xn[:, t, c * P:(c + 1) * P], ident[:, :])
                tr.then_inc(xt_ps, 1)
            pe.wait_ge(small_loaded, 64)
            pe.transpose(ps_h[:, 0, 0:E * FC], b1_rows[:, :], ident[0:E * FC, 0:E * FC]).then_inc(b1_ps, 1)
            pe.wait_ge(masks_done, 2)
            pe.wait_ge(magnitude_done, TILES)
            pe.matmul(strengths[:, 0, :], vision[:, :], magnitude[:, 0:TILES:TPB], start=True, stop=True)
            pe.matmul(strengths[:, 1, :], text[:, :], magnitude[:, 0:TILES:TPB], start=True, stop=False)
            pe.matmul(strengths[:, 1, :], ones[:, :], magnitude[:, 1:TILES:TPB], start=False, stop=True).then_inc(strength_ps, 1)
            pe.wait_ge(gate_done, 1)
            pe.wait_ge(xt_done, TILES)
            for t in range(TILES):
                for c in range(DC):
                    mm = three(ps_r[:, t * EW:(t + 1) * EW], xt_hi[:, c, t * P:(t + 1) * P], xt_lo[:, c, t * P:(t + 1) * P],
                               gate_hi[:, c, :], gate_lo[:, c, :], c == 0, c == DC - 1)
            mm.then_inc(logits_ps, 1)
            for e in range(E):
                a = e % 2
                pe.wait_ge(w_done, PIECES * e + DC)
                for s in range(STEPS):
                    tc, f, n = s // FC, s % FC, STEPS * e + s
                    if n == 0:
                        pe.wait_ge(b1_done, 1)
                    if n >= 2:
                        pe.wait_ge(hidden_done, n - 1)
                    for c in range(DC):
                        mm = three(ps_h[:, n % 2, :], w1_hi[a][:, c, f * P:(f + 1) * P], w1_lo[a][:, c, f * P:(f + 1) * P],
                                   xt_hi[:, c, tc * BANK:(tc + 1) * BANK], xt_lo[:, c, tc * BANK:(tc + 1) * BANK],
                                   c == 0, c == DC - 1)
                    mm.then_inc(h_ps, 1)
                if e == 0:
                    pe.wait_ge(chosen_done, 1)
                    pe.matmul(ps_c[:, 0:batches * 2 * E], ones[0:1, :], chosen[:, :, :, :].rearrange("p b i e -> p (b i e)"),
                              start=True, stop=True).then_inc(choices_ps, 1)
                    pe.wait_ge(pads_set, 3)
                    pe.wait_ge(b2_done, 1)
                pe.wait_ge(w_done, PIECES * (e + 1))
                for t in range(TILES):
                    n = TILES * e + t
                    if t % TPC == 0:
                        pe.wait_ge(act_done, STEPS * e + FC * (t // TPC + 1))
                    if n >= 2:
                        pe.wait_ge(added, n - 1)
                    pe.matmul(ps_y[:, n % 2, :], one_r[:, :], b2_hi[:, e, :], start=True, stop=False)
                    pe.matmul(ps_y[:, n % 2, :], one_r[:, :], b2_lo[:, e, :], start=False, stop=False)
                    for f in range(FC):
                        mm = three(ps_y[:, n % 2, :], act_hi[:, f, t * P:(t + 1) * P], act_lo[:, f, t * P:(t + 1) * P],
                                   w2_hi[a][:, f, :], w2_lo[a][:, f, :], False, f == FC - 1)
                    mm.then_inc(y_ps, 1)

        def weight_piece(e, i):
            a, c = e % 2, i % DC
            if i < DC:
                return w1_raw[:, c, :], w1_hi[a][:, c, :], w1_lo[a][:, c, :]
            return w2_raw[:, c, :], w2_hi[a][:, c, :], w2_lo[a][:, c, :]

        @block.scalar
        def _(act):
            def split_hi(e, i):
                raw, hi, _ = weight_piece(e, i)
                if i == 0:
                    act.wait_ge(w1_loaded, 16 * (e + 1))
                if i == DC:
                    act.wait_ge(w2_loaded, 16 * (e + 1))
                if e >= 2 and i == 0:
                    act.wait_ge(y_ps, TILES * (e - 1))
                act.activation(hi, raw, ACT.Copy).then_inc(w_hi_done, 1)

            for t in range(TILES):
                if t:
                    act.wait_ge(magnitude_done, t)
                act.activation(magnitudes[:, :], xn[:, t, :], ACT.Abs, accum_out=magnitude[:, t:t + 1]).then_inc(magnitude_done, 1)
                act.wait_ge(xt_ps, t + 1)
                act.activation(xt_hi[:, :, t * P:(t + 1) * P], ps_t[:, t % 2, :].rearrange("p (c n) -> p c n", c=DC),
                               ACT.Copy).then_inc(xt_hi_done, 1)
            act.wait_ge(gate_loaded, 16)
            act.wait_ge(pads_set, 3)
            act.activation(gate_hi[:, :, :], gate_raw[:, :, :], ACT.Copy).then_inc(gate_hi_done, 1)
            act.wait_ge(small_loaded, 64)
            act.activation(b2_hi[:, :, :], b2_raw[:, :, :], ACT.Copy).then_inc(b2_hi_done, 1)
            act.wait_ge(b1_ps, 1)
            act.activation(b1_cols[:, :, :], ps_h[:, 0, 0:E * FC].rearrange("p (e c) -> p e c", e=E), ACT.Copy).then_inc(b1_done, 1)
            for i in range(PIECES):
                split_hi(0, i)
            act.wait_ge(centred, 1)
            act.activation(scores[:, :, :], scores[:, :, :], ACT.Exp).then_inc(exp_done, 1)
            act.wait_ge(b1_done, 1)
            for e in range(E):
                for s in range(STEPS):
                    tc, f, n = s // FC, s % FC, STEPS * e + s
                    act.wait_ge(h_ps, n + 1)
                    if n >= 2:
                        act.wait_ge(act_done, n - 1)
                    act.activation(hidden[n % 2][:, :], ps_h[:, n % 2, :], FUNCTIONS[e], bias=b1_cols[:, e, f:f + 1]).then_inc(hidden_done, 1)
                    act.wait_ge(hidden_done, n + 1)
                    act.activation(act_hi[:, f, tc * BANK:(tc + 1) * BANK], hidden[n % 2][:, :], ACT.Copy).then_inc(act_hi_done, 1)
                    if e + 1 < E:
                        split_hi(e + 1, s)

        @block.vector
        def _(dve):
            chain = Chain(dve, router)

            def split_lo(e, i):
                raw, hi, lo = weight_piece(e, i)
                dve.wait_ge(w_hi_done, PIECES * e + i + 1)
                dve.tensor_tensor(lo, raw, hi.bitcast(F32), ALU.subtract).then_inc(w_done, 1)

            for t in range(TILES):
                dve.wait_ge(xt_hi_done, t + 1)
                dve.tensor_tensor(xt_lo[:, :, t * P:(t + 1) * P], ps_t[:, t % 2, :].rearrange("p (c n) -> p c n", c=DC),
                                  xt_hi[:, :, t * P:(t + 1) * P].bitcast(F32), ALU.subtract).then_inc(xt_done, 1)
            dve.wait_ge(gate_hi_done, 1)
            dve.tensor_tensor(gate_lo[:, :, :], gate_raw[:, :, :], gate_hi[:, :, :].bitcast(F32), ALU.subtract).then_inc(gate_done, 1)
            dve.wait_ge(b2_hi_done, 1)
            dve.tensor_tensor(b2_lo[:, :, :], b2_raw[:, :, :], b2_hi[:, :, :].bitcast(F32), ALU.subtract).then_inc(b2_done, 1)
            dve.wait_ge(strength_ps, 1)
            chain.link(dve.tensor_scalar(strength[:, :], strengths[:, 0, :], 1.0 / (VISION * D), 1e-8, ALU.mult, ALU.add))
            chain.link(dve.reciprocal(strength[:, :], strength[:, :]))
            chain.link(dve.scalar_tensor_tensor(ratio[:, :], strengths[:, 1, :], 1.0 / ((TPB * P - VISION) * D),
                                                strength[:, :], ALU.mult, ALU.mult))
            dve.wait_ge(logits_ps, 1)
            dve.wait_ge(small_loaded, 64)
            chain.link(dve.tensor_tensor(logits[:, :, :], ps_r[:, 0:TILES * EW].rearrange("p (t e) -> p t e", t=TILES)[:, :, 0:E],
                                         gate_rows[:, 1, :].unsqueeze(1).to_broadcast([P, TILES, E]), ALU.add))
            for b in range(batches):
                tiles = slice(TPB * b, TPB * (b + 1))
                chain.link(dve.scalar_tensor_tensor(logits[:, tiles, :], gate_rows[:, 0, :].unsqueeze(1).to_broadcast([P, TPB, E]),
                                                    ratio[:, b:b + 1], logits[:, tiles, :], ALU.mult, ALU.add))
            softmax_rows(dve, chain, scores[:, :, :], logits[:, :, :], row[:, :], row2[:, :], exp_done, centred)
            top_two(dve, chain, scores[:, :, :], ramp[:, :], hit[:, :, :], first[:, :, :], second[:, :, :], rest[:, :, :],
                    row[:, :], best[:, :], runner[:, :])
            chain.link(dve.tensor_tensor(row[:, :], best[:, :], runner[:, :], ALU.add))
            chain.link(dve.tensor_scalar(row[:, :], row[:, :], 1e-8, None, ALU.add))
            chain.link(dve.reciprocal(row[:, :], row[:, :]))
            chain.link(dve.tensor_tensor(best[:, :], best[:, :], row[:, :], ALU.mult))
            chain.link(dve.tensor_tensor(runner[:, :], runner[:, :], row[:, :], ALU.mult))
            dve.tensor_copy(chosen[:, :, 0, :], first[0:1, 0:TILES:TPB, :])
            dve.tensor_copy(chosen[:, :, 1, :], second[0:1, 0:TILES:TPB, :]).then_inc(chosen_done, 1)
            for i in range(PIECES):
                split_lo(0, i)

            def shares():
                dve.wait_ge(choices_ps, 1)
                for b in range(batches):
                    tiles = slice(TPB * b, TPB * (b + 1))
                    pick = lambda i: choices[:, b, i, :].unsqueeze(1).to_broadcast([P, TPB, E])
                    chain.link(dve.tensor_tensor(part[:, tiles, :], pick(0), wide(best[:, tiles], E), ALU.mult))
                    chain.link(dve.tensor_tensor(share[:, tiles, :], pick(1), wide(runner[:, tiles], E), ALU.mult))
                    chain.link(dve.tensor_tensor(share[:, tiles, :], share[:, tiles, :], part[:, tiles, :], ALU.add))

            for e in range(E):
                for s in range(STEPS):
                    tc, f, n = s // FC, s % FC, STEPS * e + s
                    dve.wait_ge(act_hi_done, n + 1)
                    dve.tensor_tensor(act_lo[:, f, tc * BANK:(tc + 1) * BANK], hidden[n % 2][:, :],
                                      act_hi[:, f, tc * BANK:(tc + 1) * BANK].bitcast(F32), ALU.subtract).then_inc(act_done, 1)
                    if e + 1 < E:
                        split_lo(e + 1, s)
                if e == 0:
                    shares()
                for t in range(TILES):
                    n = TILES * e + t
                    dve.wait_ge(y_ps, n + 1)
                    if e:
                        dve.wait_ge(added, TILES * (e - 1) + t + 1)
                    dve.scalar_tensor_tensor(x_res[:, t, :], ps_y[:, n % 2, :], share[:, t, e:e + 1], x_res[:, t, :],
                                             ALU.mult, ALU.add).then_inc(added, 1)


def normed_attention_block(nc, held, ctx_in, wq, bq, wk, bk, fn_w, qn_w, kn_w, x_res, xn, ident, ones):
    B, CTX, D = ctx_in.shape
    TILES = x_res.shape[1]
    QT = TILES // B
    DC = D // P
    KT = -(-CTX // P)
    LAST = CTX - (KT - 1) * P
    WIDTH = CTX + CTX % 2
    BANK = 512
    CHUNKS = [(c, min(BANK, WIDTH - c)) for c in range(0, WIDTH, BANK)]
    HALVES = [(0, 2 * BANK), (2 * BANK, CTX)]
    GROUP = BANK // P
    GROUPS = -(-KT // GROUP)
    EPS = 1e-6
    SCALE = 1.0 / math.sqrt(D)
    WB = 2 * DC
    SMALL = QT + GROUPS * QT
    rows_of = lambda k: LAST if k == KT - 1 else P
    assert len(CHUNKS) == 4 and D == BANK and QT == 2 and GROUPS == 4 and LAST < P

    with ExitStack() as ctx:
        sb = lambda n, s, d=F32: ctx.enter_context(nc.sbuf_tensor(f"c_{n}", s, d))
        sem = lambda n: new_semaphore(nc, held, f"c_{n}")
        raw = sb("raw", [P, KT, D])
        flat = raw[:, :, :].rearrange("p t d -> p (t d)")
        probs = [flat[:, j * WIDTH:(j + 1) * WIDTH] for j in range(QT)]
        query = [flat[:, QT * WIDTH + j * D:QT * WIDTH + (j + 1) * D] for j in range(QT)]
        w_hi, w_lo = sb("w_hi", [P, DC, D], F32R), sb("w_lo", [P, DC, D], F32R)
        f_hi, f_lo = sb("f_hi", [P, KT, D], F32R), sb("f_lo", [P, KT, D], F32R)
        k_hi, k_lo = sb("k_hi", [P, DC, WIDTH], F32R), sb("k_lo", [P, DC, WIDTH], F32R)
        t_hi, t_lo = sb("t_hi", [P, 2, DC, P], F32R), sb("t_lo", [P, 2, DC, P], F32R)
        q_hi, q_lo = sb("q_hi", [P, QT, DC, P], F32R), sb("q_lo", [P, QT, DC, P], F32R)
        bias, row_w, fn_row = sb("bias", [P, D]), sb("row_w", [P, D]), sb("fn_row", [P, D])
        scratch = sb("scratch", [P, D])
        squares, inverse = sb("squares", [P, KT]), sb("inverse", [P, KT])
        half_max, neg_max = sb("half_max", [P, 2]), sb("neg_max", [P, QT])
        half_sum, row_sum, row_inv = sb("half_sum", [P, QT, 2]), sb("row_sum", [P, QT]), sb("row_inv", [P, QT])

        ps_s = ctx.enter_context(nc.psum_tensor("c_ps_s", [P, 4, BANK], F32))
        ps_t = ctx.enter_context(nc.psum_tensor("c_ps_t", [P, 2, BANK], F32))
        ps_p = ctx.enter_context(nc.psum_tensor("c_ps_p", [P, 2, BANK], F32))
        s_flat = ps_s[:, :, :].rearrange("p c n -> p (c n)")

        w_loaded, rows_loaded, ctx_loaded, set_up = sem("w_loaded"), sem("rows_loaded"), sem("ctx_loaded"), sem("set_up")
        w_ps, w_hi_done, w_done = sem("w_ps"), sem("w_hi_done"), sem("w_done")
        x_ps, x_hi_done, x_done = sem("x_ps"), sem("x_hi_done"), sem("x_done")
        qp_ps, q_biased, q_squared, q_eps, q_root, q_inv, q_normed = (sem(n) for n in (
            "qp_ps", "q_biased", "q_squared", "q_eps", "q_root", "q_inv", "q_normed"))
        c_squared, c_eps, c_root, c_inv, f_scaled = (sem(n) for n in ("c_squared", "c_eps", "c_root", "c_inv", "f_scaled"))
        ft_ps, f_hi_done, f_done, ft_hi_done, ft_done = (sem(n) for n in ("ft_ps", "f_hi_done", "f_done", "ft_hi_done", "ft_done"))
        kp_ps, k_biased, k_squared, k_eps, k_root, k_inv, k_normed = (sem(n) for n in (
            "kp_ps", "k_biased", "k_squared", "k_eps", "k_root", "k_inv", "k_normed"))
        kt_ps, kt_hi_done, kt_done = sem("kt_ps"), sem("kt_hi_done"), sem("kt_done")
        q_fetched, qt_ps, qt_hi_done, qt_done = sem("q_fetched"), sem("qt_ps"), sem("qt_hi_done"), sem("qt_done")
        s_ps, max_done, neg_max_done, probs_done = sem("s_ps"), sem("max_done"), sem("neg_max_done"), sem("probs_done")
        sum_done, inv_done = sem("sum_done"), sem("inv_done")
        pt_ps, pt_hi_done, pt_done = sem("pt_ps"), sem("pt_hi_done"), sem("pt_done")
        pv_ps, o_ps, added = sem("pv_ps"), sem("o_ps"), sem("added")
        block = ctx.enter_context(nc.Block())
        by_chunk = lambda bank, n=P: bank.rearrange("p (c n) -> p c n", c=DC)[:, :, 0:n]

        @block.sync
        def _(sp):
            sp.dma_start(raw[:, 0:DC, :], wq.rearrange("(t p) d -> p t d", p=P)).then_inc(w_loaded, 16)
            sp.dma_start(raw[:, DC:2 * DC, :], wk.rearrange("(t p) d -> p t d", p=P)).then_inc(w_loaded, 16)
            sp.dma_start(fn_row[:, :], fn_w.partition_broadcast(P)).then_inc(rows_loaded, 16)
            sp.dma_start(bias[:, :], bq.partition_broadcast(P)).then_inc(rows_loaded, 16)
            sp.dma_start(row_w[:, :], qn_w.partition_broadcast(P)).then_inc(rows_loaded, 16)
            sp.wait_ge(q_normed, TILES)
            sp.dma_start(bias[:, :], bk.partition_broadcast(P)).then_inc(rows_loaded, 16)
            sp.dma_start(row_w[:, :], kn_w.partition_broadcast(P)).then_inc(rows_loaded, 16)
            sp.wait_ge(w_ps, WB)
            with sp.Fori(0, B) as b:
                sp.wait_ge(pt_ps, GROUPS * QT * b)
                sp.dma_start(raw[:, 0:KT - 1, :], ctx_in[b, 0:(KT - 1) * P, :].rearrange("(t p) d -> p t d", p=P)
                             ).then_inc(ctx_loaded, 16)
                sp.dma_start(raw[0:LAST, KT - 1, :], ctx_in[b, (KT - 1) * P:CTX, :]).then_inc(ctx_loaded, 16)

        @block.gpsimd
        def _(pool):
            pool.memset(squares[:, :], 1.0).then_inc(set_up, 1)
            if WIDTH > CTX:
                pool.memset(k_hi[:, :, CTX:WIDTH].bitcast(F32), 0.0).then_inc(set_up, 1)
                pool.memset(k_lo[:, :, CTX:WIDTH].bitcast(F32), 0.0).then_inc(set_up, 1)
            else:
                pool.memset(scratch[:, 0:1], 0.0).then_inc(set_up, 2)

        @block.tensor
        def _(pe):
            def three(out, a_hi, a_lo, m_hi, m_lo, first, last):
                pe.matmul(out, a_hi, m_hi, start=first, stop=False)
                pe.matmul(out, a_hi, m_lo, start=False, stop=False)
                return pe.matmul(out, a_lo, m_hi, start=False, stop=last)

            def transpose_weights(which):
                if which == 0:
                    pe.wait_ge(w_loaded, 32)
                for c in range(DC):
                    n = DC * which + c
                    if n >= 2:
                        pe.wait_ge(w_done, n - 1)
                    for t in range(DC):
                        tr = pe.transpose(ps_t[:, n % 2, t * P:(t + 1) * P], raw[:, DC * which + t, c * P:(c + 1) * P], ident[:, :])
                    tr.then_inc(w_ps, 1)

            def project(bank, n, buf):
                for c in range(DC):
                    mm = three(ps_p[0:n, bank, :], t_hi[:, buf, c, 0:n], t_lo[:, buf, c, 0:n], w_hi[:, c, :], w_lo[:, c, :],
                               c == 0, c == DC - 1)
                return mm

            transpose_weights(0)
            pe.wait_ge(w_done, DC)
            for t in range(TILES):
                if t >= 2:
                    pe.wait_ge(x_done, t - 1)
                for c in range(DC):
                    tr = pe.transpose(ps_t[:, t % 2, c * P:(c + 1) * P], xn[:, t, c * P:(c + 1) * P], ident[:, :])
                tr.then_inc(x_ps, 1)
                pe.wait_ge(x_done, t + 1)
                if t >= 2:
                    pe.wait_ge(q_biased, t - 1)
                project(t % 2, P, t % 2).then_inc(qp_ps, 1)
            pe.wait_ge(x_done, TILES)
            transpose_weights(1)
            pe.wait_ge(w_done, WB)
            with pe.Fori(0, B) as b:
                def transpose_features(t):
                    n = rows_of(t)
                    pe.wait_ge(f_scaled, KT * b + t + 1)
                    if t >= 2:
                        pe.wait_ge(ft_done, KT * b + t - 1)
                    else:
                        pe.wait_ge(pt_done, GROUPS * QT * b)
                    for c in range(DC):
                        tr = pe.transpose(ps_t[:, t % 2, c * P:c * P + n], raw[0:n, t, c * P:(c + 1) * P], ident[0:n, 0:n])
                    tr.then_inc(ft_ps, 1)

                transpose_features(0)
                for t in range(KT):
                    if t + 1 < KT:
                        transpose_features(t + 1)
                    pe.wait_ge(ft_done, KT * b + t + 1)
                    if t >= 2:
                        pe.wait_ge(k_biased, KT * b + t - 1)
                    else:
                        pe.wait_ge(added, QT * b)
                    project(t % 2, rows_of(t), t % 2).then_inc(kp_ps, 1)
                for t in range(KT):
                    n = rows_of(t)
                    pe.wait_ge(k_normed, KT * b + t + 1)
                    if t >= 2:
                        pe.wait_ge(kt_done, KT * b + t - 1)
                    else:
                        pe.wait_ge(ft_done, KT * (b + 1))
                    for c in range(DC):
                        tr = pe.transpose(ps_t[:, t % 2, c * P:c * P + n], raw[0:n, t, c * P:(c + 1) * P], ident[0:n, 0:n])
                    tr.then_inc(kt_ps, 1)
                for j in range(QT):
                    pe.wait_ge(q_fetched, QT * b + j + 1)
                    if j == 0:
                        pe.wait_ge(kt_done, KT * (b + 1))
                    for c in range(DC):
                        tr = pe.transpose(ps_t[:, j, c * P:(c + 1) * P], query[j][:, c * P:(c + 1) * P], ident[:, :])
                    tr.then_inc(qt_ps, 1)
                pe.wait_ge(set_up, 3)

                def scores(j):
                    pe.wait_ge(qt_done, QT * b + j + 1)
                    for half in range(2):
                        pe.wait_ge(probs_done, 2 * QT * b + (2 * j + half - 1 if j else 0))
                        for ch in (2 * half, 2 * half + 1):
                            c0, n = CHUNKS[ch]
                            for c in range(DC):
                                mm = three(ps_s[:, ch, 0:n], q_hi[:, j, c, :], q_lo[:, j, c, :], k_hi[:, c, c0:c0 + n],
                                           k_lo[:, c, c0:c0 + n], c == 0, c == DC - 1)
                        mm.then_inc(s_ps, 1)

                def transpose_probs(j, g):
                    n = GROUPS * j + g
                    if g == 0:
                        pe.wait_ge(probs_done, 2 * QT * b + 2 * j + 2)
                    if n >= 2:
                        pe.wait_ge(pt_done, GROUPS * QT * b + n - 1)
                    else:
                        pe.wait_ge(qt_done, QT * (b + 1))
                    for k in range(GROUP * g, min(GROUP * (g + 1), KT)):
                        r = rows_of(k)
                        tr = pe.transpose(ps_t[0:r, n % 2, (k % GROUP) * P:(k % GROUP + 1) * P], probs[j][:, k * P:k * P + r], ident[:, :])
                    tr.then_inc(pt_ps, 1)

                def weigh(j, g):
                    n = GROUPS * j + g
                    pe.wait_ge(pt_done, GROUPS * QT * b + n + 1)
                    if g == 0:
                        pe.wait_ge(k_biased, KT * (b + 1))
                    for k in range(GROUP * g, min(GROUP * (g + 1), KT)):
                        r = rows_of(k)
                        mm = three(ps_p[:, j, :], t_hi[0:r, n % 2, k % GROUP, :], t_lo[0:r, n % 2, k % GROUP, :],
                                   f_hi[0:r, k, :], f_lo[0:r, k, :], k == 0, k == KT - 1)
                    if g == GROUPS - 1:
                        mm.then_inc(o_ps, 1)
                    else:
                        mm.then_inc(pv_ps, 1)

                scores(0)
                scores(1)
                for j in range(QT):
                    transpose_probs(j, 0)
                    for g in range(GROUPS):
                        if g + 1 < GROUPS:
                            transpose_probs(j, g + 1)
                        weigh(j, g)

        @block.scalar
        def _(act):
            def weights_hi(n):
                act.wait_ge(w_ps, n + 1)
                if n >= DC:
                    act.wait_ge(qp_ps, TILES)
                act.activation(w_hi[:, n % DC, :], ps_t[:, n % 2, :], ACT.Copy).then_inc(w_hi_done, 1)

            for c in range(DC):
                weights_hi(c)
            for t in range(TILES):
                act.wait_ge(x_ps, t + 1)
                if t >= 2:
                    act.wait_ge(qp_ps, t - 1)
                act.activation(t_hi[:, t % 2, :, :], by_chunk(ps_t[:, t % 2, :]), ACT.Copy).then_inc(x_hi_done, 1)
                act.wait_ge(q_biased, t + 1)
                if t:
                    act.wait_ge(q_squared, t)
                else:
                    act.wait_ge(set_up, 3)
                act.activation(scratch[:, :], xn[:, t, :], ACT.Square, accum_out=squares[:, t:t + 1]).then_inc(q_squared, 1)
            act.wait_ge(q_eps, 1)
            act.activation(inverse[:, 0:TILES], squares[:, 0:TILES], ACT.Sqrt).then_inc(q_root, 1)
            for c in range(DC):
                weights_hi(DC + c)
            with act.Fori(0, B) as b:
                act.wait_ge(ctx_loaded, 32 * (b + 1))
                act.wait_ge(q_squared, TILES)
                act.wait_ge(q_inv, 1)
                act.wait_ge(k_squared, KT * b)
                act.wait_ge(k_inv, b)
                for t in range(KT):
                    n = rows_of(t)
                    if t:
                        act.wait_ge(c_squared, KT * b + t)
                    act.activation(scratch[0:n, :], raw[0:n, t, :], ACT.Square, accum_out=squares[0:n, t:t + 1]).then_inc(c_squared, 1)
                act.wait_ge(c_eps, b + 1)
                act.activation(inverse[:, :], squares[:, :], ACT.Sqrt).then_inc(c_root, 1)

                def square_projected(t):
                    n = rows_of(t)
                    act.wait_ge(k_biased, KT * b + t + 1)
                    if t:
                        act.wait_ge(k_squared, KT * b + t)
                    act.activation(scratch[0:n, :], raw[0:n, t, :], ACT.Square, accum_out=squares[0:n, t:t + 1]).then_inc(k_squared, 1)

                for t in range(KT):
                    n = rows_of(t)
                    act.wait_ge(f_scaled, KT * b + t + 1)
                    act.activation(f_hi[0:n, t, :], raw[0:n, t, :], ACT.Copy).then_inc(f_hi_done, 1)
                    act.wait_ge(ft_ps, KT * b + t + 1)
                    if t >= 2:
                        act.wait_ge(kp_ps, KT * b + t - 1)
                    act.activation(t_hi[:, t % 2, :, 0:n], by_chunk(ps_t[:, t % 2, :], n), ACT.Copy).then_inc(ft_hi_done, 1)
                    if t >= 2:
                        square_projected(t - 2)
                square_projected(KT - 2)
                square_projected(KT - 1)
                act.wait_ge(k_eps, b + 1)
                act.activation(inverse[:, :], squares[:, :], ACT.Sqrt).then_inc(k_root, 1)
                for t in range(KT):
                    n = rows_of(t)
                    act.wait_ge(kt_ps, KT * b + t + 1)
                    act.activation(k_hi[:, :, t * P:t * P + n], by_chunk(ps_t[:, t % 2, :], n), ACT.Copy).then_inc(kt_hi_done, 1)
                for j in range(QT):
                    act.wait_ge(qt_ps, QT * b + j + 1)
                    act.activation(q_hi[:, j, :, :], by_chunk(ps_t[:, j, :]), ACT.Copy).then_inc(qt_hi_done, 1)

                def exponentials(j):
                    act.wait_ge(neg_max_done, QT * b + j + 1)
                    act.wait_ge(qt_ps, QT * (b + 1))
                    for half, (lo, hi) in enumerate(HALVES):
                        act.activation(probs[j][:, lo:hi], s_flat[:, lo:hi], ACT.Exp, bias=neg_max[:, j:j + 1], scale=SCALE,
                                       accum_out=half_sum[:, j, half:half + 1]).then_inc(probs_done, 1)

                exponentials(0)
                exponentials(1)
                for j in range(QT):
                    for g in range(GROUPS):
                        n = GROUPS * j + g
                        m = min(GROUP, KT - GROUP * g)
                        r = P if m > 1 else LAST
                        act.wait_ge(pt_ps, GROUPS * QT * b + n + 1)
                        if n >= 2:
                            if (n - 2) % GROUPS == GROUPS - 1:
                                act.wait_ge(o_ps, QT * b + (n - 2) // GROUPS + 1)
                            else:
                                act.wait_ge(pv_ps, (GROUPS - 1) * (QT * b + (n - 2) // GROUPS) + (n - 2) % GROUPS + 1)
                        act.activation(t_hi[0:r, n % 2, 0:m, :], by_chunk(ps_t[:, n % 2, :])[0:r, 0:m, :], ACT.Copy).then_inc(pt_hi_done, 1)

        @block.vector
        def _(dve):
            def weights_lo(n):
                dve.wait_ge(w_hi_done, n + 1)
                dve.tensor_tensor(w_lo[:, n % DC, :], ps_t[:, n % 2, :], w_hi[:, n % DC, :].bitcast(F32), ALU.subtract).then_inc(w_done, 1)

            def inverse_root(eps_done, root_done, inv, n, cols):
                dve.tensor_scalar(squares[:, 0:cols], squares[:, 0:cols], 1.0 / D, EPS, ALU.mult, ALU.add).then_inc(eps_done, 1)
                dve.wait_ge(root_done, n)
                dve.reciprocal(inverse[:, 0:cols], inverse[:, 0:cols]).then_inc(inv, 1)
                dve.wait_ge(inv, n)

            for c in range(DC):
                weights_lo(c)
            dve.wait_ge(rows_loaded, 48)
            for t in range(TILES):
                dve.wait_ge(x_hi_done, t + 1)
                dve.tensor_tensor(t_lo[:, t % 2, :, :], by_chunk(ps_t[:, t % 2, :]), t_hi[:, t % 2, :, :].bitcast(F32),
                                  ALU.subtract).then_inc(x_done, 1)
                dve.wait_ge(qp_ps, t + 1)
                dve.tensor_tensor(xn[:, t, :], ps_p[:, t % 2, :], bias[:, :], ALU.add).then_inc(q_biased, 1)
            dve.wait_ge(q_squared, TILES)
            inverse_root(q_eps, q_root, q_inv, 1, TILES)
            for t in range(TILES):
                dve.scalar_tensor_tensor(xn[:, t, :], xn[:, t, :], inverse[:, t:t + 1], row_w[:, :], ALU.mult, ALU.mult).then_inc(q_normed, 1)
            for c in range(DC):
                weights_lo(DC + c)
            with dve.Fori(0, B) as b:
                dve.wait_ge(c_squared, KT * (b + 1))
                inverse_root(c_eps, c_root, c_inv, b + 1, KT)
                dve.wait_ge(rows_loaded, 80)
                dve.wait_ge(q_normed, TILES)

                def scale_features(t):
                    n = rows_of(t)
                    dve.scalar_tensor_tensor(raw[0:n, t, :], raw[0:n, t, :], inverse[0:n, t:t + 1], fn_row[0:n, :], ALU.mult,
                                             ALU.mult).then_inc(f_scaled, 1)

                def add_bias(t):
                    n = rows_of(t)
                    dve.wait_ge(kp_ps, KT * b + t + 1)
                    dve.wait_ge(f_done, KT * b + t + 1)
                    dve.tensor_tensor(raw[0:n, t, :], ps_p[0:n, t % 2, :], bias[0:n, :], ALU.add).then_inc(k_biased, 1)

                scale_features(0)
                for t in range(KT):
                    n = rows_of(t)
                    if t + 1 < KT:
                        scale_features(t + 1)
                    dve.wait_ge(ft_hi_done, KT * b + t + 1)
                    dve.tensor_tensor(t_lo[:, t % 2, :, 0:n], by_chunk(ps_t[:, t % 2, :], n), t_hi[:, t % 2, :, 0:n].bitcast(F32),
                                      ALU.subtract).then_inc(ft_done, 1)
                    dve.wait_ge(f_hi_done, KT * b + t + 1)
                    dve.tensor_tensor(f_lo[0:n, t, :], raw[0:n, t, :], f_hi[0:n, t, :].bitcast(F32), ALU.subtract).then_inc(f_done, 1)
                    if t:
                        add_bias(t - 1)
                add_bias(KT - 1)
                dve.wait_ge(k_squared, KT * (b + 1))
                inverse_root(k_eps, k_root, k_inv, b + 1, KT)

                def norm_key(t):
                    n = rows_of(t)
                    dve.scalar_tensor_tensor(raw[0:n, t, :], raw[0:n, t, :], inverse[0:n, t:t + 1], row_w[0:n, :], ALU.mult,
                                             ALU.mult).then_inc(k_normed, 1)

                norm_key(0)
                norm_key(1)
                for t in range(KT):
                    n = rows_of(t)
                    if t + 2 < KT:
                        norm_key(t + 2)
                    dve.wait_ge(kt_hi_done, KT * b + t + 1)
                    dve.tensor_tensor(k_lo[:, :, t * P:t * P + n], by_chunk(ps_t[:, t % 2, :], n),
                                      k_hi[:, :, t * P:t * P + n].bitcast(F32), ALU.subtract).then_inc(kt_done, 1)
                for j in range(QT):
                    dve.tensor_copy(query[j], xn[:, bass.ds(QT * b + j, 1), :].rearrange("p a d -> p (a d)")).then_inc(q_fetched, 1)
                for j in range(QT):
                    dve.wait_ge(qt_hi_done, QT * b + j + 1)
                    dve.tensor_tensor(q_lo[:, j, :, :], by_chunk(ps_t[:, j, :]), q_hi[:, j, :, :].bitcast(F32), ALU.subtract).then_inc(qt_done, 1)
                for j in range(QT):
                    for half, (lo, hi) in enumerate(HALVES):
                        dve.wait_ge(s_ps, 2 * QT * b + 2 * j + half + 1)
                        dve.reduce_max(half_max[:, half:half + 1], s_flat[:, lo:hi], AX.X).then_inc(max_done, 1)
                    dve.wait_ge(max_done, 2 * QT * b + 2 * j + 2)
                    dve.tensor_scalar(neg_max[:, j:j + 1], half_max[:, 0:1], half_max[:, 1:2], -SCALE, ALU.max,
                                      ALU.mult).then_inc(neg_max_done, 1)
                for j in range(QT):
                    for g in range(GROUPS):
                        n = GROUPS * j + g
                        m = min(GROUP, KT - GROUP * g)
                        r = P if m > 1 else LAST
                        dve.wait_ge(pt_hi_done, GROUPS * QT * b + n + 1)
                        dve.tensor_tensor(t_lo[0:r, n % 2, 0:m, :], by_chunk(ps_t[:, n % 2, :])[0:r, 0:m, :],
                                          t_hi[0:r, n % 2, 0:m, :].bitcast(F32), ALU.subtract).then_inc(pt_done, 1)
                    if j == 0:
                        dve.wait_ge(probs_done, 2 * QT * (b + 1))
                        dve.tensor_tensor(row_sum[:, :], half_sum[:, :, 0], half_sum[:, :, 1], ALU.add).then_inc(sum_done, 1)
                        dve.wait_ge(sum_done, b + 1)
                        dve.reciprocal(row_inv[:, :], row_sum[:, :]).then_inc(inv_done, 1)
                        dve.wait_ge(inv_done, b + 1)
                    x_tile = x_res[:, bass.ds(QT * b + j, 1), :].rearrange("p a d -> p (a d)")
                    dve.wait_ge(o_ps, QT * b + j + 1)
                    dve.scalar_tensor_tensor(x_tile, ps_p[:, j, :], row_inv[:, j:j + 1], x_tile, ALU.mult, ALU.add).then_inc(added, 1)


def routed_experts_block(nc, held, gate_w, w_gate_up, w_down, shared_gate_up, shared_down, x_res, xn, ident, ones, out):
    TILES, D = x_res.shape[1], x_res.shape[2]
    E, I2, _ = w_gate_up.shape
    I = I2 // 2
    SHARED = shared_down.shape[1] // I
    N = E + SHARED
    DC = D // P
    BANK = 512
    TC = TILES * P // BANK
    TPC = BANK // P
    JOBS = 3
    assert I == P and D == BANK and TC == 2 and E % 2 == 0 and SHARED % 2 == 0

    with ExitStack() as ctx:
        sb = lambda n, s, d=F32: ctx.enter_context(nc.sbuf_tensor(f"d_{n}", s, d))
        sem = lambda n: new_semaphore(nc, held, f"d_{n}")
        xt_hi, xt_lo = sb("xt_hi", [P, DC, TILES * P], F32R), sb("xt_lo", [P, DC, TILES * P], F32R)
        up_raw = [sb(f"up_raw{a}", [P, 2, D]) for a in range(2)]
        down_raw = [sb(f"down_raw{a}", [P, DC, I]) for a in range(2)]
        up_hi = [sb(f"up_hi{a}", [P, 2, DC, I], F32R) for a in range(2)]
        up_lo = [sb(f"up_lo{a}", [P, 2, DC, I], F32R) for a in range(2)]
        down_hi = [sb(f"down_hi{a}", [P, D], F32R) for a in range(2)]
        down_lo = [sb(f"down_lo{a}", [P, D], F32R) for a in range(2)]
        gated = [sb(f"gated{i}", [P, BANK]) for i in range(TC)]
        act_hi, act_lo = sb("act_hi", [P, TC, BANK], F32R), sb("act_lo", [P, TC, BANK], F32R)
        gate_raw, gate_hi, gate_lo = sb("gate_raw", [E, D]), sb("gate_hi", [P, DC, E], F32R), sb("gate_lo", [P, DC, E], F32R)
        ramp = sb("ramp", [P, E])
        logits, scores = sb("logits", [P, TILES, E]), sb("scores", [P, TILES, E])
        hit, first, second, rest = (sb(n, [P, TILES, E]) for n in ("hit", "first", "second", "rest"))
        row, row2, best, runner = (sb(n, [P, TILES]) for n in ("row", "row2", "best", "runner"))
        share = sb("share", [P, TILES, N])

        ps_t = ctx.enter_context(nc.psum_tensor("d_ps_t", [P, 2, BANK], F32))
        ps_h = ctx.enter_context(nc.psum_tensor("d_ps_h", [P, TC, 2, BANK], F32))
        ps_y = ctx.enter_context(nc.psum_tensor("d_ps_y", [P, 2, BANK], F32))

        gate_loaded, pads_set, gate_ps, gate_hi_done, gate_done = (sem(n) for n in (
            "gate_loaded", "pads_set", "gate_ps", "gate_hi_done", "gate_done"))
        xt_ps, xt_hi_done, xt_done, logits_ps = sem("xt_ps"), sem("xt_hi_done"), sem("xt_done"), sem("logits_ps")
        logits_out, centred, exp_done, share_done, router = (sem(n) for n in ("logits_out", "centred", "exp_done", "share_done", "router"))
        raw_loaded = [sem(f"raw_loaded{a}") for a in range(2)]
        w_ps, w_hi_done, w_done = sem("w_ps"), sem("w_hi_done"), sem("w_done")
        h_ps, silu_done, gated_done, act_hi_done, act_done = (sem(n) for n in ("h_ps", "silu_done", "gated_done", "act_hi_done", "act_done"))
        y_ps, added, stored = sem("y_ps"), sem("added"), sem("stored")
        block = ctx.enter_context(nc.Block())
        by_chunk = lambda bank: bank.rearrange("p (c n) -> p c n", c=DC)
        tile_rows = out.rearrange("b (t p) d -> (b t) p d", p=P)

        @block.sync
        def _(sp):
            def load(a, transposed, up, down):
                sp.wait_ge(w_ps, transposed)
                sp.dma_start(up_raw[a][:, :, :], up).then_inc(raw_loaded[a], 16)
                sp.dma_start(down_raw[a][:, :, :], down).then_inc(raw_loaded[a], 16)

            def routed(e):
                return (w_gate_up[bass.ds(e, 1), :, :].rearrange("a (k p) h -> p (a k) h", p=P),
                        w_down[bass.ds(e, 1), :, :].rearrange("a (c p) i -> p (a c) i", p=P))

            def shared(s):
                return (shared_gate_up.rearrange("(k r) h -> r k h", k=2)[bass.ds(s * I, I), :, :],
                        shared_down[:, bass.ds(s * I, I)].rearrange("(c p) i -> p c i", p=P))

            sp.dma_start(gate_raw[:, :], gate_w).then_inc(gate_loaded, 16)
            load(0, 0, *routed(0))
            load(1, 0, *routed(1))
            with sp.Fori(1, E // 2) as i:
                for a in range(2):
                    load(a, JOBS * (2 * i + a - 1), *routed(2 * i + a))
            with sp.Fori(0, SHARED // 2) as i:
                for a in range(2):
                    load(a, JOBS * (E + 2 * i + a - 1), *shared(2 * i + a))
            for t in range(TILES):
                sp.wait_ge(added, TILES * (N - 1) + t + 1)
                sp.dma_start(tile_rows[t], x_res[:, t, :]).then_inc(stored, 16)
            sp.wait_ge(stored, 16 * TILES)

        @block.gpsimd
        def _(pool):
            pool.iota(ramp[:, :], pattern=[[-1, E]], base=E, channel_multiplier=0,
                      allow_small_or_imprecise_dtypes=True).then_inc(pads_set, 1)
            pool.memset(share[:, :, E:N], 1.0).then_inc(pads_set, 1)

        @block.tensor
        def _(pe):
            def three(o, w_hi, w_lo, m_hi, m_lo, start, stop):
                pe.matmul(o, w_hi, m_hi, start=start, stop=False)
                pe.matmul(o, w_hi, m_lo, start=False, stop=False)
                return pe.matmul(o, w_lo, m_hi, start=False, stop=stop)

            def transpose_weights(n, a, pair, first=False):
                pe.wait_ge(raw_loaded[a], 32 * pair + 32)
                for job in range(JOBS):
                    bank = (JOBS * a + job) % 2
                    if not (first and job < 2):
                        pe.wait_ge(w_done, JOBS * n + job - 1)
                    for c in range(DC):
                        src = down_raw[a][:, c, :] if job == 2 else up_raw[a][:, job, c * P:(c + 1) * P]
                        tr = pe.transpose(ps_t[:, bank, c * P:(c + 1) * P], src, ident[:, :])
                    tr.then_inc(w_ps, 1)

            def up(n, a):
                pe.wait_ge(w_done, JOBS * n + JOBS)
                pe.wait_ge(gated_done, TC * n)
                for tc in range(TC):
                    for k in range(2):
                        for c in range(DC):
                            mm = three(ps_h[:, tc, k, :], up_hi[a][:, k, c, :], up_lo[a][:, k, c, :],
                                       xt_hi[:, c, tc * BANK:(tc + 1) * BANK], xt_lo[:, c, tc * BANK:(tc + 1) * BANK],
                                       c == 0, c == DC - 1)
                    mm.then_inc(h_ps, 1)

            def down(n, a):
                for t in range(TILES):
                    tc, p0 = t // TPC, t % TPC * P
                    if t % TPC == 0:
                        pe.wait_ge(act_done, TC * n + tc + 1)
                    pe.wait_ge(added, TILES * n + max(t - 1, 0))
                    three(ps_y[:, t % 2, :], act_hi[:, tc, p0:p0 + P], act_lo[:, tc, p0:p0 + P], down_hi[a][:, :],
                          down_lo[a][:, :], True, True).then_inc(y_ps, 1)

            for t in range(TILES):
                if t >= 2:
                    pe.wait_ge(xt_done, t - 1)
                for c in range(DC):
                    tr = pe.transpose(ps_t[:, t % 2, c * P:(c + 1) * P], xn[:, t, c * P:(c + 1) * P], ident[:, :])
                tr.then_inc(xt_ps, 1)
            pe.wait_ge(gate_loaded, 16)
            for c in range(DC):
                tr = pe.transpose(ps_h[:, 0, 0, c * E:(c + 1) * E], gate_raw[:, c * P:(c + 1) * P], ident[0:E, 0:E])
            tr.then_inc(gate_ps, 1)
            pe.wait_ge(xt_done, TILES)
            transpose_weights(0, 0, 0, first=True)
            pe.wait_ge(gate_done, 1)
            for t in range(TILES):
                for c in range(DC):
                    mm = three(ps_y[:, 0, t * E:(t + 1) * E], xt_hi[:, c, t * P:(t + 1) * P], xt_lo[:, c, t * P:(t + 1) * P],
                               gate_hi[:, c, :], gate_lo[:, c, :], c == 0, c == DC - 1)
            mm.then_inc(logits_ps, 1)
            with pe.Fori(0, N // 2 - 1) as i:
                pe.wait_ge(logits_out, 1)
                up(2 * i, 0)
                transpose_weights(2 * i + 1, 1, i)
                down(2 * i, 0)
                up(2 * i + 1, 1)
                transpose_weights(2 * i + 2, 0, i + 1)
                down(2 * i + 1, 1)
            up(N - 2, 0)
            transpose_weights(N - 1, 1, N // 2 - 1)
            down(N - 2, 0)
            up(N - 1, 1)
            down(N - 1, 1)

        @block.scalar
        def _(act):
            def weights_hi(n, a):
                for job in range(JOBS):
                    bank = ps_t[:, (JOBS * a + job) % 2, :]
                    act.wait_ge(w_ps, JOBS * n + job + 1)
                    if job == 2:
                        act.activation(down_hi[a][:, :], bank, ACT.Copy).then_inc(w_hi_done, 1)
                    else:
                        act.activation(up_hi[a][:, job, :, :], by_chunk(bank), ACT.Copy).then_inc(w_hi_done, 1)

            def hidden(n):
                for tc in range(TC):
                    act.wait_ge(h_ps, TC * n + tc + 1)
                    act.wait_ge(act_done, TC * n)
                    act.activation(gated[tc][:, :], ps_h[:, tc, 0, :], ACT.Silu).then_inc(silu_done, 1)
                    act.wait_ge(gated_done, TC * n + tc + 1)
                    act.wait_ge(y_ps, TILES * n)
                    act.activation(act_hi[:, tc, :], gated[tc][:, :], ACT.Copy).then_inc(act_hi_done, 1)

            for t in range(TILES):
                act.wait_ge(xt_ps, t + 1)
                act.activation(xt_hi[:, :, t * P:(t + 1) * P], by_chunk(ps_t[:, t % 2, :]), ACT.Copy).then_inc(xt_hi_done, 1)
            act.wait_ge(gate_ps, 1)
            act.activation(gate_hi[:, :, :], ps_h[:, 0, 0, 0:DC * E].rearrange("p (c e) -> p c e", c=DC), ACT.Copy).then_inc(gate_hi_done, 1)
            weights_hi(0, 0)
            act.wait_ge(centred, 1)
            act.activation(scores[:, :, :], scores[:, :, :], ACT.Exp).then_inc(exp_done, 1)
            with act.Fori(0, N // 2 - 1) as i:
                hidden(2 * i)
                weights_hi(2 * i + 1, 1)
                hidden(2 * i + 1)
                weights_hi(2 * i + 2, 0)
            hidden(N - 2)
            weights_hi(N - 1, 1)
            hidden(N - 1)

        @block.vector
        def _(dve):
            chain = Chain(dve, router)

            def weights_lo(n, a):
                for job in range(JOBS):
                    bank = ps_t[:, (JOBS * a + job) % 2, :]
                    dve.wait_ge(w_hi_done, JOBS * n + job + 1)
                    if job == 2:
                        dve.tensor_tensor(down_lo[a][:, :], bank, down_hi[a][:, :].bitcast(F32), ALU.subtract).then_inc(w_done, 1)
                    else:
                        dve.tensor_tensor(up_lo[a][:, job, :, :], by_chunk(bank), up_hi[a][:, job, :, :].bitcast(F32),
                                          ALU.subtract).then_inc(w_done, 1)

            def hidden(n):
                for tc in range(TC):
                    dve.wait_ge(silu_done, TC * n + tc + 1)
                    dve.tensor_tensor(gated[tc][:, :], ps_h[:, tc, 1, :], gated[tc][:, :], ALU.mult).then_inc(gated_done, 1)
                    dve.wait_ge(act_hi_done, TC * n + tc + 1)
                    dve.tensor_tensor(act_lo[:, tc, :], gated[tc][:, :], act_hi[:, tc, :].bitcast(F32), ALU.subtract).then_inc(act_done, 1)

            def add(n):
                for t in range(TILES):
                    dve.wait_ge(y_ps, TILES * n + t + 1)
                    dve.wait_ge(added, TILES * n)
                    dve.scalar_tensor_tensor(x_res[:, t, :], ps_y[:, t % 2, :], share[:, t, bass.ds(n, 1)], x_res[:, t, :],
                                             ALU.mult, ALU.add).then_inc(added, 1)

            for t in range(TILES):
                dve.wait_ge(xt_hi_done, t + 1)
                dve.tensor_tensor(xt_lo[:, :, t * P:(t + 1) * P], by_chunk(ps_t[:, t % 2, :]),
                                  xt_hi[:, :, t * P:(t + 1) * P].bitcast(F32), ALU.subtract).then_inc(xt_done, 1)
            dve.wait_ge(gate_hi_done, 1)
            dve.tensor_tensor(gate_lo[:, :, :], ps_h[:, 0, 0, 0:DC * E].rearrange("p (c e) -> p c e", c=DC),
                              gate_hi[:, :, :].bitcast(F32), ALU.subtract).then_inc(gate_done, 1)
            weights_lo(0, 0)
            dve.wait_ge(logits_ps, 1)
            dve.tensor_copy(logits[:, :, :], ps_y[:, 0, 0:TILES * E].rearrange("p (t e) -> p t e", t=TILES)).then_inc(logits_out, 1)
            dve.wait_ge(logits_out, 1)
            softmax_rows(dve, chain, scores[:, :, :], logits[:, :, :], row[:, :], row2[:, :], exp_done, centred)
            dve.wait_ge(pads_set, 2)
            top_two(dve, chain, scores[:, :, :], ramp[:, :], hit[:, :, :], first[:, :, :], second[:, :, :], rest[:, :, :],
                    row[:, :], best[:, :], runner[:, :])
            chain.link(dve.tensor_tensor(row[:, :], best[:, :], runner[:, :], ALU.add))
            chain.link(dve.reciprocal(row[:, :], row[:, :]))
            chain.link(dve.tensor_tensor(best[:, :], best[:, :], row[:, :], ALU.mult))
            chain.link(dve.tensor_tensor(runner[:, :], runner[:, :], row[:, :], ALU.mult))
            chain.link(dve.tensor_tensor(first[:, :, :], first[:, :, :], wide(best[:, :], E), ALU.mult))
            chain.link(dve.tensor_tensor(second[:, :, :], second[:, :, :], wide(runner[:, :], E), ALU.mult))
            chain.link(dve.tensor_tensor(share[:, :, 0:E], first[:, :, :], second[:, :, :], ALU.add))
            with dve.Fori(0, N // 2 - 1) as i:
                hidden(2 * i)
                weights_lo(2 * i + 1, 1)
                add(2 * i)
                hidden(2 * i + 1)
                weights_lo(2 * i + 2, 0)
                add(2 * i + 1)
            hidden(N - 2)
            weights_lo(N - 1, 1)
            add(N - 2)
            hidden(N - 1)
            add(N - 1)


def layers(nc, x, ctx_4096, L0_xattn_Wq, L0_xattn_Wk, L0_xattn_Wv, L0_xattn_Wo, L0_ffn_gate_w, L0_ffn_gate_b, L0_ffn_w1,
           L0_ffn_b1, L0_ffn_w2, L0_ffn_b2, L1_xattn_Wq_w, L1_xattn_Wq_b, L1_xattn_Wk_w, L1_xattn_Wk_b, L1_xattn_fn_w,
           L1_xattn_qn_w, L1_xattn_kn_w, L1_ffn_gate_w, L1_ffn_w_gate_up, L1_ffn_w_down, L1_ffn_shared_w_gate_up,
           L1_ffn_shared_w_down, out):
    B, S, D = x.shape
    held = []
    with ExitStack() as ctx:
        sb = lambda n, s: ctx.enter_context(nc.sbuf_tensor(n, s, F32))
        x_res, xn = sb("x_res", [P, B * S // P, D]), sb("xn", [P, B * S // P, D])
        ident, ones = sb("ident", [P, P]), sb("ones", [P, P])
        norm_block(nc, held, x_res, xn, 1e-5, "norm0", load_from=x, constants=(ident, ones))
        grouped_attention_block(nc, held, ctx_4096, L0_xattn_Wq, L0_xattn_Wk, L0_xattn_Wv, L0_xattn_Wo, x_res, xn, ident, ones)
        release(nc, held)
        norm_block(nc, held, x_res, xn, 1e-5, "norm1")
        gated_experts_block(nc, held, L0_ffn_gate_w, L0_ffn_gate_b, L0_ffn_w1, L0_ffn_b1, L0_ffn_w2, L0_ffn_b2, x_res, xn, ident,
                            ones, B)
        release(nc, held)
        norm_block(nc, held, x_res, xn, 1e-5, "norm2")
        normed_attention_block(nc, held, ctx_4096, L1_xattn_Wq_w, L1_xattn_Wq_b, L1_xattn_Wk_w, L1_xattn_Wk_b, L1_xattn_fn_w,
                               L1_xattn_qn_w, L1_xattn_kn_w, x_res, xn, ident, ones)
        release(nc, held)
        norm_block(nc, held, x_res, xn, 1e-5, "norm3")
        routed_experts_block(nc, held, L1_ffn_gate_w, L1_ffn_w_gate_up, L1_ffn_w_down, L1_ffn_shared_w_gate_up,
                             L1_ffn_shared_w_down, x_res, xn, ident, ones, out)


_INS = ["x", "ctx_4096", "L0_xattn_Wq", "L0_xattn_Wk", "L0_xattn_Wv", "L0_xattn_Wo", "L0_ffn_gate_w", "L0_ffn_gate_b",
        "L0_ffn_w1", "L0_ffn_b1", "L0_ffn_w2", "L0_ffn_b2", "L1_xattn_Wq_w", "L1_xattn_Wq_b", "L1_xattn_Wk_w",
        "L1_xattn_Wk_b", "L1_xattn_fn_w", "L1_xattn_qn_w", "L1_xattn_kn_w", "L1_ffn_gate_w", "L1_ffn_w_gate_up",
        "L1_ffn_w_down", "L1_ffn_shared_w_gate_up", "L1_ffn_shared_w_down"]


def kernel(**inputs):
    import concourse.bacc as _bacc
    import numpy as _np
    from concourse.bass_utils import run_bass_kernel_spmd as _run

    nc = _bacc.Bacc("TRN2", target_bir_lowering=False, num_devices=1)
    arrays, args = {}, []
    for name in _INS:
        a = _np.ascontiguousarray(inputs[name])
        arrays[f"in_{name}"] = a
        args.append(nc.dram_tensor(f"in_{name}", a.shape, mybir.dt.from_np(a.dtype), kind="ExternalInput").ap())
    out = nc.dram_tensor("out_x", inputs["x"].shape, F32, kind="ExternalOutput").ap()
    layers(nc, *args, out)
    return _run(nc, [arrays], core_ids=[0]).results[0]["out_x"]
```

```python
import math
from contextlib import ExitStack

import concourse.bass as bass
from concourse import mybir

F32 = mybir.dt.float32
F32R = mybir.dt.float32r
ALU = mybir.AluOpType
ACT = mybir.ActivationFunctionType
AX = mybir.AxisListType
P = 128


def new_semaphore(nc, held, name):
    held.append(nc.alloc_semaphore(name=name))
    return held[-1]


def release(nc, held):
    nc.clear_and_free_semaphores(list(held))
    nc.all_engine_barrier()
    held.clear()


def norm_block(nc, held, x_res, xn, eps, name, load_from=None, constants=None):
    tiles = x_res.shape[1]
    with ExitStack() as ctx:
        sb = lambda n, s, d=F32: ctx.enter_context(nc.sbuf_tensor(f"{name}_{n}", s, d))
        sem = lambda n: new_semaphore(nc, held, f"{name}_{n}")
        stats = sb("stats", [P, tiles, 6])
        mean_var = sb("mean_var", [P, tiles, 2])
        var_eps = sb("var_eps", [P, tiles])
        deviation = sb("deviation", [P, tiles])
        inverse = sb("inverse", [P, tiles])
        x_loaded = [sem(f"x_loaded{t}") for t in range(tiles)] if load_from is not None else None
        zeroed, constants_ready = sem("zeroed"), sem("constants_ready")
        stats_done, mean_done, var_done = sem("stats_done"), sem("mean_done"), sem("var_done")
        deviation_done, inverse_done, normed = sem("deviation_done"), sem("inverse_done"), sem("normed")
        block = ctx.enter_context(nc.Block())

        if load_from is not None:
            rows = load_from.rearrange("b (t p) d -> (b t) p d", p=P)

            @block.sync
            def _(sp):
                for t in range(tiles):
                    sp.dma_start(x_res[:, t, :], rows[t]).then_inc(x_loaded[t], 16)

            @block.gpsimd
            def _(pool):
                ident, ones = constants
                pool.memset(ident[:, :], 0.0).then_inc(zeroed, 1)
                pool.memset(ones[:, :], 1.0).then_inc(constants_ready, 1)
                pool.wait_ge(zeroed, 1)
                pool.affine_select(out=ident[:, :], in_=ident[:, :], compare_op=ALU.not_equal, fill=1.0,
                                   base=0, pattern=[[-1, P]], channel_multiplier=1).then_inc(constants_ready, 1)

        @block.vector
        def _(dve):
            for t in range(tiles):
                if x_loaded:
                    dve.wait_ge(x_loaded[t], 16)
                dve.bn_stats(stats[:, t, :], x_res[:, t, :]).then_inc(stats_done, 1)
            for t in range(tiles):
                dve.wait_ge(stats_done, t + 1)
                dve.bn_aggr(mean_var[:, t, :], stats[:, t, :]).then_inc(mean_done, 1)
            dve.wait_ge(mean_done, tiles)
            dve.tensor_scalar(var_eps[:, :], mean_var[:, :, 1], eps, None, ALU.add).then_inc(var_done, 1)
            dve.wait_ge(deviation_done, 1)
            dve.reciprocal(inverse[:, :], deviation[:, :]).then_inc(inverse_done, 1)
            dve.wait_ge(inverse_done, 1)
            for t in range(tiles):
                dve.tensor_scalar(xn[:, t, :], x_res[:, t, :], mean_var[:, t, 0:1], inverse[:, t:t + 1],
                                  ALU.subtract, ALU.mult).then_inc(normed, 1)

        @block.scalar
        def _(act):
            act.wait_ge(var_done, 1)
            act.activation(deviation[:, :], var_eps[:, :], ACT.Sqrt).then_inc(deviation_done, 1)


def grouped_attention_block(nc, held, ctx_in, wq, wk, wv, wo, x_res, xn, ident, ones):
    B, CTX, D = ctx_in.shape
    TOK = x_res.shape[1] * P // B
    QT = TOK // P
    DC = D // P
    HD = P
    KVH = wk.shape[1] // HD
    HPG = wq.shape[1] // HD // KVH
    KEYS = TOK + CTX
    WIDTH = KEYS + KEYS % 2
    KT = -(-KEYS // P)
    LAST = KEYS - (KT - 1) * P
    PAIRS = -(-KT // 2)
    BANK = 512
    CHUNKS = [(c, min(BANK, WIDTH - c)) for c in range(0, WIDTH, BANK)]
    HALVES = [(0, 2 * BANK), (2 * BANK, KEYS)]
    FIRST_PAIRS = 2 * BANK // (2 * P)
    LAT = TOK // P
    STAGES = 3
    SCALE = 1.0 / math.sqrt(HD)
    VG = -(-KT // 4)
    VPIECES = [(4 * q, 4, P) for q in range(VG - 1)] + [(4 * (VG - 1), KT - 1 - 4 * (VG - 1), P), (KT - 1, 1, LAST)]
    rows_of = lambda k: LAST if k == KT - 1 else P
    assert QT == 2 and len(CHUNKS) == 4 and HPG == 8 and KT % STAGES == 0 and KT - 1 - 4 * (VG - 1) > 0

    with ExitStack() as ctx:
        sb = lambda n, s, d=F32: ctx.enter_context(nc.sbuf_tensor(f"a_{n}", s, d))
        sem = lambda n: new_semaphore(nc, held, f"a_{n}")
        stage = [sb(f"stage{i}", [P, D]) for i in range(STAGES)]
        hid_hi, hid_lo = sb("hid_hi", [P, DC, WIDTH], F32R), sb("hid_lo", [P, DC, WIDTH], F32R)
        k_hi, k_lo = sb("k_hi", [P, WIDTH], F32R), sb("k_lo", [P, WIDTH], F32R)
        v_hi, v_lo = sb("v_hi", [P, KT, HD], F32R), sb("v_lo", [P, KT, HD], F32R)
        probs = [[sb(f"probs{a}{j}", [P, WIDTH]) for j in range(QT)] for a in range(2)]
        v_t = probs[1][1]
        pt_hi, pt_lo = sb("pt_hi", [P, 2, 2, TOK], F32R), sb("pt_lo", [P, 2, 2, TOK], F32R)
        q_hi, q_lo = [sb(f"q_hi{a}", [P, TOK], F32R) for a in range(2)], [sb(f"q_lo{a}", [P, TOK], F32R) for a in range(2)]
        wkv_raw = sb("wkv_raw", [P, 2, DC, HD])
        wkv_hi, wkv_lo = sb("wkv_hi", [P, 2, DC, HD], F32R), sb("wkv_lo", [P, 2, DC, HD], F32R)
        wq_raw, wo_raw = sb("wq_raw", [P, DC, HD]), sb("wo_raw", [P, D])
        wq_hi = [sb(f"wq_hi{a}", [P, DC, HD], F32R) for a in range(2)]
        wq_lo = [sb(f"wq_lo{a}", [P, DC, HD], F32R) for a in range(2)]
        wo_hi = [sb(f"wo_hi{a}", [P, D], F32R) for a in range(2)]
        wo_lo = [sb(f"wo_lo{a}", [P, D], F32R) for a in range(2)]
        o_f, o_hi, o_lo = sb("o_f", [P, TOK]), sb("o_hi", [P, TOK], F32R), sb("o_lo", [P, TOK], F32R)
        diag, inv_wide = sb("diag", [P, TOK]), sb("inv_wide", [P, TOK])
        half_max, neg_max = sb("half_max", [P, 2]), sb("neg_max", [P, QT])
        half_sum, row_sum, row_inv = sb("half_sum", [P, 2, QT, 2]), sb("row_sum", [P, QT]), sb("row_inv", [P, QT])

        ps_s = ctx.enter_context(nc.psum_tensor("a_ps_s", [P, 4, BANK], F32))
        ps_t = ctx.enter_context(nc.psum_tensor("a_ps_t", [P, 2, BANK], F32))
        ps_o = ctx.enter_context(nc.psum_tensor("a_ps_o", [P, BANK], F32))
        ps_m = ctx.enter_context(nc.psum_tensor("a_ps_m", [P, BANK], F32))
        s_flat = ps_s[:, :, :].rearrange("p c n -> p (c n)")

        pad_zeroed = sem("pad_zeroed")
        stage_loaded = [sem(f"stage_loaded{i}") for i in range(STAGES)]
        stage_copied, hid_ps, hid_hi_done, hid_done = sem("stage_copied"), sem("hid_ps"), sem("hid_hi_done"), sem("hid_done")
        wkv_loaded, wkv_hi_done, wkv_ready = sem("wkv_loaded"), sem("wkv_hi_done"), sem("wkv_ready")
        wq_loaded, wq_hi_done, wq_ready = sem("wq_loaded"), sem("wq_hi_done"), sem("wq_ready")
        wo_loaded, wo_hi_done, wo_ready = sem("wo_loaded"), sem("wo_hi_done"), sem("wo_ready")
        kv_ps, k_hi_done, k_done, vt_done = sem("kv_ps"), sem("k_hi_done"), sem("k_done"), sem("vt_done")
        v_ps, v_hi_done, v_done = sem("v_ps"), sem("v_hi_done"), sem("v_done")
        q_ps, q_hi_done, q_done = sem("q_ps"), sem("q_hi_done"), sem("q_done")
        s_ps, max_done, neg_max_done, probs_done = sem("s_ps"), sem("max_done"), sem("neg_max_done"), sem("probs_done")
        sum_done, inv_done, diag_done, inv_ps = sem("sum_done"), sem("inv_done"), sem("diag_done"), sem("inv_ps")
        pt_ps, pt_hi_done, pt_done, pv_ps = sem("pt_ps"), sem("pt_hi_done"), sem("pt_done"), sem("pv_ps")
        o_f_done, o_hi_done, o_done = sem("o_f_done"), sem("o_hi_done"), sem("o_done")
        wo_ps, wo_added, inv_copied = sem("wo_ps"), sem("wo_added"), sem("inv_copied")
        block = ctx.enter_context(nc.Block())

        wk_v = wk.rearrange("(c p) n -> p c n", p=P)
        wv_v = wv.rearrange("(c p) n -> p c n", p=P)
        wq_v = wq.rearrange("(c p) n -> p c n", p=P)

        @block.sync
        def _(sp):
            def load_wq(u, head):
                sp.wait_ge(wq_ready, u)
                sp.dma_start(wq_raw[:, :, :], wq_v[:, :, bass.ds(head * HD, HD)]).then_inc(wq_loaded, 16)

            def load_wo(u, head):
                sp.wait_ge(wo_ready, u)
                sp.dma_start(wo_raw[:, :], wo[bass.ds(head * HD, HD), :]).then_inc(wo_loaded, 16)

            def load_wkv(G, g):
                sp.wait_ge(wkv_ready, G)
                sp.dma_start(wkv_raw[:, 0, :, :], wk_v[:, :, bass.ds(g * HD, HD)]).then_inc(wkv_loaded, 16)
                sp.dma_start(wkv_raw[:, 1, :, :], wv_v[:, :, bass.ds(g * HD, HD)]).then_inc(wkv_loaded, 16)

            def load_context(i, b):
                for r in range(LAT, KT):
                    sp.wait_ge(hid_ps, KT * i + (r - STAGES + 1 if r >= STAGES else 0))
                    n = rows_of(r)
                    sp.dma_start(stage[r % STAGES][0:n, :], ctx_in[b, (r - LAT) * P:(r - LAT) * P + n, :]
                                 ).then_inc(stage_loaded[r % STAGES], 16)

            load_wkv(0, 0)
            load_wq(0, 0)
            load_context(0, 0)
            with sp.Fori(0, B) as b:
                with sp.Fori(0, KVH) as g:
                    G = b * KVH + g
                    u0 = G * HPG
                    with sp.Fori(0, HPG - 2) as h:
                        load_wq(u0 + h + 1, g * HPG + h + 1)
                        load_wo(u0 + h, g * HPG + h)
                    load_wq(u0 + HPG - 1, g * HPG + HPG - 1)
                    load_wkv(G + 1, (g + 1) % KVH)
                    load_wo(u0 + HPG - 2, g * HPG + HPG - 2)
                    load_wq(u0 + HPG, (g + 1) % KVH * HPG)
                    load_wo(u0 + HPG - 1, g * HPG + HPG - 1)
                load_context(b + 1, (b + 1) % B)

        @block.gpsimd
        def _(pool):
            pool.memset(hid_hi[:, :, KEYS:WIDTH].bitcast(F32), 0.0).then_inc(pad_zeroed, 1)
            pool.memset(hid_lo[:, :, KEYS:WIDTH].bitcast(F32), 0.0).then_inc(pad_zeroed, 1)

            def split(hi, lo, raw, hi_done, ready, n):
                pool.tensor_tensor(hi, raw, ones[:, 0:1].to_broadcast(raw.shape), ALU.mult).then_inc(hi_done, 1)
                pool.wait_ge(hi_done, n + 1)
                pool.tensor_tensor(lo, raw, hi.bitcast(F32), ALU.subtract).then_inc(ready, 1)

            def flat(w):
                return w[:].rearrange("p c n -> p (c n)" if len(w.shape) == 3 else "p a c n -> p (a c n)")

            def split_wq(u, a, free):
                pool.wait_ge(wq_loaded, 16 * (u + 1))
                pool.wait_ge(q_ps, free)
                split(flat(wq_hi[a]), flat(wq_lo[a]), flat(wq_raw), wq_hi_done, wq_ready, u)

            def split_wo(u, a, free):
                pool.wait_ge(wo_loaded, 16 * (u + 1))
                pool.wait_ge(wo_ps, QT * free)
                split(wo_hi[a][:, :], wo_lo[a][:, :], wo_raw[:, :], wo_hi_done, wo_ready, u)

            def split_wkv(G):
                pool.wait_ge(wkv_loaded, 32 * (G + 1))
                pool.wait_ge(kv_ps, 8 * G)
                split(flat(wkv_hi), flat(wkv_lo), flat(wkv_raw), wkv_hi_done, wkv_ready, G)

            def copy_latents(i, b):
                for r in range(LAT):
                    pool.wait_ge(hid_ps, KT * i)
                    pool.tensor_tensor(stage[r][:, :], xn[:, bass.ds(QT * b + r, 1), :].rearrange("p a d -> p (a d)"),
                                       ones[:, 0:1].to_broadcast([P, D]), ALU.mult).then_inc(stage_copied, 1)

            copy_latents(0, 0)
            split_wkv(0)
            split_wq(0, 0, 0)
            with pool.Fori(0, B) as b:
                copy_latents(b + 1, (b + 1) % B)
                with pool.Fori(0, KVH) as g:
                    G = b * KVH + g
                    u0 = G * HPG
                    split_wq(u0 + 1, 1, u0)
                    split_wo(u0, 0, u0)
                    split_wq(u0 + 2, 0, u0 + 1)
                    split_wo(u0 + 1, 1, u0)
                    with pool.Fori(0, HPG // 2 - 2) as i:
                        for a in range(2):
                            u = u0 + 2 * i + 2 + a
                            split_wq(u + 1, 1 - a, u)
                            split_wo(u, a, u - 1)
                    split_wq(u0 + 7, 1, u0 + 6)
                    split_wkv(G + 1)
                    split_wo(u0 + 6, 0, u0 + 5)
                    split_wq(u0 + 8, 0, u0 + 7)
                    split_wo(u0 + 7, 1, u0 + 6)

        @block.tensor
        def _(pe):
            def three(out, w_hi, w_lo, m_hi, m_lo, first, last):
                pe.matmul(out, w_hi, m_hi, start=first, stop=False)
                pe.matmul(out, w_hi, m_lo, start=False, stop=False)
                return pe.matmul(out, w_lo, m_hi, start=False, stop=last)

            def project(out, w_hi, w_lo, c0, n, lo=0, hi=DC):
                for c in range(lo, hi):
                    mm = three(out, w_hi[:, c, :], w_lo[:, c, :], hid_hi[:, c, c0:c0 + n], hid_lo[:, c, c0:c0 + n],
                               c == 0, c == DC - 1)
                return mm

            def queries(u, a, part=None):
                if part != 1:
                    pe.wait_ge(wq_ready, u + 1)
                lo, hi = (0, DC) if part is None else (part * DC // 2, (part + 1) * DC // 2)
                mm = project(ps_m[:, 0:TOK], wq_hi[a], wq_lo[a], 0, TOK, lo, hi)
                if hi == DC:
                    mm.then_inc(q_ps, 1)

            def scores(u, a, j, first, halves=(0, 1)):
                if j == 0:
                    pe.wait_ge(q_done, u + 1)
                for half in halves:
                    if not first:
                        pe.wait_ge(probs_done, 4 * u + 2 * j + half - 1)
                    for c in (2 * half, 2 * half + 1):
                        c0, n = CHUNKS[c]
                        mm = three(ps_s[:, c, 0:n], q_hi[a][:, P * j:P * j + P], q_lo[a][:, P * j:P * j + P],
                                   k_hi[:, c0:c0 + n], k_lo[:, c0:c0 + n], True, True)
                    mm.then_inc(s_ps, 1)

            def transpose_probs(v, a, p, first):
                if p == 0:
                    pe.wait_ge(probs_done, 4 * v + 3)
                elif p == FIRST_PAIRS:
                    pe.wait_ge(probs_done, 4 * (v + 1))
                if not (first and p < 2):
                    pe.wait_ge(pt_done, PAIRS * v + p - 1)
                for k in range(2 * p, min(2 * p + 2, KT)):
                    n = rows_of(k)
                    for j in range(QT):
                        at = (k % 2) * TOK + j * P
                        tr = pe.transpose(ps_t[0:n, p % 2, at:at + P], probs[a][j][:, k * P:k * P + n], ident[:, :])
                tr.then_inc(pt_ps, 1)

            def weigh_values(v, p):
                pe.wait_ge(pt_done, PAIRS * v + p + 1)
                if p == 0:
                    pe.wait_ge(o_f_done, v)
                for k in range(2 * p, min(2 * p + 2, KT)):
                    n = rows_of(k)
                    mm = three(ps_o[:, 0:TOK], v_hi[0:n, k, :], v_lo[0:n, k, :], pt_hi[0:n, p % 2, k % 2, :],
                               pt_lo[0:n, p % 2, k % 2, :], k == 0, k == KT - 1)
                mm.then_inc(pv_ps, 1)

            def spread_inverse(v):
                pe.wait_ge(diag_done, QT * (v + 1))
                pe.matmul(ps_m[:, 0:TOK], ones[:, :], diag[:, :], start=True, stop=True).then_inc(inv_ps, 1)

            def output(w, a, j):
                if j == 0:
                    pe.wait_ge(o_done, w + 1)
                    pe.wait_ge(wo_ready, w + 1)
                else:
                    pe.wait_ge(wo_added, QT * w + 1)
                three(ps_m[:, :], o_hi[:, P * j:P * j + P], o_lo[:, P * j:P * j + P], wo_hi[a][:, :], wo_lo[a][:, :],
                      True, True).then_inc(wo_ps, 1)

            def step(u, a, out, ahead, first_pv=False):
                v = u - 1
                transpose_probs(v, 1 - a, 0, first_pv)
                transpose_probs(v, 1 - a, 1, first_pv)
                scores(u, a, 0, False)
                spread_inverse(v)
                weigh_values(v, 0)
                transpose_probs(v, 1 - a, 2, False)
                pe.wait_ge(inv_copied, v + 1)
                if out:
                    output(u - 2, a, 0)
                weigh_values(v, 1)
                transpose_probs(v, 1 - a, 3, False)
                scores(u, a, 1, False, (0,))
                weigh_values(v, 2)
                transpose_probs(v, 1 - a, 4, False)
                scores(u, a, 1, False, (1,))
                weigh_values(v, 3)
                transpose_probs(v, 1 - a, 5, False)
                if out:
                    output(u - 2, a, 1)
                weigh_values(v, 4)
                transpose_probs(v, 1 - a, 6, False)
                if ahead:
                    if out:
                        pe.wait_ge(wo_added, QT * (u - 1))
                    queries(u + 1, 1 - a, 0)
                weigh_values(v, 5)
                transpose_probs(v, 1 - a, 7, False)
                if ahead:
                    queries(u + 1, 1 - a, 1)
                weigh_values(v, 6)
                weigh_values(v, 7)

            def transpose_inputs(i, r):
                st, n = r % STAGES, rows_of(r)
                if r < LAT:
                    pe.wait_ge(stage_copied, LAT * i + r + 1)
                else:
                    loads = [q for q in range(LAT, KT) if q % STAGES == st]
                    pe.wait_ge(stage_loaded[st], 16 * (len(loads) * i + loads.index(r) + 1))
                if r >= 4:
                    pe.wait_ge(hid_done, KT * i + r - 3)
                for c in range(DC):
                    tr = pe.transpose(ps_s[:, r % 4, c * P:c * P + n], stage[st][0:n, c * P:(c + 1) * P], ident[0:n, 0:n])
                tr.then_inc(hid_ps, 1)

            def keys(G, c):
                c0, n = CHUNKS[c]
                if c == 0:
                    pe.wait_ge(wkv_ready, G + 1)
                project(ps_s[:, c, 0:n], wkv_hi[:, 0], wkv_lo[:, 0], c0, n).then_inc(kv_ps, 1)

            def values(G, c):
                c0, n = CHUNKS[c]
                pe.wait_ge(k_done, 4 * G + c + 1)
                project(ps_s[:, c, 0:n], wkv_hi[:, 1], wkv_lo[:, 1], c0, n).then_inc(kv_ps, 1)

            def transpose_values(G, q):
                pe.wait_ge(vt_done, 4 * G + q + 1)
                if q >= 2:
                    pe.wait_ge(v_done, len(VPIECES) * G + q - 1)
                else:
                    pe.wait_ge(pt_done, PAIRS * HPG * G)
                for k in range(4 * q, min(4 * q + 4, KT)):
                    n = rows_of(k)
                    tr = pe.transpose(ps_t[0:n, q % 2, (k % 4) * P:(k % 4 + 1) * P], v_t[:, k * P:k * P + n], ident[:, :])
                tr.then_inc(v_ps, 1)

            def first_step(G):
                u0 = G * HPG
                transpose_values(G, 0)
                transpose_values(G, 1)
                pe.wait_ge(vt_done, 4 * (G + 1))
                scores(u0, 0, 0, True)
                transpose_values(G, 2)
                transpose_values(G, 3)
                queries(u0 + 1, 1)
                scores(u0, 0, 1, False)
                pe.wait_ge(v_done, len(VPIECES) * (G + 1))

            def group(G):
                u0 = G * HPG
                first_step(G)
                step(u0 + 1, 1, False, True, first_pv=True)
                with pe.Fori(0, HPG // 2 - 2) as i:
                    step(u0 + 2 * i + 2, 0, True, True)
                    step(u0 + 2 * i + 3, 1, True, True)
                step(u0 + 6, 0, True, True)
                step(u0 + 7, 1, True, False)

            def last_step(G, i, to_next_group):
                u = G * HPG + HPG
                v = u - 1

                def meanwhile(n):
                    if n == 1:
                        pe.wait_ge(probs_done, 4 * (v + 1))
                    if to_next_group:
                        if n % 2 == 0:
                            keys(G + 1, n // 2)
                    else:
                        for r in range(2 * n, min(2 * n + 2, KT)):
                            transpose_inputs(i, r)

                transpose_probs(v, 1, 0, False)
                transpose_probs(v, 1, 1, False)
                meanwhile(0)
                spread_inverse(v)
                weigh_values(v, 0)
                transpose_probs(v, 1, 2, False)
                pe.wait_ge(inv_copied, v + 1)
                output(u - 2, 0, 0)
                meanwhile(1)
                weigh_values(v, 1)
                transpose_probs(v, 1, 3, False)
                meanwhile(2)
                output(u - 2, 0, 1)
                weigh_values(v, 2)
                transpose_probs(v, 1, 4, False)
                meanwhile(3)
                weigh_values(v, 3)
                transpose_probs(v, 1, 5, False)
                meanwhile(4)
                weigh_values(v, 4)
                transpose_probs(v, 1, 6, False)
                meanwhile(5)
                weigh_values(v, 5)
                transpose_probs(v, 1, 7, False)
                meanwhile(6)
                weigh_values(v, 6)
                weigh_values(v, 7)
                meanwhile(7)

            for r in range(KT):
                transpose_inputs(0, r)
            pe.wait_ge(pad_zeroed, 2)
            with pe.Fori(0, B) as b:
                G0 = b * KVH
                for c in range(4):
                    if c == 0:
                        pe.wait_ge(hid_done, KT * (b + 1))
                    keys(G0, c)
                for c in range(4):
                    values(G0, c)
                pe.wait_ge(wo_added, QT * HPG * G0)
                queries(G0 * HPG, 0)
                with pe.Fori(0, KVH - 1) as g:
                    G = b * KVH + g
                    group(G)
                    last_step(G, None, True)
                    u0 = G * HPG + HPG
                    values(G + 1, 0)
                    output(u0 - 1, 1, 0)
                    values(G + 1, 1)
                    output(u0 - 1, 1, 1)
                    values(G + 1, 2)
                    pe.wait_ge(wo_added, QT * u0)
                    queries(u0, 0)
                    values(G + 1, 3)
                G = b * KVH + (KVH - 1)
                group(G)
                last_step(G, b + 1, False)
                output(G * HPG + HPG - 1, 1, 0)
                output(G * HPG + HPG - 1, 1, 1)

        @block.scalar
        def _(act):
            def probs_hi(v, p):
                act.wait_ge(pt_ps, PAIRS * v + p + 1)
                full = 2 if 2 * p + 2 < KT else 1
                n = P if full == 2 else LAST
                if p >= 2:
                    act.wait_ge(pv_ps, PAIRS * v + p - 1)
                else:
                    act.wait_ge(pv_ps, PAIRS * v)
                act.activation(pt_hi[0:n, p % 2, 0:full, :],
                               ps_t[0:n, p % 2, 0:full * TOK].rearrange("p (k q) -> p k q", k=full),
                               ACT.Copy).then_inc(pt_hi_done, 1)

            def exponentials(u, a, j, half):
                act.wait_ge(neg_max_done, QT * u + j + 1)
                lo, hi = HALVES[half]
                act.activation(probs[a][j][:, lo:hi], s_flat[:, lo:hi], ACT.Exp, bias=neg_max[:, j:j + 1], scale=SCALE,
                               accum_out=half_sum[:, a, j, half:half + 1]).then_inc(probs_done, 1)

            def queries_hi(u, a):
                act.wait_ge(q_ps, u + 1)
                act.activation(q_hi[a][:, :], ps_m[:, 0:TOK], ACT.Copy).then_inc(q_hi_done, 1)

            def inverse_out(v):
                act.wait_ge(inv_ps, v + 1)
                act.wait_ge(o_f_done, v)
                act.activation(inv_wide[:, :], ps_m[:, 0:TOK], ACT.Copy).then_inc(inv_copied, 1)

            def output_hi(w):
                act.wait_ge(o_f_done, w + 1)
                act.activation(o_hi[:, :], o_f[:, :], ACT.Copy).then_inc(o_hi_done, 1)

            def step(u, a, out, ahead):
                v = u - 1
                probs_hi(v, 0)
                probs_hi(v, 1)
                if out:
                    output_hi(u - 2)
                inverse_out(v)
                exponentials(u, a, 0, 0)
                probs_hi(v, 2)
                exponentials(u, a, 0, 1)
                probs_hi(v, 3)
                probs_hi(v, 4)
                probs_hi(v, 5)
                exponentials(u, a, 1, 0)
                probs_hi(v, 6)
                exponentials(u, a, 1, 1)
                probs_hi(v, 7)
                if ahead:
                    queries_hi(u + 1, 1 - a)

            def inputs_hi(i, r):
                n = rows_of(r)
                act.wait_ge(hid_ps, KT * i + r + 1)
                act.activation(hid_hi[:, :, r * P:r * P + n],
                               ps_s[:, r % 4, :].rearrange("p (c n) -> p c n", c=DC)[:, :, 0:n],
                               ACT.Copy).then_inc(hid_hi_done, 1)

            def keys_hi(G, c):
                c0, n = CHUNKS[c]
                act.wait_ge(kv_ps, 8 * G + c + 1)
                act.activation(k_hi[:, c0:c0 + n], ps_s[:, c, 0:n], ACT.Copy).then_inc(k_hi_done, 1)

            def values_out(G, c):
                c0, n = CHUNKS[c]
                act.wait_ge(kv_ps, 8 * G + 4 + c + 1)
                act.activation(v_t[:, c0:c0 + n], ps_s[:, c, 0:n], ACT.Copy).then_inc(vt_done, 1)

            def values_hi(G, i):
                k, m, n = VPIECES[i]
                act.wait_ge(v_ps, VG * G + min(i, VG - 1) + 1)
                act.activation(v_hi[0:n, k:k + m, :],
                               ps_t[0:n, k // 4 % 2, (k % 4) * P:(k % 4 + m) * P].rearrange("p (k d) -> p k d", k=m),
                               ACT.Copy).then_inc(v_hi_done, 1)

            def group(G):
                u0 = G * HPG
                values_hi(G, 0)
                values_hi(G, 1)
                exponentials(u0, 0, 0, 0)
                exponentials(u0, 0, 0, 1)
                for i in range(2, len(VPIECES)):
                    values_hi(G, i)
                queries_hi(u0 + 1, 1)
                exponentials(u0, 0, 1, 0)
                exponentials(u0, 0, 1, 1)
                step(u0 + 1, 1, False, True)
                with act.Fori(0, HPG // 2 - 2) as i:
                    step(u0 + 2 * i + 2, 0, True, True)
                    step(u0 + 2 * i + 3, 1, True, True)
                step(u0 + 6, 0, True, True)
                step(u0 + 7, 1, True, False)

            def last_step(G, i, to_next_group):
                u = G * HPG + HPG
                v = u - 1

                def meanwhile(n):
                    if to_next_group:
                        if n % 2 == 0:
                            keys_hi(G + 1, n // 2)
                    else:
                        for r in range(2 * n, min(2 * n + 2, KT)):
                            inputs_hi(i, r)

                probs_hi(v, 0)
                probs_hi(v, 1)
                output_hi(u - 2)
                meanwhile(0)
                inverse_out(v)
                for p in range(2, PAIRS):
                    probs_hi(v, p)
                    meanwhile(p - 1)
                meanwhile(PAIRS - 1)
                output_hi(v)

            for r in range(KT):
                inputs_hi(0, r)
            with act.Fori(0, B) as b:
                G0 = b * KVH
                for c in range(4):
                    keys_hi(G0, c)
                for c in range(4):
                    values_out(G0, c)
                queries_hi(G0 * HPG, 0)
                with act.Fori(0, KVH - 1) as g:
                    G = b * KVH + g
                    group(G)
                    last_step(G, None, True)
                    values_out(G + 1, 0)
                    values_out(G + 1, 1)
                    values_out(G + 1, 2)
                    queries_hi(G * HPG + HPG, 0)
                    values_out(G + 1, 3)
                G = b * KVH + (KVH - 1)
                group(G)
                last_step(G, b + 1, False)

        @block.vector
        def _(dve):
            def probs_lo(v, p):
                full = 2 if 2 * p + 2 < KT else 1
                n = P if full == 2 else LAST
                dve.wait_ge(pt_hi_done, PAIRS * v + p + 1)
                dve.tensor_tensor(pt_lo[0:n, p % 2, 0:full, :],
                                  ps_t[0:n, p % 2, 0:full * TOK].rearrange("p (k q) -> p k q", k=full),
                                  pt_hi[0:n, p % 2, 0:full, :].bitcast(F32), ALU.subtract).then_inc(pt_done, 1)

            def maximum(u, j, half):
                lo, hi = HALVES[half]
                dve.wait_ge(s_ps, 4 * u + 2 * j + half + 1)
                dve.reduce_max(half_max[:, half:half + 1], s_flat[:, lo:hi], AX.X).then_inc(max_done, 1)

            def negate_maximum(u, j):
                dve.wait_ge(max_done, 4 * u + 2 * j + 2)
                dve.tensor_scalar(neg_max[:, j:j + 1], half_max[:, 0:1], half_max[:, 1:2], -SCALE, ALU.max,
                                  ALU.mult).then_inc(neg_max_done, 1)

            def maxima(u, j):
                maximum(u, j, 0)
                maximum(u, j, 1)
                negate_maximum(u, j)

            def queries_lo(u, a):
                dve.wait_ge(q_hi_done, u + 1)
                dve.tensor_tensor(q_lo[a][:, :], ps_m[:, 0:TOK], q_hi[a][:, :].bitcast(F32), ALU.subtract).then_inc(q_done, 1)

            def inverse_sums(v, a):
                dve.wait_ge(probs_done, 4 * (v + 1))
                dve.tensor_tensor(row_sum[:, :], half_sum[:, a, :, 0], half_sum[:, a, :, 1], ALU.add).then_inc(sum_done, 1)
                dve.wait_ge(sum_done, v + 1)
                dve.reciprocal(row_inv[:, :], row_sum[:, :]).then_inc(inv_done, 1)
                dve.wait_ge(inv_done, v + 1)
                for j in range(QT):
                    dve.tensor_scalar(diag[:, P * j:P * j + P], ident[:, :], row_inv[:, j:j + 1], None,
                                      ALU.mult).then_inc(diag_done, 1)

            def normalise(w):
                dve.wait_ge(pv_ps, PAIRS * (w + 1))
                dve.wait_ge(inv_copied, w + 1)
                dve.tensor_tensor(o_f[:, :], ps_o[:, 0:TOK], inv_wide[:, :], ALU.mult).then_inc(o_f_done, 1)

            def output_lo(w):
                dve.wait_ge(o_hi_done, w + 1)
                dve.tensor_tensor(o_lo[:, :], o_f[:, :], o_hi[:, :].bitcast(F32), ALU.subtract).then_inc(o_done, 1)

            def add_output(w, j, tile):
                x_tile = x_res[:, bass.ds(tile, 1), :].rearrange("p a d -> p (a d)")
                dve.wait_ge(wo_ps, QT * w + j + 1)
                dve.wait_ge(wo_added, QT * w + j)
                dve.tensor_tensor(x_tile, ps_m[:, :], x_tile, ALU.add).then_inc(wo_added, 1)

            def step(u, a, tile, out, ahead):
                v = u - 1
                if out:
                    normalise(u - 2)
                inverse_sums(v, 1 - a)
                probs_lo(v, 0)
                maximum(u, 0, 0)
                if out:
                    output_lo(u - 2)
                probs_lo(v, 1)
                maximum(u, 0, 1)
                negate_maximum(u, 0)
                probs_lo(v, 2)
                if out:
                    add_output(u - 2, 0, tile)
                probs_lo(v, 3)
                maximum(u, 1, 0)
                probs_lo(v, 4)
                maximum(u, 1, 1)
                negate_maximum(u, 1)
                if out:
                    add_output(u - 2, 1, tile + 1)
                probs_lo(v, 5)
                probs_lo(v, 6)
                probs_lo(v, 7)
                if ahead:
                    queries_lo(u + 1, 1 - a)

            def inputs_lo(i, r):
                n = rows_of(r)
                dve.wait_ge(hid_hi_done, KT * i + r + 1)
                dve.tensor_tensor(hid_lo[:, :, r * P:r * P + n],
                                  ps_s[:, r % 4, :].rearrange("p (c n) -> p c n", c=DC)[:, :, 0:n],
                                  hid_hi[:, :, r * P:r * P + n].bitcast(F32), ALU.subtract).then_inc(hid_done, 1)

            def keys_lo(G, c):
                c0, n = CHUNKS[c]
                dve.wait_ge(k_hi_done, 4 * G + c + 1)
                dve.tensor_tensor(k_lo[:, c0:c0 + n], ps_s[:, c, 0:n], k_hi[:, c0:c0 + n].bitcast(F32),
                                  ALU.subtract).then_inc(k_done, 1)

            def values_lo(G, i):
                k, m, n = VPIECES[i]
                dve.wait_ge(v_hi_done, len(VPIECES) * G + (i + 1 if i < VG - 1 else VG + 1))
                dve.tensor_tensor(v_lo[0:n, k:k + m, :],
                                  ps_t[0:n, k // 4 % 2, (k % 4) * P:(k % 4 + m) * P].rearrange("p (k d) -> p k d", k=m),
                                  v_hi[0:n, k:k + m, :].bitcast(F32), ALU.subtract).then_inc(v_done, 1)

            def group(G, tile):
                u0 = G * HPG
                values_lo(G, 0)
                values_lo(G, 1)
                maxima(u0, 0)
                for i in range(2, len(VPIECES)):
                    values_lo(G, i)
                queries_lo(u0 + 1, 1)
                maxima(u0, 1)
                step(u0 + 1, 1, tile, False, True)
                with dve.Fori(0, HPG // 2 - 2) as i:
                    step(u0 + 2 * i + 2, 0, tile, True, True)
                    step(u0 + 2 * i + 3, 1, tile, True, True)
                step(u0 + 6, 0, tile, True, True)
                step(u0 + 7, 1, tile, True, False)

            def last_step(G, tile, i, to_next_group):
                u = G * HPG + HPG
                v = u - 1

                def meanwhile(n):
                    if to_next_group:
                        if n % 2 == 0:
                            keys_lo(G + 1, n // 2)
                    else:
                        for r in range(2 * n, min(2 * n + 2, KT)):
                            inputs_lo(i, r)

                normalise(u - 2)
                inverse_sums(v, 1)
                probs_lo(v, 0)
                probs_lo(v, 1)
                output_lo(u - 2)
                meanwhile(0)
                add_output(u - 2, 0, tile)
                probs_lo(v, 2)
                meanwhile(1)
                probs_lo(v, 3)
                meanwhile(2)
                add_output(u - 2, 1, tile + 1)
                for p in range(4, PAIRS):
                    probs_lo(v, p)
                    meanwhile(p - 1)
                normalise(v)
                meanwhile(PAIRS - 1)
                output_lo(v)
                add_output(v, 0, tile)
                add_output(v, 1, tile + 1)

            for r in range(KT):
                inputs_lo(0, r)
            with dve.Fori(0, B) as b:
                G0 = b * KVH
                for c in range(4):
                    keys_lo(G0, c)
                queries_lo(G0 * HPG, 0)
                with dve.Fori(0, KVH - 1) as g:
                    G = b * KVH + g
                    group(G, QT * b)
                    last_step(G, QT * b, None, True)
                    queries_lo(G * HPG + HPG, 0)
                G = b * KVH + (KVH - 1)
                group(G, QT * b)
                last_step(G, QT * b, b + 1, False)


class Chain:

    def __init__(self, engine, semaphore):
        self.engine, self.semaphore, self.count = engine, semaphore, 0

    def link(self, instruction):
        self.count += 1
        instruction.then_inc(self.semaphore, 1)
        self.engine.wait_ge(self.semaphore, self.count)


def wide(x, n):
    return x.unsqueeze(2).to_broadcast([x.shape[0], x.shape[1], n])


def softmax_rows(dve, chain, scores, logits, row, row2, exp_wait, max_done):
    E = logits.shape[2]
    chain.link(dve.reduce_max(row, logits, AX.X))
    dve.tensor_tensor(scores, logits, wide(row, E), ALU.subtract).then_inc(max_done, 1)
    dve.wait_ge(exp_wait, 1)
    chain.link(dve.reduce_sum(row, scores, AX.X))
    chain.link(dve.reciprocal(row2, row))
    chain.link(dve.tensor_tensor(scores, scores, wide(row2, E), ALU.mult))


def top_two(dve, chain, scores, ramp, hit, first, second, rest, row, best, runner):
    E, tiles = scores.shape[2], scores.shape[1]
    ramps = ramp.unsqueeze(1).to_broadcast([P, tiles, E])
    for values, value, one_hot in ((scores, best, first), (rest, runner, second)):
        chain.link(dve.reduce_max(value, values, AX.X))
        chain.link(dve.tensor_tensor(hit, values, wide(value, E), ALU.is_equal))
        chain.link(dve.tensor_tensor(hit, hit, ramps, ALU.mult))
        chain.link(dve.reduce_max(row, hit, AX.X))
        chain.link(dve.tensor_tensor(one_hot, hit, wide(row, E), ALU.is_equal))
        if values is scores:
            chain.link(dve.scalar_tensor_tensor(rest, first, -4.0, scores, ALU.mult, ALU.add))


def gated_experts_block(nc, held, gate_w, gate_b, w1, b1, w2, b2, x_res, xn, ident, ones, batches):
    TILES, D = x_res.shape[1], x_res.shape[2]
    E, _, F = w1.shape
    DC, FC = D // P, F // P
    TPB = TILES // batches
    VISION = int(TPB * P * 0.3)
    EW = E + E % 2
    BANK = 512
    TC = TILES * P // BANK
    TPC = BANK // P
    STEPS = TC * FC
    PIECES = DC + FC
    FUNCTIONS = (ACT.Tanh, ACT.Gelu, ACT.Silu)
    assert E == len(FUNCTIONS) and TPB == 2 and VISION <= P and PIECES == STEPS and D == BANK and F == BANK

    with ExitStack() as ctx:
        sb = lambda n, s, d=F32: ctx.enter_context(nc.sbuf_tensor(f"b_{n}", s, d))
        sem = lambda n: new_semaphore(nc, held, f"b_{n}")
        xt_hi, xt_lo = sb("xt_hi", [P, DC, TILES * P], F32R), sb("xt_lo", [P, DC, TILES * P], F32R)
        w1_raw, w2_raw = sb("w1_raw", [P, DC, F]), sb("w2_raw", [P, FC, D])
        w1_hi = [sb(f"w1_hi{a}", [P, DC, F], F32R) for a in range(2)]
        w1_lo = [sb(f"w1_lo{a}", [P, DC, F], F32R) for a in range(2)]
        w2_hi = [sb(f"w2_hi{a}", [P, FC, D], F32R) for a in range(2)]
        w2_lo = [sb(f"w2_lo{a}", [P, FC, D], F32R) for a in range(2)]
        hidden = [sb(f"hidden{i}", [P, BANK]) for i in range(2)]
        act_hi, act_lo = sb("act_hi", [P, FC, TILES * P], F32R), sb("act_lo", [P, FC, TILES * P], F32R)
        b1_rows, b1_cols = sb("b1_rows", [E * FC, P]), sb("b1_cols", [P, E, FC])
        b2_raw, b2_hi, b2_lo = sb("b2_raw", [1, E, D]), sb("b2_hi", [1, E, D], F32R), sb("b2_lo", [1, E, D], F32R)
        one_r = sb("one_r", [1, P], F32R)
        gate_raw, gate_hi, gate_lo = sb("gate_raw", [P, DC, EW]), sb("gate_hi", [P, DC, EW], F32R), sb("gate_lo", [P, DC, EW], F32R)
        gate_rows = sb("gate_rows", [P, 2, E])
        vision, text = sb("vision", [P, P]), sb("text", [P, P])
        ramp = sb("ramp", [P, E])
        magnitudes, magnitude = sb("magnitudes", [P, D]), sb("magnitude", [P, TILES])
        strength, ratio = sb("strength", [P, batches]), sb("ratio", [P, batches])
        logits, scores = sb("logits", [P, TILES, E]), sb("scores", [P, TILES, E])
        hit, first, second, rest = (sb(n, [P, TILES, E]) for n in ("hit", "first", "second", "rest"))
        row, row2, best, runner = (sb(n, [P, TILES]) for n in ("row", "row2", "best", "runner"))
        chosen = sb("chosen", [1, batches, 2, E])
        part, share = sb("part", [P, TILES, E]), sb("share", [P, TILES, E])

        ps_t = ctx.enter_context(nc.psum_tensor("b_ps_t", [P, 2, BANK], F32))
        ps_h = ctx.enter_context(nc.psum_tensor("b_ps_h", [P, 2, BANK], F32))
        ps_y = ctx.enter_context(nc.psum_tensor("b_ps_y", [P, 2, BANK], F32))
        ps_r = ctx.enter_context(nc.psum_tensor("b_ps_r", [P, BANK], F32))
        ps_c = ctx.enter_context(nc.psum_tensor("b_ps_c", [P, BANK], F32))
        strengths = ps_c[:, 0:2 * batches].rearrange("p (k b) -> p k b", k=2)
        choices = ps_c[:, 0:batches * 2 * E].rearrange("p (b i e) -> p b i e", b=batches, i=2)

        small_loaded, gate_loaded = sem("small_loaded"), sem("gate_loaded")
        w1_loaded, w2_loaded = sem("w1_loaded"), sem("w2_loaded")
        masks_set, masks_done, pads_set = sem("masks_set"), sem("masks_done"), sem("pads_set")
        magnitude_done, strength_ps, gate_hi_done, gate_done = sem("magnitude_done"), sem("strength_ps"), sem("gate_hi_done"), sem("gate_done")
        b1_ps, b1_done = sem("b1_ps"), sem("b1_done")
        b2_hi_done, b2_done = sem("b2_hi_done"), sem("b2_done")
        xt_ps, xt_hi_done, xt_done, logits_ps = sem("xt_ps"), sem("xt_hi_done"), sem("xt_done"), sem("logits_ps")
        centred, exp_done, chosen_done, choices_ps = sem("centred"), sem("exp_done"), sem("chosen_done"), sem("choices_ps")
        w_hi_done, w_done = sem("w_hi_done"), sem("w_done")
        h_ps, hidden_done, act_hi_done, act_done = sem("h_ps"), sem("hidden_done"), sem("act_hi_done"), sem("act_done")
        y_ps, added, router = sem("y_ps"), sem("added"), sem("router")
        block = ctx.enter_context(nc.Block())

        @block.sync
        def _(sp):
            for e in range(E):
                if e:
                    sp.wait_ge(w_done, PIECES * e)
                sp.dma_start(w1_raw[:, :, :], w1[e].rearrange("(c p) f -> p c f", p=P)).then_inc(w1_loaded, 16)
                sp.dma_start(w2_raw[:, :, :], w2[e].rearrange("(c p) d -> p c d", p=P)).then_inc(w2_loaded, 16)
                if e == 0:
                    sp.dma_start(gate_raw[:, :, 0:E], gate_w[0:D, :].rearrange("(c p) e -> p c e", p=P)).then_inc(gate_loaded, 16)
                    sp.dma_start(gate_rows[:, 0, :], gate_w[D, :].partition_broadcast(P)).then_inc(small_loaded, 16)
                    sp.dma_start(gate_rows[:, 1, :], gate_b.partition_broadcast(P)).then_inc(small_loaded, 16)
                    sp.dma_start(b1_rows[:, :], b1.rearrange("e (c p) -> (e c) p", p=P)).then_inc(small_loaded, 16)
                    sp.dma_start(b2_raw[:, :, :], b2.rearrange("(a e) d -> a e d", a=1)).then_inc(small_loaded, 16)

        @block.gpsimd
        def _(pool):
            pool.memset(gate_raw[:, :, E:EW], 0.0).then_inc(pads_set, 1)
            pool.memset(one_r[:, :].bitcast(F32), 1.0).then_inc(pads_set, 1)
            pool.iota(ramp[:, :], pattern=[[-1, E]], base=E, channel_multiplier=0,
                      allow_small_or_imprecise_dtypes=True).then_inc(pads_set, 1)
            pool.memset(vision[:, :], 1.0).then_inc(masks_set, 1)
            pool.memset(text[:, :], 1.0).then_inc(masks_set, 1)
            pool.wait_ge(masks_set, 2)
            pool.affine_select(out=vision[:, :], in_=vision[:, :], compare_op=ALU.is_ge, fill=0.0,
                               base=VISION - 1, pattern=[[0, P]], channel_multiplier=-1).then_inc(masks_done, 1)
            pool.affine_select(out=text[:, :], in_=text[:, :], compare_op=ALU.is_ge, fill=0.0,
                               base=-VISION, pattern=[[0, P]], channel_multiplier=1).then_inc(masks_done, 1)

        @block.tensor
        def _(pe):
            def three(out, w_hi, w_lo, m_hi, m_lo, first, last):
                pe.matmul(out, w_hi, m_hi, start=first, stop=False)
                pe.matmul(out, w_hi, m_lo, start=False, stop=False)
                return pe.matmul(out, w_lo, m_hi, start=False, stop=last)

            for t in range(TILES):
                if t >= 2:
                    pe.wait_ge(xt_done, t - 1)
                for c in range(DC):
                    tr = pe.transpose(ps_t[:, t % 2, c * P:(c + 1) * P], xn[:, t, c * P:(c + 1) * P], ident[:, :])
                tr.then_inc(xt_ps, 1)
            pe.wait_ge(small_loaded, 64)
            pe.transpose(ps_h[:, 0, 0:E * FC], b1_rows[:, :], ident[0:E * FC, 0:E * FC]).then_inc(b1_ps, 1)
            pe.wait_ge(masks_done, 2)
            pe.wait_ge(magnitude_done, TILES)
            pe.matmul(strengths[:, 0, :], vision[:, :], magnitude[:, 0:TILES:TPB], start=True, stop=True)
            pe.matmul(strengths[:, 1, :], text[:, :], magnitude[:, 0:TILES:TPB], start=True, stop=False)
            pe.matmul(strengths[:, 1, :], ones[:, :], magnitude[:, 1:TILES:TPB], start=False, stop=True).then_inc(strength_ps, 1)
            pe.wait_ge(gate_done, 1)
            pe.wait_ge(xt_done, TILES)
            for t in range(TILES):
                for c in range(DC):
                    mm = three(ps_r[:, t * EW:(t + 1) * EW], xt_hi[:, c, t * P:(t + 1) * P], xt_lo[:, c, t * P:(t + 1) * P],
                               gate_hi[:, c, :], gate_lo[:, c, :], c == 0, c == DC - 1)
            mm.then_inc(logits_ps, 1)
            for e in range(E):
                a = e % 2
                pe.wait_ge(w_done, PIECES * e + DC)
                for s in range(STEPS):
                    tc, f, n = s // FC, s % FC, STEPS * e + s
                    if n == 0:
                        pe.wait_ge(b1_done, 1)
                    if n >= 2:
                        pe.wait_ge(hidden_done, n - 1)
                    for c in range(DC):
                        mm = three(ps_h[:, n % 2, :], w1_hi[a][:, c, f * P:(f + 1) * P], w1_lo[a][:, c, f * P:(f + 1) * P],
                                   xt_hi[:, c, tc * BANK:(tc + 1) * BANK], xt_lo[:, c, tc * BANK:(tc + 1) * BANK],
                                   c == 0, c == DC - 1)
                    mm.then_inc(h_ps, 1)
                if e == 0:
                    pe.wait_ge(chosen_done, 1)
                    pe.matmul(ps_c[:, 0:batches * 2 * E], ones[0:1, :], chosen[:, :, :, :].rearrange("p b i e -> p (b i e)"),
                              start=True, stop=True).then_inc(choices_ps, 1)
                    pe.wait_ge(pads_set, 3)
                    pe.wait_ge(b2_done, 1)
                pe.wait_ge(w_done, PIECES * (e + 1))
                for t in range(TILES):
                    n = TILES * e + t
                    if t % TPC == 0:
                        pe.wait_ge(act_done, STEPS * e + FC * (t // TPC + 1))
                    if n >= 2:
                        pe.wait_ge(added, n - 1)
                    pe.matmul(ps_y[:, n % 2, :], one_r[:, :], b2_hi[:, e, :], start=True, stop=False)
                    pe.matmul(ps_y[:, n % 2, :], one_r[:, :], b2_lo[:, e, :], start=False, stop=False)
                    for f in range(FC):
                        mm = three(ps_y[:, n % 2, :], act_hi[:, f, t * P:(t + 1) * P], act_lo[:, f, t * P:(t + 1) * P],
                                   w2_hi[a][:, f, :], w2_lo[a][:, f, :], False, f == FC - 1)
                    mm.then_inc(y_ps, 1)

        def weight_piece(e, i):
            a, c = e % 2, i % DC
            if i < DC:
                return w1_raw[:, c, :], w1_hi[a][:, c, :], w1_lo[a][:, c, :]
            return w2_raw[:, c, :], w2_hi[a][:, c, :], w2_lo[a][:, c, :]

        @block.scalar
        def _(act):
            def split_hi(e, i):
                raw, hi, _ = weight_piece(e, i)
                if i == 0:
                    act.wait_ge(w1_loaded, 16 * (e + 1))
                if i == DC:
                    act.wait_ge(w2_loaded, 16 * (e + 1))
                if e >= 2 and i == 0:
                    act.wait_ge(y_ps, TILES * (e - 1))
                act.activation(hi, raw, ACT.Copy).then_inc(w_hi_done, 1)

            for t in range(TILES):
                if t:
                    act.wait_ge(magnitude_done, t)
                act.activation(magnitudes[:, :], xn[:, t, :], ACT.Abs, accum_out=magnitude[:, t:t + 1]).then_inc(magnitude_done, 1)
                act.wait_ge(xt_ps, t + 1)
                act.activation(xt_hi[:, :, t * P:(t + 1) * P], ps_t[:, t % 2, :].rearrange("p (c n) -> p c n", c=DC),
                               ACT.Copy).then_inc(xt_hi_done, 1)
            act.wait_ge(gate_loaded, 16)
            act.wait_ge(pads_set, 3)
            act.activation(gate_hi[:, :, :], gate_raw[:, :, :], ACT.Copy).then_inc(gate_hi_done, 1)
            act.wait_ge(small_loaded, 64)
            act.activation(b2_hi[:, :, :], b2_raw[:, :, :], ACT.Copy).then_inc(b2_hi_done, 1)
            act.wait_ge(b1_ps, 1)
            act.activation(b1_cols[:, :, :], ps_h[:, 0, 0:E * FC].rearrange("p (e c) -> p e c", e=E), ACT.Copy).then_inc(b1_done, 1)
            for i in range(PIECES):
                split_hi(0, i)
            act.wait_ge(centred, 1)
            act.activation(scores[:, :, :], scores[:, :, :], ACT.Exp).then_inc(exp_done, 1)
            act.wait_ge(b1_done, 1)
            for e in range(E):
                for s in range(STEPS):
                    tc, f, n = s // FC, s % FC, STEPS * e + s
                    act.wait_ge(h_ps, n + 1)
                    if n >= 2:
                        act.wait_ge(act_done, n - 1)
                    act.activation(hidden[n % 2][:, :], ps_h[:, n % 2, :], FUNCTIONS[e], bias=b1_cols[:, e, f:f + 1]).then_inc(hidden_done, 1)
                    act.wait_ge(hidden_done, n + 1)
                    act.activation(act_hi[:, f, tc * BANK:(tc + 1) * BANK], hidden[n % 2][:, :], ACT.Copy).then_inc(act_hi_done, 1)
                    if e + 1 < E:
                        split_hi(e + 1, s)

        @block.vector
        def _(dve):
            chain = Chain(dve, router)

            def split_lo(e, i):
                raw, hi, lo = weight_piece(e, i)
                dve.wait_ge(w_hi_done, PIECES * e + i + 1)
                dve.tensor_tensor(lo, raw, hi.bitcast(F32), ALU.subtract).then_inc(w_done, 1)

            for t in range(TILES):
                dve.wait_ge(xt_hi_done, t + 1)
                dve.tensor_tensor(xt_lo[:, :, t * P:(t + 1) * P], ps_t[:, t % 2, :].rearrange("p (c n) -> p c n", c=DC),
                                  xt_hi[:, :, t * P:(t + 1) * P].bitcast(F32), ALU.subtract).then_inc(xt_done, 1)
            dve.wait_ge(gate_hi_done, 1)
            dve.tensor_tensor(gate_lo[:, :, :], gate_raw[:, :, :], gate_hi[:, :, :].bitcast(F32), ALU.subtract).then_inc(gate_done, 1)
            dve.wait_ge(b2_hi_done, 1)
            dve.tensor_tensor(b2_lo[:, :, :], b2_raw[:, :, :], b2_hi[:, :, :].bitcast(F32), ALU.subtract).then_inc(b2_done, 1)
            dve.wait_ge(strength_ps, 1)
            chain.link(dve.tensor_scalar(strength[:, :], strengths[:, 0, :], 1.0 / (VISION * D), 1e-8, ALU.mult, ALU.add))
            chain.link(dve.reciprocal(strength[:, :], strength[:, :]))
            chain.link(dve.scalar_tensor_tensor(ratio[:, :], strengths[:, 1, :], 1.0 / ((TPB * P - VISION) * D),
                                                strength[:, :], ALU.mult, ALU.mult))
            dve.wait_ge(logits_ps, 1)
            dve.wait_ge(small_loaded, 64)
            chain.link(dve.tensor_tensor(logits[:, :, :], ps_r[:, 0:TILES * EW].rearrange("p (t e) -> p t e", t=TILES)[:, :, 0:E],
                                         gate_rows[:, 1, :].unsqueeze(1).to_broadcast([P, TILES, E]), ALU.add))
            for b in range(batches):
                tiles = slice(TPB * b, TPB * (b + 1))
                chain.link(dve.scalar_tensor_tensor(logits[:, tiles, :], gate_rows[:, 0, :].unsqueeze(1).to_broadcast([P, TPB, E]),
                                                    ratio[:, b:b + 1], logits[:, tiles, :], ALU.mult, ALU.add))
            softmax_rows(dve, chain, scores[:, :, :], logits[:, :, :], row[:, :], row2[:, :], exp_done, centred)
            top_two(dve, chain, scores[:, :, :], ramp[:, :], hit[:, :, :], first[:, :, :], second[:, :, :], rest[:, :, :],
                    row[:, :], best[:, :], runner[:, :])
            chain.link(dve.tensor_tensor(row[:, :], best[:, :], runner[:, :], ALU.add))
            chain.link(dve.tensor_scalar(row[:, :], row[:, :], 1e-8, None, ALU.add))
            chain.link(dve.reciprocal(row[:, :], row[:, :]))
            chain.link(dve.tensor_tensor(best[:, :], best[:, :], row[:, :], ALU.mult))
            chain.link(dve.tensor_tensor(runner[:, :], runner[:, :], row[:, :], ALU.mult))
            dve.tensor_copy(chosen[:, :, 0, :], first[0:1, 0:TILES:TPB, :])
            dve.tensor_copy(chosen[:, :, 1, :], second[0:1, 0:TILES:TPB, :]).then_inc(chosen_done, 1)
            for i in range(PIECES):
                split_lo(0, i)

            def shares():
                dve.wait_ge(choices_ps, 1)
                for b in range(batches):
                    tiles = slice(TPB * b, TPB * (b + 1))
                    pick = lambda i: choices[:, b, i, :].unsqueeze(1).to_broadcast([P, TPB, E])
                    chain.link(dve.tensor_tensor(part[:, tiles, :], pick(0), wide(best[:, tiles], E), ALU.mult))
                    chain.link(dve.tensor_tensor(share[:, tiles, :], pick(1), wide(runner[:, tiles], E), ALU.mult))
                    chain.link(dve.tensor_tensor(share[:, tiles, :], share[:, tiles, :], part[:, tiles, :], ALU.add))

            for e in range(E):
                for s in range(STEPS):
                    tc, f, n = s // FC, s % FC, STEPS * e + s
                    dve.wait_ge(act_hi_done, n + 1)
                    dve.tensor_tensor(act_lo[:, f, tc * BANK:(tc + 1) * BANK], hidden[n % 2][:, :],
                                      act_hi[:, f, tc * BANK:(tc + 1) * BANK].bitcast(F32), ALU.subtract).then_inc(act_done, 1)
                    if e + 1 < E:
                        split_lo(e + 1, s)
                if e == 0:
                    shares()
                for t in range(TILES):
                    n = TILES * e + t
                    dve.wait_ge(y_ps, n + 1)
                    if e:
                        dve.wait_ge(added, TILES * (e - 1) + t + 1)
                    dve.scalar_tensor_tensor(x_res[:, t, :], ps_y[:, n % 2, :], share[:, t, e:e + 1], x_res[:, t, :],
                                             ALU.mult, ALU.add).then_inc(added, 1)


def normed_attention_block(nc, held, ctx_in, wq, bq, wk, bk, fn_w, qn_w, kn_w, x_res, xn, ident, ones):
    B, CTX, D = ctx_in.shape
    TILES = x_res.shape[1]
    QT = TILES // B
    TOK = QT * P
    DC = D // P
    KT = -(-CTX // P)
    LAST = CTX - (KT - 1) * P
    WIDTH = CTX + CTX % 2
    BANK = 512
    CHUNKS = [(c, min(BANK, WIDTH - c)) for c in range(0, WIDTH, BANK)]
    HALVES = [(0, 2 * BANK), (2 * BANK, CTX)]
    STEPS = KT // 2
    TILES_OF = [[2 * s, 2 * s + 1] + ([KT - 1] if s == STEPS - 1 else []) for s in range(STEPS)]
    COLS = [(2 * P * s, 2 * P if s < STEPS - 1 else WIDTH - 2 * P * s) for s in range(STEPS)]
    RING = 4
    GROUP = BANK // P
    GROUPS = -(-KT // GROUP)
    EPS = 1e-6
    SCALE = 1.0 / math.sqrt(D)
    rows_of = lambda k: LAST if k == KT - 1 else P
    step_of = lambda t: min(t // 2, STEPS - 1)
    widths = [max(n for s, (_, n) in enumerate(COLS) if s % 2 == a) for a in range(2)]
    assert len(CHUNKS) == 4 and D == BANK and QT == 2 and GROUPS == 4 and LAST < P and KT % 2 == 1 and STEPS % 2 == 0

    with ExitStack() as ctx:
        sb = lambda n, s, d=F32: ctx.enter_context(nc.sbuf_tensor(f"c_{n}", s, d))
        sem = lambda n: new_semaphore(nc, held, f"c_{n}")
        raw = sb("raw", [P, RING, D])
        w_hi, w_lo = sb("w_hi", [P, DC, D], F32R), sb("w_lo", [P, DC, D], F32R)
        f_hi, f_lo = sb("f_hi", [P, KT, D], F32R), sb("f_lo", [P, KT, D], F32R)
        k_hi, k_lo = sb("k_hi", [P, DC, WIDTH], F32R), sb("k_lo", [P, DC, WIDTH], F32R)
        t_hi = [sb(f"t_hi{a}", [P, DC, widths[a]], F32R) for a in range(2)]
        t_lo = [sb(f"t_lo{a}", [P, DC, widths[a]], F32R) for a in range(2)]
        q_hi, q_lo = sb("q_hi", [P, DC, TOK], F32R), sb("q_lo", [P, DC, TOK], F32R)
        shared = sb("shared", [P, 2 * WIDTH])
        probs = [shared[:, j * WIDTH:(j + 1) * WIDTH] for j in range(QT)]
        squared = [shared[:, a * DC * widths[0]:a * DC * widths[0] + DC * widths[a]].rearrange("p (c n) -> p c n", c=DC) for a in range(2)]
        scratch = shared[:, DC * sum(widths):DC * sum(widths) + D]
        key_inv = sb("key_inv", [P, WIDTH])
        wk_raw = [key_inv[:, t * D:(t + 1) * D] for t in range(DC - 1)] + [scratch]
        fn_row = sb("fn_row", [P, D])
        columns = sb("columns", [P, 5, DC])
        vectors = sb("vectors", [5 * DC, P])
        qk_w, eps_col = sb("qk_w", [P, DC]), sb("eps_col", [P, 1])
        squares, inverse = sb("squares", [P, KT]), sb("inverse", [P, KT])
        q_inv, q_inv_now = sb("q_inv", [P, TILES]), sb("q_inv_now", [P, QT])
        half_max, neg_max = sb("half_max", [P, 2]), sb("neg_max", [P, QT])
        half_sum, row_sum, row_inv = sb("half_sum", [P, QT, 2]), sb("row_sum", [P, QT]), sb("row_inv", [P, QT])
        BQ, BK, FN, QN, KN = range(5)
        queries = xn[:, :, :].rearrange("p t d -> p (t d)").rearrange("p (b n) -> p b n", b=B)

        ps_s = ctx.enter_context(nc.psum_tensor("c_ps_s", [P, 4, BANK], F32))
        ps_t = ctx.enter_context(nc.psum_tensor("c_ps_t", [P, 2, BANK], F32))
        ps_p = ctx.enter_context(nc.psum_tensor("c_ps_p", [P, 2, BANK], F32))
        s_flat = ps_s[:, :, :].rearrange("p c n -> p (c n)")

        wq_loaded, wk_loaded, rows_loaded, set_up, qk_w_done = sem("wq_loaded"), sem("wk_loaded"), sem("rows_loaded"), sem("set_up"), sem("qk_w_done")
        columns_ps, columns_done = sem("columns_ps"), sem("columns_done")
        ctx_loaded = [sem(f"ctx_loaded{i}") for i in range(RING)]
        w_ps, w_hi_done, w_done = sem("w_ps"), sem("w_hi_done"), sem("w_done")
        xt_ps, xt_hi_done, xt_done = sem("xt_ps"), sem("xt_hi_done"), sem("xt_done")
        qp_ps, q_squared, q_kept, qs_ps, q_root, q_inv_done = (sem(n) for n in (
            "qp_ps", "q_squared", "q_kept", "qs_ps", "q_root", "q_inv_done"))
        c_squared, c_root, c_inv, f_scaled, f_hi_done, f_done = (sem(n) for n in (
            "c_squared", "c_root", "c_inv", "f_scaled", "f_hi_done", "f_done"))
        ft_ps, ft_hi_done, ft_done = sem("ft_ps"), sem("ft_hi_done"), sem("ft_done")
        kp_ps, k_squared, k_hi_done, k_done = sem("kp_ps"), sem("k_squared"), sem("k_hi_done"), sem("k_done")
        k_added, k_summed, ks_ps, k_root, k_inv = (sem(n) for n in ("k_added", "k_summed", "ks_ps", "k_root", "k_inv"))
        q_hi_done, q_done, q_inv_copied = sem("q_hi_done"), sem("q_done"), sem("q_inv_copied")
        s_ps, s_scaled, max_done, neg_max_done = sem("s_ps"), sem("s_scaled"), sem("max_done"), sem("neg_max_done")
        probs_done, sum_done, inv_done = sem("probs_done"), sem("sum_done"), sem("inv_done")
        pt_ps, pt_hi_done, pt_done = sem("pt_ps"), sem("pt_hi_done"), sem("pt_done")
        pv_ps, o_ps, o_scaled, added = sem("pv_ps"), sem("o_ps"), sem("o_scaled"), sem("added")
        block = ctx.enter_context(nc.Block())
        by_chunk = lambda bank, n=P: bank.rearrange("p (c n) -> p c n", c=DC)[:, :, 0:n]

        @block.sync
        def _(sp):
            sp.dma_start(raw[:, 0:DC, :], wq.rearrange("(t p) d -> p t d", p=P)).then_inc(wq_loaded, 16)
            for i, column in enumerate((bq, bk, fn_w, qn_w, kn_w)):
                sp.dma_start(vectors[DC * i:DC * (i + 1), :], column.rearrange("(c p) -> c p", p=P)).then_inc(rows_loaded, 16)
            for t in range(DC):
                sp.dma_start(wk_raw[t], wk[t * P:(t + 1) * P, :]).then_inc(wk_loaded, 16)
            sp.dma_start(fn_row[:, :], fn_w.partition_broadcast(P)).then_inc(rows_loaded, 16)

            def load_tile(b, t):
                n = rows_of(t)
                sp.dma_start(raw[0:n, t % RING, :], ctx_in[b, t * P:t * P + n, :]).then_inc(ctx_loaded[t % RING], 16)

            sp.wait_ge(w_ps, DC)
            for t in range(RING):
                load_tile(0, t)
            with sp.Fori(0, B) as b:
                for t in range(RING, KT):
                    sp.wait_ge(ft_ps, KT * b + t - RING + 1)
                    sp.wait_ge(f_done, KT * b + t - RING + 1)
                    load_tile(b, t)
                sp.wait_ge(ft_ps, KT * (b + 1))
                sp.wait_ge(f_done, KT * (b + 1))
                for t in range(RING):
                    load_tile((b + 1) % B, t)

        @block.gpsimd
        def _(pool):
            pool.memset(squares[:, :], 1.0).then_inc(set_up, 1)
            pool.memset(eps_col[:, :], EPS).then_inc(set_up, 1)
            pool.memset(t_hi[1][:, :, widths[1] - 1:widths[1]].bitcast(F32), 0.0).then_inc(set_up, 1)
            pool.memset(t_lo[1][:, :, widths[1] - 1:widths[1]].bitcast(F32), 0.0).then_inc(set_up, 1)
            with pool.Fori(0, B) as b:
                for t in range(KT):
                    n = rows_of(t)
                    pool.wait_ge(f_scaled, KT * b + t + 1)
                    if t == 0:
                        pool.wait_ge(o_ps, QT * b)
                    pool.tensor_tensor(f_hi[0:n, t, :], raw[0:n, t % RING, :], ones[0:n, 0:1].to_broadcast([n, D]),
                                       ALU.mult).then_inc(f_hi_done, 1)
                    pool.wait_ge(f_hi_done, KT * b + t + 1)
                    pool.tensor_tensor(f_lo[0:n, t, :], raw[0:n, t % RING, :], f_hi[0:n, t, :].bitcast(F32),
                                       ALU.subtract).then_inc(f_done, 1)

        @block.tensor
        def _(pe):
            def three(out, a_hi, a_lo, m_hi, m_lo, first, last):
                pe.matmul(out, a_hi, m_hi, start=first, stop=False)
                pe.matmul(out, a_hi, m_lo, start=False, stop=False)
                return pe.matmul(out, a_lo, m_hi, start=False, stop=last)

            def transpose_weights(which, tiles):
                pe.wait_ge(*((wk_loaded, 16 * DC) if which else (wq_loaded, 16)))
                for c in range(DC):
                    n = DC * which + c
                    if n >= 2:
                        pe.wait_ge(w_done, n - 1)
                    if n == DC:
                        pe.wait_ge(xt_done, TILES)
                    for t in range(DC):
                        tr = pe.transpose(ps_t[:, n % 2, t * P:(t + 1) * P], tiles[t][:, c * P:(c + 1) * P], ident[:, :])
                    tr.then_inc(w_ps, 1)

            def project(f, a, n):
                for c in range(DC):
                    mm = three(ps_s[:, f, 0:n], w_hi[:, c, f * P:(f + 1) * P], w_lo[:, c, f * P:(f + 1) * P],
                               t_hi[a][:, c, 0:n], t_lo[a][:, c, 0:n], c == 0, c == DC - 1)
                return mm

            def transpose_x(i):
                for t in range(QT * i, QT * (i + 1)):
                    if t >= 2:
                        pe.wait_ge(xt_done, t - 1)
                    else:
                        pe.wait_ge(w_done, DC)
                    for c in range(DC):
                        tr = pe.transpose(ps_t[:, t % 2, c * P:(c + 1) * P], xn[:, t, c * P:(c + 1) * P], ident[:, :])
                    tr.then_inc(xt_ps, 1)

            def sum_query_squares(i):
                pe.wait_ge(q_squared, DC * (i + 1))
                for j in range(QT):
                    for f in range(DC):
                        mm = pe.matmul(ps_p[:, 0, QT * i + j:QT * i + j + 1], squared[i % 2][:, f, j * P:(j + 1) * P], ones[:, 0:1],
                                       start=f == 0, stop=f == DC - 1)
                mm.then_inc(qs_ps, 1)

            transpose_weights(0, [raw[:, t, :] for t in range(DC)])
            pe.wait_ge(rows_loaded, 96)
            pe.transpose(ps_p[:, 1, 0:5 * DC], vectors[:, :], ident[0:5 * DC, 0:5 * DC]).then_inc(columns_ps, 1)
            transpose_x(0)
            for i in range(B):
                if i + 1 < B:
                    transpose_x(i + 1)
                pe.wait_ge(xt_done, QT * (i + 1))
                for f in range(DC):
                    if i:
                        pe.wait_ge(q_kept, DC * (i - 1) + f + 1)
                    project(f, i % 2, TOK).then_inc(qp_ps, 1)
                if i:
                    sum_query_squares(i - 1)
            sum_query_squares(B - 1)
            transpose_weights(1, wk_raw)
            pe.wait_ge(w_done, 2 * DC)
            pe.wait_ge(set_up, 4)
            pe.wait_ge(q_kept, DC * B)
            pe.wait_ge(q_root, 1)
            with pe.Fori(0, B) as b:
                def transpose_features(s, third=False):
                    for t in TILES_OF[s][2:] if third else TILES_OF[s][:2]:
                        n = rows_of(t)
                        pe.wait_ge(f_scaled, KT * b + t + 1)
                        if t >= 2:
                            pe.wait_ge(ft_done, KT * b + t - 1)
                        else:
                            pe.wait_ge(pt_done, GROUPS * QT * b)
                        for c in range(DC):
                            tr = pe.transpose(ps_t[:, t % 2, c * P:c * P + n], raw[0:n, t % RING, c * P:(c + 1) * P], ident[0:n, 0:n])
                        tr.then_inc(ft_ps, 1)

                def sum_key_squares(s):
                    n = COLS[s][1]
                    pe.wait_ge(k_summed, STEPS * b + s + 1)
                    if s >= 2:
                        pe.wait_ge(k_root, STEPS * b + s - 1)
                    else:
                        pe.wait_ge(o_scaled, QT * b)
                    pe.matmul(ps_p[:, s % 2, 0:n], ones[:, :], squared[s % 2][:, 0, :][:, 0:n], start=True, stop=True).then_inc(ks_ps, 1)

                transpose_features(0)
                for s in range(STEPS):
                    if s + 1 < STEPS:
                        transpose_features(s + 1)
                    pe.wait_ge(ft_done, KT * b + TILES_OF[s][-1] + 1)
                    for f in range(DC):
                        if s:
                            pe.wait_ge(k_done, DC * (STEPS * b + s - 1) + f + 1)
                        elif f == 0:
                            pe.wait_ge(s_scaled, 2 * QT * b)
                        project(f, s % 2, COLS[s][1]).then_inc(kp_ps, 1)
                        if s and f == 1:
                            sum_key_squares(s - 1)
                        if f == 1 and s + 1 < STEPS:
                            transpose_features(s + 1, third=True)

                def scores(j):
                    for half in range(2):
                        if j:
                            pe.wait_ge(s_scaled, 2 * QT * b + half + 1)
                        for ch in (2 * half, 2 * half + 1):
                            c0, n = CHUNKS[ch]
                            if j == 0:
                                last = max(s for s in range(STEPS) if COLS[s][0] < c0 + n)
                                pe.wait_ge(k_done, DC * (STEPS * b + STEPS - 1) + (ch + 1 if last < STEPS - 1 else DC))
                            for c in range(DC):
                                mm = three(ps_s[:, ch, 0:n], q_hi[:, c, j * P:(j + 1) * P], q_lo[:, c, j * P:(j + 1) * P],
                                           k_hi[:, c, c0:c0 + n], k_lo[:, c, c0:c0 + n], c == 0, c == DC - 1)
                            if j == 0 and ch == 0:
                                sum_key_squares(STEPS - 1)
                        mm.then_inc(s_ps, 1)
                        if j == 1 and half == 0:
                            transpose_probs(0, 0)
                            transpose_probs(0, 1)

                def transpose_probs(j, g):
                    n = GROUPS * j + g
                    if g == 0:
                        pe.wait_ge(probs_done, 2 * QT * b + 2 * j + 1)
                    if g == GROUPS // 2:
                        pe.wait_ge(probs_done, 2 * QT * b + 2 * j + 2)
                    if n >= 2:
                        pe.wait_ge(pt_done, GROUPS * QT * b + n - 1)
                    for k in range(GROUP * g, min(GROUP * (g + 1), KT)):
                        r = rows_of(k)
                        tr = pe.transpose(ps_t[0:r, n % 2, (k % GROUP) * P:(k % GROUP + 1) * P], probs[j][:, k * P:k * P + r], ident[:, :])
                    tr.then_inc(pt_ps, 1)

                def weigh(j, g):
                    n = GROUPS * j + g
                    pe.wait_ge(pt_done, GROUPS * QT * b + n + 1)
                    for k in range(GROUP * g, min(GROUP * (g + 1), KT)):
                        r = rows_of(k)
                        mm = three(ps_p[:, j, :], t_hi[n % 2][0:r, k % GROUP, 0:P], t_lo[n % 2][0:r, k % GROUP, 0:P],
                                   f_hi[0:r, k, :], f_lo[0:r, k, :], k == 0, k == KT - 1)
                    if g == GROUPS - 1:
                        mm.then_inc(o_ps, 1)
                    else:
                        mm.then_inc(pv_ps, 1)

                pe.wait_ge(q_done, b + 1)
                scores(0)
                scores(1)
                pe.wait_ge(f_done, KT * (b + 1))
                pe.wait_ge(k_root, STEPS * (b + 1))
                steps = [(j, g) for j in range(QT) for g in range(GROUPS)]
                for n, (j, g) in enumerate(steps):
                    if 1 < n + 1 < len(steps):
                        transpose_probs(*steps[n + 1])
                    weigh(j, g)

        @block.scalar
        def _(act):
            def weights_hi(n):
                act.wait_ge(w_ps, n + 1)
                if n == DC:
                    act.wait_ge(qp_ps, DC * B)
                act.activation(w_hi[:, n % DC, :], ps_t[:, n % 2, :], ACT.Copy,
                               scale=1.0 if n < DC else columns[:, FN, n % DC:n % DC + 1]).then_inc(w_hi_done, 1)

            for c in range(DC):
                weights_hi(c)
            act.wait_ge(columns_done, 1)
            act.wait_ge(set_up, 4)

            def inputs_hi(i):
                for t in range(QT * i, QT * (i + 1)):
                    act.wait_ge(xt_ps, t + 1)
                    if i >= 2:
                        act.wait_ge(qp_ps, DC * (i - 1))
                    act.activation(t_hi[i % 2][:, :, t % 2 * P:(t % 2 + 1) * P], by_chunk(ps_t[:, t % 2, :]),
                                   ACT.Copy).then_inc(xt_hi_done, 1)

            inputs_hi(0)
            for i in range(B):
                if i + 1 < B:
                    inputs_hi(i + 1)
                for f in range(DC):
                    act.wait_ge(qp_ps, DC * i + f + 1)
                    if i >= 2:
                        act.wait_ge(qs_ps, i - 1)
                    act.activation(squared[i % 2][:, f, 0:TOK], ps_s[:, f, 0:TOK], ACT.Square,
                                   bias=columns[:, BQ, f:f + 1]).then_inc(q_squared, 1)
            act.wait_ge(qs_ps, B)
            act.activation(q_inv[:, :], ps_p[:, 0, 0:TILES], ACT.Sqrt, bias=eps_col[:, :], scale=1.0 / D).then_inc(q_root, 1)

            def root_of_tiles(b, s, place, scratch):
                for t in TILES_OF[s]:
                    n = rows_of(t)
                    per_batch = [q for q in range(KT) if q % RING == t % RING]
                    act.wait_ge(ctx_loaded[t % RING], 16 * (len(per_batch) * place + per_batch.index(t) + 1))
                    act.wait_ge(c_squared, KT * place + t)
                    act.activation(scratch[0:n, :], raw[0:n, t % RING, :], ACT.Square,
                                   accum_out=squares[0:n, t:t + 1]).then_inc(c_squared, 1)
                t0, t1 = TILES_OF[s][0], TILES_OF[s][-1] + 1
                act.wait_ge(c_squared, KT * place + t1)
                act.activation(inverse[:, t0:t1], squares[:, t0:t1], ACT.Sqrt, bias=eps_col[:, :], scale=1.0 / D).then_inc(c_root, 1)

            root_of_tiles(0, 0, 0, shared[:, 0:D])
            root_of_tiles(0, 1, 0, shared[:, 0:D])
            for c in range(DC):
                weights_hi(DC + c)
            with act.Fori(0, B) as b:
                def features_hi(s, third=False):
                    for t in TILES_OF[s][2:] if third else TILES_OF[s][:2]:
                        n = rows_of(t)
                        act.wait_ge(ft_ps, KT * b + t + 1)
                        if s >= 2:
                            act.wait_ge(kp_ps, DC * (STEPS * b + s - 1))
                        else:
                            act.wait_ge(o_ps, QT * b)
                        at = t * P - COLS[s][0]
                        act.activation(t_hi[s % 2][:, :, at:at + n], by_chunk(ps_t[:, t % 2, :], n), ACT.Copy).then_inc(ft_hi_done, 1)

                def key_roots(s):
                    c0, n = COLS[s]
                    act.wait_ge(ks_ps, STEPS * b + s + 1)
                    act.activation(key_inv[:, c0:c0 + n], ps_p[:, s % 2, 0:n], ACT.Sqrt, bias=eps_col[:, :], scale=1.0 / D
                                   ).then_inc(k_root, 1)

                features_hi(0)
                for s in range(STEPS):
                    c0, w = COLS[s]
                    if s + 1 < STEPS:
                        features_hi(s + 1)
                    if s == 0:
                        act.wait_ge(s_ps, 2 * QT * b)
                        act.activation(q_hi[:, :, :].rearrange("p c n -> p (c n)"),
                                       queries[:, bass.ds(b, 1), :].rearrange("p a n -> p (a n)"), ACT.Copy).then_inc(q_hi_done, 1)
                    for f in range(DC):
                        act.wait_ge(kp_ps, DC * (STEPS * b + s) + f + 1)
                        if s >= 2:
                            act.wait_ge(ks_ps, STEPS * b + s - 1)
                        act.activation(k_hi[:, f, c0:c0 + w], ps_s[:, f, 0:w], ACT.Identity, bias=columns[:, BK, f:f + 1]
                                       ).then_inc(k_hi_done, 1)
                        act.activation(squared[s % 2][:, f, 0:w], ps_s[:, f, 0:w], ACT.Square, bias=columns[:, BK, f:f + 1]
                                       ).then_inc(k_squared, 1)
                        if f == 0 and s + 2 < STEPS:
                            root_of_tiles(b, s + 2, b, scratch)
                        if f == 1 and s + 1 < STEPS:
                            features_hi(s + 1, third=True)
                        if f == 2 and s:
                            key_roots(s - 1)
                key_roots(STEPS - 1)
                root_of_tiles(b + 1, 0, b + 1, scratch)
                root_of_tiles(b + 1, 1, b + 1, scratch)

                def probs_hi(j, g):
                    n = GROUPS * j + g
                    m = min(GROUP, KT - GROUP * g)
                    r = P if m > 1 else LAST
                    act.wait_ge(pt_ps, GROUPS * QT * b + n + 1)
                    if n >= 2:
                        if (n - 2) % GROUPS == GROUPS - 1:
                            act.wait_ge(o_ps, QT * b + (n - 2) // GROUPS + 1)
                        else:
                            act.wait_ge(pv_ps, (GROUPS - 1) * (QT * b + (n - 2) // GROUPS) + (n - 2) % GROUPS + 1)
                    act.activation(t_hi[n % 2][0:r, 0:m, 0:P], by_chunk(ps_t[:, n % 2, :])[0:r, 0:m, :], ACT.Copy).then_inc(pt_hi_done, 1)

                for j in range(QT):
                    act.wait_ge(neg_max_done, QT * b + j + 1)
                    for half, (lo, hi) in enumerate(HALVES):
                        act.activation(probs[j][:, lo:hi], probs[j][:, lo:hi], ACT.Exp, bias=neg_max[:, j:j + 1], scale=SCALE,
                                       accum_out=half_sum[:, j, half:half + 1]).then_inc(probs_done, 1)
                    if j == 0:
                        probs_hi(0, 0)
                        probs_hi(0, 1)
                for j in range(QT):
                    for g in range(GROUPS):
                        if GROUPS * j + g >= 2:
                            probs_hi(j, g)

        @block.vector
        def _(dve):
            def weights_lo(n):
                dve.wait_ge(w_hi_done, n + 1)
                if n < DC:
                    dve.tensor_tensor(w_lo[:, n, :], ps_t[:, n % 2, :], w_hi[:, n, :].bitcast(F32), ALU.subtract).then_inc(w_done, 1)
                else:
                    dve.scalar_tensor_tensor(w_lo[:, n % DC, :], ps_t[:, n % 2, :], columns[:, FN, n % DC:n % DC + 1],
                                             w_hi[:, n % DC, :].bitcast(F32), ALU.mult, ALU.subtract).then_inc(w_done, 1)

            for c in range(DC):
                weights_lo(c)
            dve.wait_ge(columns_ps, 1)
            dve.tensor_copy(columns[:, :, :].rearrange("p i c -> p (i c)"), ps_p[:, 1, 0:5 * DC]).then_inc(columns_done, 1)
            dve.wait_ge(columns_done, 1)
            dve.tensor_tensor(qk_w[:, :], columns[:, QN, :], columns[:, KN, :], ALU.mult).then_inc(qk_w_done, 1)

            def inputs_lo(i):
                for t in range(QT * i, QT * (i + 1)):
                    dve.wait_ge(xt_hi_done, t + 1)
                    at = t % 2 * P
                    dve.tensor_tensor(t_lo[i % 2][:, :, at:at + P], by_chunk(ps_t[:, t % 2, :]),
                                      t_hi[i % 2][:, :, at:at + P].bitcast(F32), ALU.subtract).then_inc(xt_done, 1)

            inputs_lo(0)
            dve.wait_ge(qk_w_done, 1)
            for i in range(B):
                if i + 1 < B:
                    inputs_lo(i + 1)
                for f in range(DC):
                    dve.wait_ge(q_squared, DC * i + f + 1)
                    dve.tensor_scalar(queries[:, i, f * TOK:(f + 1) * TOK], ps_s[:, f, 0:TOK], columns[:, BQ, f:f + 1],
                                      qk_w[:, f:f + 1], ALU.add, ALU.mult).then_inc(q_kept, 1)
            dve.wait_ge(q_root, 1)
            dve.reciprocal(q_inv[:, :], q_inv[:, :]).then_inc(q_inv_done, 1)

            def scale_tiles(s, place):
                dve.wait_ge(c_root, STEPS * place + s + 1)
                t0, t1 = TILES_OF[s][0], TILES_OF[s][-1] + 1
                dve.reciprocal(inverse[:, t0:t1], inverse[:, t0:t1]).then_inc(c_inv, 1)
                dve.wait_ge(c_inv, STEPS * place + s + 1)
                for t in TILES_OF[s]:
                    n = rows_of(t)
                    dve.tensor_scalar(raw[0:n, t % RING, :], raw[0:n, t % RING, :], inverse[0:n, t:t + 1], None,
                                      ALU.mult).then_inc(f_scaled, 1)

            scale_tiles(0, 0)
            scale_tiles(1, 0)
            for c in range(DC):
                weights_lo(DC + c)
            dve.wait_ge(q_inv_done, 1)
            with dve.Fori(0, B) as b:
                def features_lo(s, third=False):
                    for t in TILES_OF[s][2:] if third else TILES_OF[s][:2]:
                        n = rows_of(t)
                        at = t * P - COLS[s][0]
                        dve.wait_ge(ft_hi_done, KT * b + t + 1)
                        dve.tensor_tensor(t_lo[s % 2][:, :, at:at + n], by_chunk(ps_t[:, t % 2, :], n),
                                          t_hi[s % 2][:, :, at:at + n].bitcast(F32), ALU.subtract).then_inc(ft_done, 1)

                def output(b, j):
                    x_tile = x_res[:, bass.ds(QT * b + j, 1), :].rearrange("p a d -> p (a d)")
                    dve.wait_ge(o_ps, QT * b + j + 1)
                    dve.scalar_tensor_tensor(probs[j][:, 0:D], ps_p[:, j, :], row_inv[:, j:j + 1], fn_row[:, :], ALU.mult,
                                             ALU.mult).then_inc(o_scaled, 1)
                    dve.wait_ge(o_scaled, QT * b + j + 1)
                    dve.tensor_tensor(x_tile, probs[j][:, 0:D], x_tile, ALU.add).then_inc(added, 1)

                def key_inverses(s):
                    c0, n = COLS[s]
                    dve.wait_ge(k_root, STEPS * b + s + 1)
                    dve.reciprocal(key_inv[:, c0:c0 + n], key_inv[:, c0:c0 + n]).then_inc(k_inv, 1)

                features_lo(0)
                for s in range(STEPS):
                    c0, w = COLS[s]
                    if s + 1 < STEPS:
                        features_lo(s + 1)
                    if s == 0:
                        dve.wait_ge(q_hi_done, b + 1)
                        dve.tensor_tensor(q_lo[:, :, :].rearrange("p c n -> p (c n)"),
                                          queries[:, bass.ds(b, 1), :].rearrange("p a n -> p (a n)"),
                                          q_hi[:, :, :].rearrange("p c n -> p (c n)").bitcast(F32), ALU.subtract).then_inc(q_done, 1)
                        dve.tensor_copy(q_inv_now[:, :], q_inv[:, bass.ds(QT * b, QT)]).then_inc(q_inv_copied, 1)
                    for f in range(DC):
                        dve.wait_ge(k_squared, DC * (STEPS * b + s) + f + 1)
                        dve.scalar_tensor_tensor(k_lo[:, f, c0:c0 + w], ps_s[:, f, 0:w], columns[:, BK, f:f + 1],
                                                 k_hi[:, f, c0:c0 + w].bitcast(F32), ALU.add, ALU.subtract).then_inc(k_done, 1)
                        if f == 1 and s + 2 < STEPS:
                            scale_tiles(s + 2, b)
                        if f == 1 and s + 1 < STEPS:
                            features_lo(s + 1, third=True)
                        if f == 2 and s:
                            key_inverses(s - 1)
                    sq = squared[s % 2][:, :, 0:w]
                    dve.tensor_tensor(sq[:, 0:2, :], sq[:, 0:2, :], sq[:, 2:4, :], ALU.add).then_inc(k_added, 1)
                    dve.wait_ge(k_added, STEPS * b + s + 1)
                    dve.tensor_tensor(sq[:, 0, :], sq[:, 0, :], sq[:, 1, :], ALU.add).then_inc(k_summed, 1)
                key_inverses(STEPS - 1)
                dve.wait_ge(q_inv_copied, b + 1)
                dve.wait_ge(k_inv, STEPS * (b + 1))
                def probs_lo(j, g):
                    n = GROUPS * j + g
                    m = min(GROUP, KT - GROUP * g)
                    r = P if m > 1 else LAST
                    dve.wait_ge(pt_hi_done, GROUPS * QT * b + n + 1)
                    dve.tensor_tensor(t_lo[n % 2][0:r, 0:m, 0:P], by_chunk(ps_t[:, n % 2, :])[0:r, 0:m, :],
                                      t_hi[n % 2][0:r, 0:m, 0:P].bitcast(F32), ALU.subtract).then_inc(pt_done, 1)

                for j in range(QT):
                    for half, (lo, hi) in enumerate(HALVES):
                        if j == 1 and half == 1:
                            probs_lo(0, 0)
                            probs_lo(0, 1)
                        dve.wait_ge(s_ps, 2 * QT * b + 2 * j + half + 1)
                        dve.scalar_tensor_tensor(probs[j][:, lo:hi], s_flat[:, lo:hi], q_inv_now[:, j:j + 1], key_inv[:, lo:hi],
                                                 ALU.mult, ALU.mult).then_inc(s_scaled, 1)
                        dve.wait_ge(s_scaled, 2 * QT * b + 2 * j + half + 1)
                        dve.reduce_max(half_max[:, half:half + 1], probs[j][:, lo:hi], AX.X).then_inc(max_done, 1)
                    dve.wait_ge(max_done, 2 * QT * b + 2 * j + 2)
                    dve.tensor_scalar(neg_max[:, j:j + 1], half_max[:, 0:1], half_max[:, 1:2], -SCALE, ALU.max,
                                      ALU.mult).then_inc(neg_max_done, 1)
                    if j == 0:
                        scale_tiles(0, b + 1)
                        scale_tiles(1, b + 1)
                for j in range(QT):
                    for g in range(GROUPS):
                        if GROUPS * j + g >= 2:
                            probs_lo(j, g)
                        if GROUPS * j + g == GROUPS:
                            output(b, 0)
                    if j == 0:
                        dve.wait_ge(probs_done, 2 * QT * (b + 1))
                        dve.tensor_tensor(row_sum[:, :], half_sum[:, :, 0], half_sum[:, :, 1], ALU.add).then_inc(sum_done, 1)
                        dve.wait_ge(sum_done, b + 1)
                        dve.reciprocal(row_inv[:, :], row_sum[:, :]).then_inc(inv_done, 1)
                        dve.wait_ge(inv_done, b + 1)
                output(b, 1)


def routed_experts_block(nc, held, gate_w, w_gate_up, w_down, shared_gate_up, shared_down, x_res, xn, ident, ones, out):
    TILES, D = x_res.shape[1], x_res.shape[2]
    E, I2, _ = w_gate_up.shape
    I = I2 // 2
    SHARED = shared_down.shape[1] // I
    N = E + SHARED
    DC = D // P
    BANK = 512
    TC = TILES * P // BANK
    TPC = BANK // P
    JOBS = 3
    assert I == P and D == BANK and TC == 2 and E % 2 == 0 and SHARED % 2 == 0

    with ExitStack() as ctx:
        sb = lambda n, s, d=F32: ctx.enter_context(nc.sbuf_tensor(f"d_{n}", s, d))
        sem = lambda n: new_semaphore(nc, held, f"d_{n}")
        xt_hi, xt_lo = sb("xt_hi", [P, DC, TILES * P], F32R), sb("xt_lo", [P, DC, TILES * P], F32R)
        up_raw = [sb(f"up_raw{a}", [P, 2, D]) for a in range(2)]
        down_raw = [sb(f"down_raw{a}", [P, DC, I]) for a in range(2)]
        up_hi = [sb(f"up_hi{a}", [P, 2, DC, I], F32R) for a in range(2)]
        up_lo = [sb(f"up_lo{a}", [P, 2, DC, I], F32R) for a in range(2)]
        down_hi = [sb(f"down_hi{a}", [P, D], F32R) for a in range(2)]
        down_lo = [sb(f"down_lo{a}", [P, D], F32R) for a in range(2)]
        gated = [sb(f"gated{i}", [P, BANK]) for i in range(TC)]
        act_hi, act_lo = sb("act_hi", [P, TC, BANK], F32R), sb("act_lo", [P, TC, BANK], F32R)
        gate_raw, gate_hi, gate_lo = sb("gate_raw", [E, D]), sb("gate_hi", [P, DC, E], F32R), sb("gate_lo", [P, DC, E], F32R)
        ramp = sb("ramp", [P, E])
        logits, scores = sb("logits", [P, TILES, E]), sb("scores", [P, TILES, E])
        hit, first, second, rest = (sb(n, [P, TILES, E]) for n in ("hit", "first", "second", "rest"))
        row, row2, best, runner = (sb(n, [P, TILES]) for n in ("row", "row2", "best", "runner"))
        share = sb("share", [P, TILES, N])

        ps_t = ctx.enter_context(nc.psum_tensor("d_ps_t", [P, 2, BANK], F32))
        ps_h = ctx.enter_context(nc.psum_tensor("d_ps_h", [P, TC, 2, BANK], F32))
        ps_y = ctx.enter_context(nc.psum_tensor("d_ps_y", [P, 2, BANK], F32))

        gate_loaded, pads_set, gate_ps, gate_hi_done, gate_done = (sem(n) for n in (
            "gate_loaded", "pads_set", "gate_ps", "gate_hi_done", "gate_done"))
        xt_ps, xt_hi_done, xt_done, logits_ps = sem("xt_ps"), sem("xt_hi_done"), sem("xt_done"), sem("logits_ps")
        logits_out, centred, exp_done, share_done, router = (sem(n) for n in ("logits_out", "centred", "exp_done", "share_done", "router"))
        raw_loaded = [sem(f"raw_loaded{a}") for a in range(2)]
        w_ps, w_hi_done, w_done = sem("w_ps"), sem("w_hi_done"), sem("w_done")
        h_ps, silu_done, gated_done, act_hi_done, act_done = (sem(n) for n in ("h_ps", "silu_done", "gated_done", "act_hi_done", "act_done"))
        y_ps, added, stored = sem("y_ps"), sem("added"), sem("stored")
        block = ctx.enter_context(nc.Block())
        by_chunk = lambda bank: bank.rearrange("p (c n) -> p c n", c=DC)
        tile_rows = out.rearrange("b (t p) d -> (b t) p d", p=P)

        @block.sync
        def _(sp):
            def load(a, transposed, up, down):
                sp.wait_ge(w_ps, transposed)
                sp.dma_start(up_raw[a][:, :, :], up).then_inc(raw_loaded[a], 16)
                sp.dma_start(down_raw[a][:, :, :], down).then_inc(raw_loaded[a], 16)

            def routed(e):
                return (w_gate_up[bass.ds(e, 1), :, :].rearrange("a (k p) h -> p (a k) h", p=P),
                        w_down[bass.ds(e, 1), :, :].rearrange("a (c p) i -> p (a c) i", p=P))

            def shared(s):
                return (shared_gate_up.rearrange("(k r) h -> r k h", k=2)[bass.ds(s * I, I), :, :],
                        shared_down[:, bass.ds(s * I, I)].rearrange("(c p) i -> p c i", p=P))

            sp.dma_start(gate_raw[:, :], gate_w).then_inc(gate_loaded, 16)
            load(0, 0, *routed(0))
            load(1, 0, *routed(1))
            with sp.Fori(1, E // 2) as i:
                for a in range(2):
                    load(a, JOBS * (2 * i + a - 1), *routed(2 * i + a))
            with sp.Fori(0, SHARED // 2) as i:
                for a in range(2):
                    load(a, JOBS * (E + 2 * i + a - 1), *shared(2 * i + a))
            for t in range(TILES):
                sp.wait_ge(added, TILES * (N - 1) + t + 1)
                sp.dma_start(tile_rows[t], x_res[:, t, :]).then_inc(stored, 16)
            sp.wait_ge(stored, 16 * TILES)

        @block.gpsimd
        def _(pool):
            pool.iota(ramp[:, :], pattern=[[-1, E]], base=E, channel_multiplier=0,
                      allow_small_or_imprecise_dtypes=True).then_inc(pads_set, 1)
            pool.memset(share[:, :, E:N], 1.0).then_inc(pads_set, 1)

        @block.tensor
        def _(pe):
            def three(o, w_hi, w_lo, m_hi, m_lo, start, stop):
                pe.matmul(o, w_hi, m_hi, start=start, stop=False)
                pe.matmul(o, w_hi, m_lo, start=False, stop=False)
                return pe.matmul(o, w_lo, m_hi, start=False, stop=stop)

            def transpose_weights(n, a, pair, first=False):
                pe.wait_ge(raw_loaded[a], 32 * pair + 32)
                for job in range(JOBS):
                    bank = (JOBS * a + job) % 2
                    if not (first and job < 2):
                        pe.wait_ge(w_done, JOBS * n + job - 1)
                    for c in range(DC):
                        src = down_raw[a][:, c, :] if job == 2 else up_raw[a][:, job, c * P:(c + 1) * P]
                        tr = pe.transpose(ps_t[:, bank, c * P:(c + 1) * P], src, ident[:, :])
                    tr.then_inc(w_ps, 1)

            def up(n, a):
                pe.wait_ge(w_done, JOBS * n + JOBS)
                pe.wait_ge(gated_done, TC * n)
                for tc in range(TC):
                    for k in range(2):
                        for c in range(DC):
                            mm = three(ps_h[:, tc, k, :], up_hi[a][:, k, c, :], up_lo[a][:, k, c, :],
                                       xt_hi[:, c, tc * BANK:(tc + 1) * BANK], xt_lo[:, c, tc * BANK:(tc + 1) * BANK],
                                       c == 0, c == DC - 1)
                    mm.then_inc(h_ps, 1)

            def down(n, a):
                for t in range(TILES):
                    tc, p0 = t // TPC, t % TPC * P
                    if t % TPC == 0:
                        pe.wait_ge(act_done, TC * n + tc + 1)
                    pe.wait_ge(added, TILES * n + max(t - 1, 0))
                    three(ps_y[:, t % 2, :], act_hi[:, tc, p0:p0 + P], act_lo[:, tc, p0:p0 + P], down_hi[a][:, :],
                          down_lo[a][:, :], True, True).then_inc(y_ps, 1)

            for t in range(TILES):
                if t >= 2:
                    pe.wait_ge(xt_done, t - 1)
                for c in range(DC):
                    tr = pe.transpose(ps_t[:, t % 2, c * P:(c + 1) * P], xn[:, t, c * P:(c + 1) * P], ident[:, :])
                tr.then_inc(xt_ps, 1)
            pe.wait_ge(gate_loaded, 16)
            for c in range(DC):
                tr = pe.transpose(ps_h[:, 0, 0, c * E:(c + 1) * E], gate_raw[:, c * P:(c + 1) * P], ident[0:E, 0:E])
            tr.then_inc(gate_ps, 1)
            pe.wait_ge(xt_done, TILES)
            transpose_weights(0, 0, 0, first=True)
            pe.wait_ge(gate_done, 1)
            for t in range(TILES):
                for c in range(DC):
                    mm = three(ps_y[:, 0, t * E:(t + 1) * E], xt_hi[:, c, t * P:(t + 1) * P], xt_lo[:, c, t * P:(t + 1) * P],
                               gate_hi[:, c, :], gate_lo[:, c, :], c == 0, c == DC - 1)
            mm.then_inc(logits_ps, 1)
            with pe.Fori(0, N // 2 - 1) as i:
                pe.wait_ge(logits_out, 1)
                up(2 * i, 0)
                transpose_weights(2 * i + 1, 1, i)
                down(2 * i, 0)
                up(2 * i + 1, 1)
                transpose_weights(2 * i + 2, 0, i + 1)
                down(2 * i + 1, 1)
            up(N - 2, 0)
            transpose_weights(N - 1, 1, N // 2 - 1)
            down(N - 2, 0)
            up(N - 1, 1)
            down(N - 1, 1)

        @block.scalar
        def _(act):
            def weights_hi(n, a):
                for job in range(JOBS):
                    bank = ps_t[:, (JOBS * a + job) % 2, :]
                    act.wait_ge(w_ps, JOBS * n + job + 1)
                    if job == 2:
                        act.activation(down_hi[a][:, :], bank, ACT.Copy).then_inc(w_hi_done, 1)
                    else:
                        act.activation(up_hi[a][:, job, :, :], by_chunk(bank), ACT.Copy).then_inc(w_hi_done, 1)

            def hidden(n):
                for tc in range(TC):
                    act.wait_ge(h_ps, TC * n + tc + 1)
                    act.wait_ge(act_done, TC * n)
                    act.activation(gated[tc][:, :], ps_h[:, tc, 0, :], ACT.Silu).then_inc(silu_done, 1)
                    act.wait_ge(gated_done, TC * n + tc + 1)
                    act.wait_ge(y_ps, TILES * n)
                    act.activation(act_hi[:, tc, :], gated[tc][:, :], ACT.Copy).then_inc(act_hi_done, 1)

            for t in range(TILES):
                act.wait_ge(xt_ps, t + 1)
                act.activation(xt_hi[:, :, t * P:(t + 1) * P], by_chunk(ps_t[:, t % 2, :]), ACT.Copy).then_inc(xt_hi_done, 1)
            act.wait_ge(gate_ps, 1)
            act.activation(gate_hi[:, :, :], ps_h[:, 0, 0, 0:DC * E].rearrange("p (c e) -> p c e", c=DC), ACT.Copy).then_inc(gate_hi_done, 1)
            weights_hi(0, 0)
            act.wait_ge(centred, 1)
            act.activation(scores[:, :, :], scores[:, :, :], ACT.Exp).then_inc(exp_done, 1)
            with act.Fori(0, N // 2 - 1) as i:
                hidden(2 * i)
                weights_hi(2 * i + 1, 1)
                hidden(2 * i + 1)
                weights_hi(2 * i + 2, 0)
            hidden(N - 2)
            weights_hi(N - 1, 1)
            hidden(N - 1)

        @block.vector
        def _(dve):
            chain = Chain(dve, router)

            def weights_lo(n, a):
                for job in range(JOBS):
                    bank = ps_t[:, (JOBS * a + job) % 2, :]
                    dve.wait_ge(w_hi_done, JOBS * n + job + 1)
                    if job == 2:
                        dve.tensor_tensor(down_lo[a][:, :], bank, down_hi[a][:, :].bitcast(F32), ALU.subtract).then_inc(w_done, 1)
                    else:
                        dve.tensor_tensor(up_lo[a][:, job, :, :], by_chunk(bank), up_hi[a][:, job, :, :].bitcast(F32),
                                          ALU.subtract).then_inc(w_done, 1)

            def hidden(n):
                for tc in range(TC):
                    dve.wait_ge(silu_done, TC * n + tc + 1)
                    dve.tensor_tensor(gated[tc][:, :], ps_h[:, tc, 1, :], gated[tc][:, :], ALU.mult).then_inc(gated_done, 1)
                    dve.wait_ge(act_hi_done, TC * n + tc + 1)
                    dve.tensor_tensor(act_lo[:, tc, :], gated[tc][:, :], act_hi[:, tc, :].bitcast(F32), ALU.subtract).then_inc(act_done, 1)

            def add(n):
                for t in range(TILES):
                    dve.wait_ge(y_ps, TILES * n + t + 1)
                    dve.wait_ge(added, TILES * n)
                    dve.scalar_tensor_tensor(x_res[:, t, :], ps_y[:, t % 2, :], share[:, t, bass.ds(n, 1)], x_res[:, t, :],
                                             ALU.mult, ALU.add).then_inc(added, 1)

            for t in range(TILES):
                dve.wait_ge(xt_hi_done, t + 1)
                dve.tensor_tensor(xt_lo[:, :, t * P:(t + 1) * P], by_chunk(ps_t[:, t % 2, :]),
                                  xt_hi[:, :, t * P:(t + 1) * P].bitcast(F32), ALU.subtract).then_inc(xt_done, 1)
            dve.wait_ge(gate_hi_done, 1)
            dve.tensor_tensor(gate_lo[:, :, :], ps_h[:, 0, 0, 0:DC * E].rearrange("p (c e) -> p c e", c=DC),
                              gate_hi[:, :, :].bitcast(F32), ALU.subtract).then_inc(gate_done, 1)
            weights_lo(0, 0)
            dve.wait_ge(logits_ps, 1)
            dve.tensor_copy(logits[:, :, :], ps_y[:, 0, 0:TILES * E].rearrange("p (t e) -> p t e", t=TILES)).then_inc(logits_out, 1)
            dve.wait_ge(logits_out, 1)
            softmax_rows(dve, chain, scores[:, :, :], logits[:, :, :], row[:, :], row2[:, :], exp_done, centred)
            dve.wait_ge(pads_set, 2)
            top_two(dve, chain, scores[:, :, :], ramp[:, :], hit[:, :, :], first[:, :, :], second[:, :, :], rest[:, :, :],
                    row[:, :], best[:, :], runner[:, :])
            chain.link(dve.tensor_tensor(row[:, :], best[:, :], runner[:, :], ALU.add))
            chain.link(dve.reciprocal(row[:, :], row[:, :]))
            chain.link(dve.tensor_tensor(best[:, :], best[:, :], row[:, :], ALU.mult))
            chain.link(dve.tensor_tensor(runner[:, :], runner[:, :], row[:, :], ALU.mult))
            chain.link(dve.tensor_tensor(first[:, :, :], first[:, :, :], wide(best[:, :], E), ALU.mult))
            chain.link(dve.tensor_tensor(second[:, :, :], second[:, :, :], wide(runner[:, :], E), ALU.mult))
            chain.link(dve.tensor_tensor(share[:, :, 0:E], first[:, :, :], second[:, :, :], ALU.add))
            with dve.Fori(0, N // 2 - 1) as i:
                hidden(2 * i)
                weights_lo(2 * i + 1, 1)
                add(2 * i)
                hidden(2 * i + 1)
                weights_lo(2 * i + 2, 0)
                add(2 * i + 1)
            hidden(N - 2)
            weights_lo(N - 1, 1)
            add(N - 2)
            hidden(N - 1)
            add(N - 1)


def layers(nc, x, ctx_4096, L0_xattn_Wq, L0_xattn_Wk, L0_xattn_Wv, L0_xattn_Wo, L0_ffn_gate_w, L0_ffn_gate_b, L0_ffn_w1,
           L0_ffn_b1, L0_ffn_w2, L0_ffn_b2, L1_xattn_Wq_w, L1_xattn_Wq_b, L1_xattn_Wk_w, L1_xattn_Wk_b, L1_xattn_fn_w,
           L1_xattn_qn_w, L1_xattn_kn_w, L1_ffn_gate_w, L1_ffn_w_gate_up, L1_ffn_w_down, L1_ffn_shared_w_gate_up,
           L1_ffn_shared_w_down, out):
    B, S, D = x.shape
    held = []
    with ExitStack() as ctx:
        sb = lambda n, s: ctx.enter_context(nc.sbuf_tensor(n, s, F32))
        x_res, xn = sb("x_res", [P, B * S // P, D]), sb("xn", [P, B * S // P, D])
        ident, ones = sb("ident", [P, P]), sb("ones", [P, P])
        norm_block(nc, held, x_res, xn, 1e-5, "norm0", load_from=x, constants=(ident, ones))
        grouped_attention_block(nc, held, ctx_4096, L0_xattn_Wq, L0_xattn_Wk, L0_xattn_Wv, L0_xattn_Wo, x_res, xn, ident, ones)
        release(nc, held)
        norm_block(nc, held, x_res, xn, 1e-5, "norm1")
        gated_experts_block(nc, held, L0_ffn_gate_w, L0_ffn_gate_b, L0_ffn_w1, L0_ffn_b1, L0_ffn_w2, L0_ffn_b2, x_res, xn, ident,
                            ones, B)
        release(nc, held)
        norm_block(nc, held, x_res, xn, 1e-5, "norm2")
        normed_attention_block(nc, held, ctx_4096, L1_xattn_Wq_w, L1_xattn_Wq_b, L1_xattn_Wk_w, L1_xattn_Wk_b, L1_xattn_fn_w,
                               L1_xattn_qn_w, L1_xattn_kn_w, x_res, xn, ident, ones)
        release(nc, held)
        norm_block(nc, held, x_res, xn, 1e-5, "norm3")
        routed_experts_block(nc, held, L1_ffn_gate_w, L1_ffn_w_gate_up, L1_ffn_w_down, L1_ffn_shared_w_gate_up,
                             L1_ffn_shared_w_down, x_res, xn, ident, ones, out)


_INS = ["x", "ctx_4096", "L0_xattn_Wq", "L0_xattn_Wk", "L0_xattn_Wv", "L0_xattn_Wo", "L0_ffn_gate_w", "L0_ffn_gate_b",
        "L0_ffn_w1", "L0_ffn_b1", "L0_ffn_w2", "L0_ffn_b2", "L1_xattn_Wq_w", "L1_xattn_Wq_b", "L1_xattn_Wk_w",
        "L1_xattn_Wk_b", "L1_xattn_fn_w", "L1_xattn_qn_w", "L1_xattn_kn_w", "L1_ffn_gate_w", "L1_ffn_w_gate_up",
        "L1_ffn_w_down", "L1_ffn_shared_w_gate_up", "L1_ffn_shared_w_down"]


def kernel(**inputs):
    import concourse.bacc as _bacc
    import numpy as _np
    from concourse.bass_utils import run_bass_kernel_spmd as _run

    nc = _bacc.Bacc("TRN2", target_bir_lowering=False, num_devices=1)
    arrays, args = {}, []
    for name in _INS:
        a = _np.ascontiguousarray(inputs[name])
        arrays[f"in_{name}"] = a
        args.append(nc.dram_tensor(f"in_{name}", a.shape, mybir.dt.from_np(a.dtype), kind="ExternalInput").ap())
    out = nc.dram_tensor("out_x", inputs["x"].shape, F32, kind="ExternalOutput").ap()
    layers(nc, *args, out)
    return _run(nc, [arrays], core_ids=[0]).results[0]["out_x"]
```

```python
import math
from contextlib import ExitStack

import concourse.bass as bass
from concourse import mybir

F32 = mybir.dt.float32
F32R = mybir.dt.float32r
ALU = mybir.AluOpType
ACT = mybir.ActivationFunctionType
AX = mybir.AxisListType
P = 128


def new_semaphore(nc, held, name):
    held.append(nc.alloc_semaphore(name=name))
    return held[-1]


PRIMED = 1


def prime(nc, semaphores):
    for semaphore in semaphores:
        nc.gpsimd.sem_inc(semaphore, PRIMED)


def release(nc, held):
    nc.clear_and_free_semaphores(list(held))
    nc.all_engine_barrier()
    held.clear()


def tile_statistics(dve, stats, x_tile, tile, done):
    dve.bn_stats(stats[:, bass.ds(tile, 1), :].rearrange("p a s -> p (a s)"), x_tile).then_inc(done, 1)


def norm_block(nc, held, x_res, xn, stats, eps, name, load_from=None, constants=None, prefetch=None):
    tiles = x_res.shape[1]
    with ExitStack() as ctx:
        sb = lambda n, s, d=F32: ctx.enter_context(nc.sbuf_tensor(f"{name}_{n}", s, d))
        sem = lambda n: new_semaphore(nc, held, f"{name}_{n}")
        mean_var = sb("mean_var", [P, tiles, 2])
        var_eps = sb("var_eps", [P, tiles])
        deviation = sb("deviation", [P, tiles])
        inverse = sb("inverse", [P, tiles])
        shift = sb("shift", [P, tiles])
        x_loaded = [sem(f"x_loaded{t}") for t in range(tiles)] if load_from is not None else None
        zeroed, constants_ready = sem("zeroed"), sem("constants_ready")
        stats_done, mean_done, var_done = sem("stats_done"), sem("mean_done"), sem("var_done")
        deviation_done, inverse_done, shift_done, normed = (sem(n) for n in ("deviation_done", "inverse_done", "shift_done", "normed"))
        block = ctx.enter_context(nc.Block())

        if load_from is not None:
            rows = load_from.rearrange("b (t p) d -> (b t) p d", p=P)

            @block.sync
            def _(sp):
                for t in range(tiles):
                    sp.dma_start(x_res[:, t, :], rows[t]).then_inc(x_loaded[t], 16)

            @block.gpsimd
            def _(pool):
                ident, ones = constants
                pool.memset(ident[:, :], 0.0).then_inc(zeroed, 1)
                pool.memset(ones[:, :], 1.0).then_inc(constants_ready, 1)
                pool.wait_ge(zeroed, 1)
                pool.affine_select(out=ident[:, :], in_=ident[:, :], compare_op=ALU.not_equal, fill=1.0,
                                   base=0, pattern=[[-1, P]], channel_multiplier=1).then_inc(constants_ready, 1)

        if prefetch is not None:
            block.sync(prefetch)

        @block.vector
        def _(dve):
            if x_loaded:
                for t in range(tiles):
                    dve.wait_ge(x_loaded[t], 16)
                    dve.bn_stats(stats[:, t, :], x_res[:, t, :]).then_inc(stats_done, 1)
            for t in range(tiles):
                if x_loaded:
                    dve.wait_ge(stats_done, t + 1)
                dve.bn_aggr(mean_var[:, t, :], stats[:, t, :]).then_inc(mean_done, 1)
            dve.wait_ge(mean_done, tiles)
            dve.tensor_scalar(var_eps[:, :], mean_var[:, :, 1], eps, None, ALU.add).then_inc(var_done, 1)
            dve.wait_ge(deviation_done, 1)
            dve.reciprocal(inverse[:, :], deviation[:, :]).then_inc(inverse_done, 1)
            dve.wait_ge(inverse_done, 1)
            dve.scalar_tensor_tensor(shift[:, :], mean_var[:, :, 0], -1.0, inverse[:, :], ALU.mult, ALU.mult).then_inc(shift_done, 1)
            for t in range(0, tiles, 2):
                dve.tensor_scalar(xn[:, t, :], x_res[:, t, :], mean_var[:, t, 0:1], inverse[:, t:t + 1],
                                  ALU.subtract, ALU.mult).then_inc(normed, 1)

        @block.scalar
        def _(act):
            act.wait_ge(var_done, 1)
            act.activation(deviation[:, :], var_eps[:, :], ACT.Sqrt).then_inc(deviation_done, 1)
            act.wait_ge(shift_done, 1)
            for t in range(1, tiles, 2):
                act.activation(xn[:, t, :], x_res[:, t, :], ACT.Identity, scale=inverse[:, t:t + 1],
                               bias=shift[:, t:t + 1]).then_inc(normed, 1)


def grouped_attention_block(nc, held, x, ctx_in, wq, wk, wv, wo, x_res, xn, stats, ident, ones):
    B, CTX, D = ctx_in.shape
    TOK = x_res.shape[1] * P // B
    QT = TOK // P
    DC = D // P
    HD = P
    KVH = wk.shape[1] // HD
    HPG = wq.shape[1] // HD // KVH
    KEYS = TOK + CTX
    WIDTH = KEYS + KEYS % 2
    KT = -(-KEYS // P)
    LAST = KEYS - (KT - 1) * P
    PAIRS = -(-KT // 2)
    BANK = 512
    CHUNKS = [(c, min(BANK, WIDTH - c)) for c in range(0, WIDTH, BANK)]
    HALVES = [(0, 2 * BANK), (2 * BANK, KEYS)]
    FIRST_PAIRS = 2 * BANK // (2 * P)
    LAT = TOK // P
    STAGES = 3
    SCALE = 1.0 / math.sqrt(HD)
    VG = -(-KT // 4)
    VPIECES = [(4 * q, 4, P) for q in range(VG - 1)] + [(4 * (VG - 1), KT - 1 - 4 * (VG - 1), P), (KT - 1, 1, LAST)]
    rows_of = lambda k: LAST if k == KT - 1 else P
    assert QT == 2 and len(CHUNKS) == 4 and HPG == 8 and KT % STAGES == 0 and KT - 1 - 4 * (VG - 1) > 0

    with ExitStack() as ctx:
        sb = lambda n, s, d=F32: ctx.enter_context(nc.sbuf_tensor(f"a_{n}", s, d))
        sem = lambda n: new_semaphore(nc, held, f"a_{n}")
        stage = [sb(f"stage{i}", [P, D]) for i in range(STAGES)]
        hid_hi, hid_lo = sb("hid_hi", [P, DC, WIDTH], F32R), sb("hid_lo", [P, DC, WIDTH], F32R)
        k_hi, k_lo = sb("k_hi", [P, WIDTH], F32R), sb("k_lo", [P, WIDTH], F32R)
        v_hi, v_lo = sb("v_hi", [P, KT, HD], F32R), sb("v_lo", [P, KT, HD], F32R)
        probs = [[sb(f"probs{a}{j}", [P, WIDTH]) for j in range(QT)] for a in range(2)]
        v_t = probs[1][1]
        pt_hi, pt_lo = sb("pt_hi", [P, 2, 2, TOK], F32R), sb("pt_lo", [P, 2, 2, TOK], F32R)
        q_hi, q_lo = [sb(f"q_hi{a}", [P, TOK], F32R) for a in range(2)], [sb(f"q_lo{a}", [P, TOK], F32R) for a in range(2)]
        wkv_raw = sb("wkv_raw", [P, 2, DC, HD])
        wkv_hi, wkv_lo = sb("wkv_hi", [P, 2, DC, HD], F32R), sb("wkv_lo", [P, 2, DC, HD], F32R)
        wq_raw, wo_raw = sb("wq_raw", [P, DC, HD]), sb("wo_raw", [P, D])
        wq_hi = [sb(f"wq_hi{a}", [P, DC, HD], F32R) for a in range(2)]
        wq_lo = [sb(f"wq_lo{a}", [P, DC, HD], F32R) for a in range(2)]
        wo_hi = [sb(f"wo_hi{a}", [P, D], F32R) for a in range(2)]
        wo_lo = [sb(f"wo_lo{a}", [P, D], F32R) for a in range(2)]
        o_hi, o_lo = sb("o_hi", [P, TOK], F32R), sb("o_lo", [P, TOK], F32R)
        half_max, neg_max = sb("half_max", [P, 2]), sb("neg_max", [P, QT])
        half_sum, row_sum, row_inv = sb("half_sum", [P, 2, QT, 2]), sb("row_sum", [P, QT]), sb("row_inv", [P, 2, QT])

        ps_s = ctx.enter_context(nc.psum_tensor("a_ps_s", [P, 4, BANK], F32))
        ps_t = ctx.enter_context(nc.psum_tensor("a_ps_t", [P, 2, BANK], F32))
        ps_o = ctx.enter_context(nc.psum_tensor("a_ps_o", [P, BANK], F32))
        ps_m = ctx.enter_context(nc.psum_tensor("a_ps_m", [P, BANK], F32))
        s_flat = ps_s[:, :, :].rearrange("p c n -> p (c n)")

        pad_zeroed = sem("pad_zeroed")
        stage_loaded = [sem(f"stage_loaded{i}") for i in range(STAGES)]
        stage_copied, hid_ps, hid_hi_done, hid_done = sem("stage_copied"), sem("hid_ps"), sem("hid_hi_done"), sem("hid_done")
        wkv_loaded, wkv_hi_done, wkv_ready = sem("wkv_loaded"), sem("wkv_hi_done"), sem("wkv_ready")
        wq_loaded, wq_hi_done, wq_ready = sem("wq_loaded"), sem("wq_hi_done"), sem("wq_ready")
        wo_loaded, wo_hi_done, wo_ready = sem("wo_loaded"), sem("wo_hi_done"), sem("wo_ready")
        kv_ps, k_hi_done, k_done, vt_done = sem("kv_ps"), sem("k_hi_done"), sem("k_done"), sem("vt_done")
        v_ps, v_hi_done, v_done = sem("v_ps"), sem("v_hi_done"), sem("v_done")
        q_ps, q_hi_done, q_done = sem("q_ps"), sem("q_hi_done"), sem("q_done")
        s_ps, max_done, neg_max_done, probs_done = sem("s_ps"), sem("max_done"), sem("neg_max_done"), sem("probs_done")
        sum_done, inv_done = sem("sum_done"), sem("inv_done")
        pt_ps, pt_hi_done, pt_done, pv_ps = sem("pt_ps"), sem("pt_hi_done"), sem("pt_done"), sem("pv_ps")
        o_hi_done, o_done = sem("o_hi_done"), sem("o_done")
        stats_done = sem("stats_done")
        wo_ps, wo_added = sem("wo_ps"), sem("wo_added")
        prime(nc, (wq_ready, wo_ready, wkv_ready, q_ps, wo_ps, kv_ps, hid_ps, o_done, wo_added, pt_done, pv_ps))
        norm_block(nc, held, x_res, xn, stats, 1e-5, "norm0", load_from=x, constants=(ident, ones))
        block = ctx.enter_context(nc.Block())

        wk_v = wk.rearrange("(c p) n -> p c n", p=P)
        wv_v = wv.rearrange("(c p) n -> p c n", p=P)
        wq_v = wq.rearrange("(c p) n -> p c n", p=P)

        @block.sync
        def _(sp):
            def load_wq(u, head):
                sp.wait_ge(wq_ready, PRIMED + u)
                sp.dma_start(wq_raw[:, :, :], wq_v[:, :, bass.ds(head * HD, HD)]).then_inc(wq_loaded, 16)

            def load_wo(u, head):
                sp.wait_ge(wo_ready, PRIMED + u)
                sp.dma_start(wo_raw[:, :], wo[bass.ds(head * HD, HD), :]).then_inc(wo_loaded, 16)

            def load_wkv(G, g):
                sp.wait_ge(wkv_ready, PRIMED + G)
                sp.dma_start(wkv_raw[:, 0, :, :], wk_v[:, :, bass.ds(g * HD, HD)]).then_inc(wkv_loaded, 16)
                sp.dma_start(wkv_raw[:, 1, :, :], wv_v[:, :, bass.ds(g * HD, HD)]).then_inc(wkv_loaded, 16)

            def load_context(i, b):
                for r in range(LAT, KT):
                    sp.wait_ge(hid_ps, PRIMED + KT * i + (r - STAGES + 1 if r >= STAGES else 0))
                    n = rows_of(r)
                    sp.dma_start(stage[r % STAGES][0:n, :], ctx_in[b, (r - LAT) * P:(r - LAT) * P + n, :]
                                 ).then_inc(stage_loaded[r % STAGES], 16)

            load_wkv(0, 0)
            load_wq(0, 0)
            load_context(0, 0)
            with sp.Fori(0, B) as b:
                with sp.Fori(0, KVH) as g:
                    G = b * KVH + g
                    u0 = G * HPG
                    with sp.Fori(0, HPG - 2) as h:
                        load_wq(u0 + h + 1, g * HPG + h + 1)
                        load_wo(u0 + h, g * HPG + h)
                    load_wq(u0 + HPG - 1, g * HPG + HPG - 1)
                    load_wkv(G + 1, (g + 1) % KVH)
                    load_wo(u0 + HPG - 2, g * HPG + HPG - 2)
                    load_wq(u0 + HPG, (g + 1) % KVH * HPG)
                    load_wo(u0 + HPG - 1, g * HPG + HPG - 1)
                load_context(b + 1, (b + 1) % B)

        @block.gpsimd
        def _(pool):
            pool.memset(hid_hi[:, :, KEYS:WIDTH].bitcast(F32), 0.0).then_inc(pad_zeroed, 1)
            pool.memset(hid_lo[:, :, KEYS:WIDTH].bitcast(F32), 0.0).then_inc(pad_zeroed, 1)

            def split(hi, lo, raw, hi_done, ready, n):
                pool.tensor_tensor(hi, raw, ones[:, 0:1].to_broadcast(raw.shape), ALU.mult).then_inc(hi_done, 1)
                pool.wait_ge(hi_done, n + 1)
                pool.tensor_tensor(lo, raw, hi.bitcast(F32), ALU.subtract).then_inc(ready, 1)

            def flat(w):
                return w[:].rearrange("p c n -> p (c n)" if len(w.shape) == 3 else "p a c n -> p (a c n)")

            def split_wq(u, a, free):
                pool.wait_ge(wq_loaded, 16 * (u + 1))
                pool.wait_ge(q_ps, PRIMED + free)
                split(flat(wq_hi[a]), flat(wq_lo[a]), flat(wq_raw), wq_hi_done, wq_ready, u)

            def split_wo(u, a, free):
                pool.wait_ge(wo_loaded, 16 * (u + 1))
                pool.wait_ge(wo_ps, PRIMED + QT * free)
                split(wo_hi[a][:, :], wo_lo[a][:, :], wo_raw[:, :], wo_hi_done, wo_ready, u)

            def split_wkv(G):
                pool.wait_ge(wkv_loaded, 32 * (G + 1))
                pool.wait_ge(kv_ps, PRIMED + 8 * G)
                split(flat(wkv_hi), flat(wkv_lo), flat(wkv_raw), wkv_hi_done, wkv_ready, G)

            def copy_latents(i, b):
                for r in range(LAT):
                    pool.wait_ge(hid_ps, PRIMED + KT * i)
                    pool.tensor_tensor(stage[r][:, :], xn[:, bass.ds(QT * b + r, 1), :].rearrange("p a d -> p (a d)"),
                                       ones[:, 0:1].to_broadcast([P, D]), ALU.mult).then_inc(stage_copied, 1)

            copy_latents(0, 0)
            split_wkv(0)
            split_wq(0, 0, 0)
            with pool.Fori(0, B) as b:
                copy_latents(b + 1, (b + 1) % B)
                with pool.Fori(0, KVH) as g:
                    G = b * KVH + g
                    u0 = G * HPG
                    split_wq(u0 + 1, 1, u0)
                    split_wo(u0, 0, u0)
                    split_wq(u0 + 2, 0, u0 + 1)
                    split_wo(u0 + 1, 1, u0)
                    with pool.Fori(0, HPG // 2 - 2) as i:
                        for a in range(2):
                            u = u0 + 2 * i + 2 + a
                            split_wq(u + 1, 1 - a, u)
                            split_wo(u, a, u - 1)
                    split_wq(u0 + 7, 1, u0 + 6)
                    split_wkv(G + 1)
                    split_wo(u0 + 6, 0, u0 + 5)
                    split_wq(u0 + 8, 0, u0 + 7)
                    split_wo(u0 + 7, 1, u0 + 6)

        @block.tensor
        def _(pe):
            def three(out, w_hi, w_lo, m_hi, m_lo, first, last):
                pe.matmul(out, w_hi, m_hi, start=first, stop=False)
                pe.matmul(out, w_hi, m_lo, start=False, stop=False)
                return pe.matmul(out, w_lo, m_hi, start=False, stop=last)

            def project(out, w_hi, w_lo, c0, n, lo=0, hi=DC):
                for c in range(lo, hi):
                    mm = three(out, w_hi[:, c, :], w_lo[:, c, :], hid_hi[:, c, c0:c0 + n], hid_lo[:, c, c0:c0 + n],
                               c == 0, c == DC - 1)
                return mm

            def queries(u, a, part=None):
                if part != 1:
                    pe.wait_ge(wq_ready, PRIMED + u + 1)
                lo, hi = (0, DC) if part is None else (part * DC // 2, (part + 1) * DC // 2)
                mm = project(ps_m[:, 0:TOK], wq_hi[a], wq_lo[a], 0, TOK, lo, hi)
                if hi == DC:
                    mm.then_inc(q_ps, 1)

            def scores(u, a, j, first, halves=(0, 1)):
                if j == 0:
                    pe.wait_ge(q_done, u + 1)
                for half in halves:
                    if not first:
                        pe.wait_ge(probs_done, 4 * u + 2 * j + half - 1)
                    for c in (2 * half, 2 * half + 1):
                        c0, n = CHUNKS[c]
                        mm = three(ps_s[:, c, 0:n], q_hi[a][:, P * j:P * j + P], q_lo[a][:, P * j:P * j + P],
                                   k_hi[:, c0:c0 + n], k_lo[:, c0:c0 + n], True, True)
                    mm.then_inc(s_ps, 1)

            def transpose_probs(v, a, p, first):
                if p == 0:
                    pe.wait_ge(probs_done, 4 * v + 3)
                elif p == FIRST_PAIRS:
                    pe.wait_ge(probs_done, 4 * (v + 1))
                if not (first and p < 2):
                    pe.wait_ge(pt_done, PRIMED + PAIRS * v + p - 1)
                for k in range(2 * p, min(2 * p + 2, KT)):
                    n = rows_of(k)
                    for j in range(QT):
                        at = (k % 2) * TOK + j * P
                        tr = pe.transpose(ps_t[0:n, p % 2, at:at + P], probs[a][j][:, k * P:k * P + n], ident[:, :])
                tr.then_inc(pt_ps, 1)

            def weigh_values(v, p):
                pe.wait_ge(pt_done, PRIMED + PAIRS * v + p + 1)
                if p == 0:
                    pe.wait_ge(o_done, PRIMED + v)
                for k in range(2 * p, min(2 * p + 2, KT)):
                    n = rows_of(k)
                    mm = three(ps_o[:, 0:TOK], v_hi[0:n, k, :], v_lo[0:n, k, :], pt_hi[0:n, p % 2, k % 2, :],
                               pt_lo[0:n, p % 2, k % 2, :], k == 0, k == KT - 1)
                mm.then_inc(pv_ps, 1)

            def output(w, a, j):
                if j == 0:
                    pe.wait_ge(o_done, PRIMED + w + 1)
                    pe.wait_ge(wo_ready, PRIMED + w + 1)
                else:
                    pe.wait_ge(wo_added, PRIMED + QT * w + 1)
                three(ps_m[:, :], o_hi[:, P * j:P * j + P], o_lo[:, P * j:P * j + P], wo_hi[a][:, :], wo_lo[a][:, :],
                      True, True).then_inc(wo_ps, 1)

            def step(u, a, out, ahead, first_pv=False):
                v = u - 1
                transpose_probs(v, 1 - a, 0, first_pv)
                transpose_probs(v, 1 - a, 1, first_pv)
                scores(u, a, 0, False)
                weigh_values(v, 0)
                transpose_probs(v, 1 - a, 2, False)
                if out:
                    output(u - 2, a, 0)
                weigh_values(v, 1)
                transpose_probs(v, 1 - a, 3, False)
                weigh_values(v, 2)
                scores(u, a, 1, False, (0,))
                transpose_probs(v, 1 - a, 4, False)
                weigh_values(v, 3)
                scores(u, a, 1, False, (1,))
                transpose_probs(v, 1 - a, 5, False)
                if out:
                    output(u - 2, a, 1)
                weigh_values(v, 4)
                transpose_probs(v, 1 - a, 6, False)
                if ahead:
                    if out:
                        pe.wait_ge(wo_added, PRIMED + QT * (u - 1))
                    queries(u + 1, 1 - a, 0)
                weigh_values(v, 5)
                transpose_probs(v, 1 - a, 7, False)
                if ahead:
                    queries(u + 1, 1 - a, 1)
                weigh_values(v, 6)
                weigh_values(v, 7)

            def transpose_inputs(i, r):
                st, n = r % STAGES, rows_of(r)
                if r < LAT:
                    pe.wait_ge(stage_copied, LAT * i + r + 1)
                else:
                    loads = [q for q in range(LAT, KT) if q % STAGES == st]
                    pe.wait_ge(stage_loaded[st], 16 * (len(loads) * i + loads.index(r) + 1))
                if r >= 4:
                    pe.wait_ge(hid_done, KT * i + r - 3)
                for c in range(DC):
                    tr = pe.transpose(ps_s[:, r % 4, c * P:c * P + n], stage[st][0:n, c * P:(c + 1) * P], ident[0:n, 0:n])
                tr.then_inc(hid_ps, 1)

            def keys(G, c):
                c0, n = CHUNKS[c]
                if c == 0:
                    pe.wait_ge(wkv_ready, PRIMED + G + 1)
                project(ps_s[:, c, 0:n], wkv_hi[:, 0], wkv_lo[:, 0], c0, n).then_inc(kv_ps, 1)

            def values(G, c):
                c0, n = CHUNKS[c]
                if c == 0:
                    pe.wait_ge(o_done, PRIMED + HPG * G)
                elif c == 1:
                    pe.wait_ge(wo_added, PRIMED + QT * HPG * G)
                else:
                    pe.wait_ge(vt_done, 4 * G + c - 1)
                bank = ps_m if c % 2 else ps_o
                project(bank[:, 0:n], wkv_hi[:, 1], wkv_lo[:, 1], c0, n).then_inc(kv_ps, 1)

            def transpose_values(G, q):
                pe.wait_ge(vt_done, 4 * G + q + 1)
                if q >= 2:
                    pe.wait_ge(v_done, len(VPIECES) * G + q - 1)
                else:
                    pe.wait_ge(pt_done, PRIMED + PAIRS * HPG * G)
                for k in range(4 * q, min(4 * q + 4, KT)):
                    n = rows_of(k)
                    tr = pe.transpose(ps_t[0:n, q % 2, (k % 4) * P:(k % 4 + 1) * P], v_t[:, k * P:k * P + n], ident[:, :])
                tr.then_inc(v_ps, 1)

            def first_step(G, out):
                u0 = G * HPG
                pe.wait_ge(k_done, 4 * (G + 1))
                scores(u0, 0, 0, True)
                if out:
                    output(u0 - 1, 1, 0)
                values(G, 0)
                if out:
                    output(u0 - 1, 1, 1)
                scores(u0, 0, 1, False)
                values(G, 1)
                values(G, 2)
                transpose_values(G, 0)
                transpose_values(G, 1)
                values(G, 3)
                transpose_values(G, 2)
                pe.wait_ge(vt_done, 4 * (G + 1))
                queries(u0 + 1, 1)
                transpose_values(G, 3)

            def group(G):
                u0 = G * HPG
                pe.wait_ge(v_done, len(VPIECES) * (G + 1))
                step(u0 + 1, 1, False, True, first_pv=True)
                with pe.Fori(0, HPG // 2 - 2) as i:
                    step(u0 + 2 * i + 2, 0, True, True)
                    step(u0 + 2 * i + 3, 1, True, True)
                step(u0 + 6, 0, True, True)
                step(u0 + 7, 1, True, False)

            def last_step(G, i, to_next_group):
                u = G * HPG + HPG
                v = u - 1

                def meanwhile(n):
                    if n == 1:
                        pe.wait_ge(probs_done, 4 * (v + 1))
                    if to_next_group:
                        if n % 2 == 0:
                            keys(G + 1, n // 2)
                    else:
                        for r in range(2 * n, min(2 * n + 2, KT)):
                            transpose_inputs(i, r)

                transpose_probs(v, 1, 0, False)
                transpose_probs(v, 1, 1, False)
                meanwhile(0)
                weigh_values(v, 0)
                transpose_probs(v, 1, 2, False)
                output(u - 2, 0, 0)
                meanwhile(1)
                weigh_values(v, 1)
                transpose_probs(v, 1, 3, False)
                meanwhile(2)
                output(u - 2, 0, 1)
                weigh_values(v, 2)
                transpose_probs(v, 1, 4, False)
                meanwhile(3)
                weigh_values(v, 3)
                transpose_probs(v, 1, 5, False)
                meanwhile(4)
                weigh_values(v, 4)
                transpose_probs(v, 1, 6, False)
                meanwhile(5)
                weigh_values(v, 5)
                transpose_probs(v, 1, 7, False)
                meanwhile(6)
                if to_next_group:
                    pe.wait_ge(wo_added, PRIMED + QT * (u - 1))
                    queries(u, 0)
                weigh_values(v, 6)
                weigh_values(v, 7)
                meanwhile(7)

            for r in range(KT):
                transpose_inputs(0, r)
            pe.wait_ge(pad_zeroed, 2)
            with pe.Fori(0, B) as b:
                G0 = b * KVH
                for c in range(4):
                    if c == 0:
                        pe.wait_ge(hid_done, KT * (b + 1))
                    keys(G0, c)
                pe.wait_ge(wo_added, PRIMED + QT * HPG * G0)
                queries(G0 * HPG, 0)
                first_step(G0, False)
                with pe.Fori(0, KVH - 1) as g:
                    G = b * KVH + g
                    group(G)
                    last_step(G, None, True)
                    first_step(G + 1, True)
                G = b * KVH + (KVH - 1)
                group(G)
                last_step(G, b + 1, False)
                output(G * HPG + HPG - 1, 1, 0)
                output(G * HPG + HPG - 1, 1, 1)

        @block.scalar
        def _(act):
            def probs_hi(v, p):
                act.wait_ge(pt_ps, PAIRS * v + p + 1)
                full = 2 if 2 * p + 2 < KT else 1
                n = P if full == 2 else LAST
                if p >= 2:
                    act.wait_ge(pv_ps, PRIMED + PAIRS * v + p - 1)
                else:
                    act.wait_ge(pv_ps, PRIMED + PAIRS * v)
                act.activation(pt_hi[0:n, p % 2, 0:full, :],
                               ps_t[0:n, p % 2, 0:full * TOK].rearrange("p (k q) -> p k q", k=full),
                               ACT.Copy).then_inc(pt_hi_done, 1)

            def exponentials(u, a, j, half):
                act.wait_ge(neg_max_done, QT * u + j + 1)
                lo, hi = HALVES[half]
                act.activation(probs[a][j][:, lo:hi], s_flat[:, lo:hi], ACT.Exp, bias=neg_max[:, j:j + 1], scale=SCALE,
                               accum_out=half_sum[:, a, j, half:half + 1]).then_inc(probs_done, 1)

            def queries_hi(u, a):
                act.wait_ge(q_ps, PRIMED + u + 1)
                act.activation(q_hi[a][:, :], ps_m[:, 0:TOK], ACT.Copy).then_inc(q_hi_done, 1)

            def output_hi(w):
                act.wait_ge(pv_ps, PRIMED + PAIRS * (w + 1))
                act.wait_ge(wo_ps, PRIMED + QT * w)
                act.activation(o_hi[:, :], ps_o[:, 0:TOK], ACT.Copy).then_inc(o_hi_done, 1)

            def step(u, a, out, ahead):
                v = u - 1
                if out:
                    output_hi(u - 2)
                probs_hi(v, 0)
                probs_hi(v, 1)
                probs_hi(v, 2)
                exponentials(u, a, 0, 0)
                probs_hi(v, 3)
                exponentials(u, a, 0, 1)
                probs_hi(v, 4)
                probs_hi(v, 5)
                exponentials(u, a, 1, 0)
                probs_hi(v, 6)
                exponentials(u, a, 1, 1)
                probs_hi(v, 7)
                if ahead:
                    queries_hi(u + 1, 1 - a)

            def inputs_hi(i, r):
                n = rows_of(r)
                act.wait_ge(hid_ps, PRIMED + KT * i + r + 1)
                act.activation(hid_hi[:, :, r * P:r * P + n],
                               ps_s[:, r % 4, :].rearrange("p (c n) -> p c n", c=DC)[:, :, 0:n],
                               ACT.Copy).then_inc(hid_hi_done, 1)

            def keys_hi(G, c):
                c0, n = CHUNKS[c]
                act.wait_ge(kv_ps, PRIMED + 8 * G + c + 1)
                act.activation(k_hi[:, c0:c0 + n], ps_s[:, c, 0:n], ACT.Copy).then_inc(k_hi_done, 1)

            def values_out(G, c):
                c0, n = CHUNKS[c]
                act.wait_ge(kv_ps, PRIMED + 8 * G + 4 + c + 1)
                act.activation(v_t[:, c0:c0 + n], (ps_m if c % 2 else ps_o)[:, 0:n], ACT.Copy).then_inc(vt_done, 1)

            def values_hi(G, i):
                k, m, n = VPIECES[i]
                act.wait_ge(v_ps, VG * G + min(i, VG - 1) + 1)
                act.activation(v_hi[0:n, k:k + m, :],
                               ps_t[0:n, k // 4 % 2, (k % 4) * P:(k % 4 + m) * P].rearrange("p (k d) -> p k d", k=m),
                               ACT.Copy).then_inc(v_hi_done, 1)

            def first_step(G):
                u0 = G * HPG
                exponentials(u0, 0, 0, 0)
                exponentials(u0, 0, 0, 1)
                values_out(G, 0)
                values_out(G, 1)
                exponentials(u0, 0, 1, 0)
                exponentials(u0, 0, 1, 1)
                values_out(G, 2)
                values_hi(G, 0)
                values_hi(G, 1)
                values_out(G, 3)
                values_hi(G, 2)
                queries_hi(u0 + 1, 1)
                for i in range(3, len(VPIECES)):
                    values_hi(G, i)

            def group(G):
                u0 = G * HPG
                step(u0 + 1, 1, False, True)
                with act.Fori(0, HPG // 2 - 2) as i:
                    step(u0 + 2 * i + 2, 0, True, True)
                    step(u0 + 2 * i + 3, 1, True, True)
                step(u0 + 6, 0, True, True)
                step(u0 + 7, 1, True, False)

            def last_step(G, i, to_next_group):
                u = G * HPG + HPG
                v = u - 1

                def meanwhile(n):
                    if to_next_group:
                        if n % 2 == 0:
                            keys_hi(G + 1, n // 2)
                    else:
                        for r in range(2 * n, min(2 * n + 2, KT)):
                            inputs_hi(i, r)

                output_hi(u - 2)
                probs_hi(v, 0)
                probs_hi(v, 1)
                meanwhile(0)
                for p in range(2, PAIRS):
                    probs_hi(v, p)
                    meanwhile(p - 1)
                if to_next_group:
                    queries_hi(u, 0)
                meanwhile(PAIRS - 1)
                output_hi(v)

            for r in range(KT):
                inputs_hi(0, r)
            with act.Fori(0, B) as b:
                G0 = b * KVH
                for c in range(4):
                    keys_hi(G0, c)
                queries_hi(G0 * HPG, 0)
                first_step(G0)
                with act.Fori(0, KVH - 1) as g:
                    G = b * KVH + g
                    group(G)
                    last_step(G, None, True)
                    first_step(G + 1)
                G = b * KVH + (KVH - 1)
                group(G)
                last_step(G, b + 1, False)

        @block.vector
        def _(dve):
            def probs_lo(v, p):
                full = 2 if 2 * p + 2 < KT else 1
                n = P if full == 2 else LAST
                dve.wait_ge(pt_hi_done, PAIRS * v + p + 1)
                dve.tensor_tensor(pt_lo[0:n, p % 2, 0:full, :],
                                  ps_t[0:n, p % 2, 0:full * TOK].rearrange("p (k q) -> p k q", k=full),
                                  pt_hi[0:n, p % 2, 0:full, :].bitcast(F32), ALU.subtract).then_inc(pt_done, 1)

            def maximum(u, j, half):
                lo, hi = HALVES[half]
                dve.wait_ge(s_ps, 4 * u + 2 * j + half + 1)
                dve.reduce_max(half_max[:, half:half + 1], s_flat[:, lo:hi], AX.X).then_inc(max_done, 1)

            def negate_maximum(u, j):
                dve.wait_ge(max_done, 4 * u + 2 * j + 2)
                dve.tensor_scalar(neg_max[:, j:j + 1], half_max[:, 0:1], half_max[:, 1:2], -SCALE, ALU.max,
                                  ALU.mult).then_inc(neg_max_done, 1)

            def maxima(u, j):
                maximum(u, j, 0)
                maximum(u, j, 1)
                negate_maximum(u, j)

            def queries_lo(u, a):
                dve.wait_ge(q_hi_done, u + 1)
                dve.tensor_tensor(q_lo[a][:, :], ps_m[:, 0:TOK], q_hi[a][:, :].bitcast(F32), ALU.subtract).then_inc(q_done, 1)

            def inverse_sums(v, a):
                dve.wait_ge(probs_done, 4 * (v + 1))
                dve.tensor_tensor(row_sum[:, :], half_sum[:, a, :, 0], half_sum[:, a, :, 1], ALU.add).then_inc(sum_done, 1)
                dve.wait_ge(sum_done, v + 1)
                dve.reciprocal(row_inv[:, a, :], row_sum[:, :]).then_inc(inv_done, 1)

            def output_lo(w):
                dve.wait_ge(o_hi_done, w + 1)
                dve.tensor_tensor(o_lo[:, :], ps_o[:, 0:TOK], o_hi[:, :].bitcast(F32), ALU.subtract).then_inc(o_done, 1)

            def add_output(w, a, j, tile):
                x_tile = x_res[:, bass.ds(tile, 1), :].rearrange("p a d -> p (a d)")
                dve.wait_ge(wo_ps, PRIMED + QT * w + j + 1)
                dve.wait_ge(wo_added, PRIMED + QT * w + j)
                dve.wait_ge(inv_done, w + 1)
                dve.scalar_tensor_tensor(x_tile, ps_m[:, :], row_inv[:, a, j:j + 1], x_tile, ALU.mult, ALU.add).then_inc(wo_added, 1)

            def step(u, a, tile, out, ahead):
                v = u - 1
                if out:
                    output_lo(u - 2)
                inverse_sums(v, 1 - a)
                probs_lo(v, 0)
                probs_lo(v, 1)
                maximum(u, 0, 0)
                maximum(u, 0, 1)
                negate_maximum(u, 0)
                probs_lo(v, 2)
                if out:
                    add_output(u - 2, a, 0, tile)
                probs_lo(v, 3)
                maximum(u, 1, 0)
                probs_lo(v, 4)
                maximum(u, 1, 1)
                negate_maximum(u, 1)
                if out:
                    add_output(u - 2, a, 1, tile + 1)
                probs_lo(v, 5)
                probs_lo(v, 6)
                probs_lo(v, 7)
                if ahead:
                    queries_lo(u + 1, 1 - a)

            def inputs_lo(i, r):
                n = rows_of(r)
                dve.wait_ge(hid_hi_done, KT * i + r + 1)
                dve.tensor_tensor(hid_lo[:, :, r * P:r * P + n],
                                  ps_s[:, r % 4, :].rearrange("p (c n) -> p c n", c=DC)[:, :, 0:n],
                                  hid_hi[:, :, r * P:r * P + n].bitcast(F32), ALU.subtract).then_inc(hid_done, 1)

            def keys_lo(G, c):
                c0, n = CHUNKS[c]
                dve.wait_ge(k_hi_done, 4 * G + c + 1)
                dve.tensor_tensor(k_lo[:, c0:c0 + n], ps_s[:, c, 0:n], k_hi[:, c0:c0 + n].bitcast(F32),
                                  ALU.subtract).then_inc(k_done, 1)

            def values_lo(G, i):
                k, m, n = VPIECES[i]
                dve.wait_ge(v_hi_done, len(VPIECES) * G + (i + 1 if i < VG - 1 else VG + 1))
                dve.tensor_tensor(v_lo[0:n, k:k + m, :],
                                  ps_t[0:n, k // 4 % 2, (k % 4) * P:(k % 4 + m) * P].rearrange("p (k d) -> p k d", k=m),
                                  v_hi[0:n, k:k + m, :].bitcast(F32), ALU.subtract).then_inc(v_done, 1)

            def first_step(G, tile, out):
                u0 = G * HPG
                if out:
                    output_lo(u0 - 1)
                maxima(u0, 0)
                if out:
                    add_output(u0 - 1, 1, 0, tile)
                    add_output(u0 - 1, 1, 1, tile + 1)
                maxima(u0, 1)
                for i in range(3):
                    values_lo(G, i)
                queries_lo(u0 + 1, 1)
                for i in range(3, len(VPIECES)):
                    values_lo(G, i)

            def group(G, tile):
                u0 = G * HPG
                step(u0 + 1, 1, tile, False, True)
                with dve.Fori(0, HPG // 2 - 2) as i:
                    step(u0 + 2 * i + 2, 0, tile, True, True)
                    step(u0 + 2 * i + 3, 1, tile, True, True)
                step(u0 + 6, 0, tile, True, True)
                step(u0 + 7, 1, tile, True, False)

            def last_step(G, tile, i, to_next_group):
                u = G * HPG + HPG
                v = u - 1

                def meanwhile(n):
                    if to_next_group:
                        if n % 2 == 0:
                            keys_lo(G + 1, n // 2)
                    else:
                        for r in range(2 * n, min(2 * n + 2, KT)):
                            inputs_lo(i, r)

                output_lo(u - 2)
                inverse_sums(v, 1)
                probs_lo(v, 0)
                probs_lo(v, 1)
                meanwhile(0)
                add_output(u - 2, 0, 0, tile)
                probs_lo(v, 2)
                meanwhile(1)
                probs_lo(v, 3)
                meanwhile(2)
                add_output(u - 2, 0, 1, tile + 1)
                for p in range(4, PAIRS):
                    probs_lo(v, p)
                    meanwhile(p - 1)
                if to_next_group:
                    queries_lo(u, 0)
                if not to_next_group:
                    meanwhile(PAIRS - 1)
                    output_lo(v)
                    add_output(v, 1, 0, tile)
                    add_output(v, 1, 1, tile + 1)

            for r in range(KT):
                inputs_lo(0, r)
            with dve.Fori(0, B) as b:
                G0 = b * KVH
                for c in range(4):
                    keys_lo(G0, c)
                queries_lo(G0 * HPG, 0)
                first_step(G0, QT * b, False)
                with dve.Fori(0, KVH - 1) as g:
                    G = b * KVH + g
                    group(G, QT * b)
                    last_step(G, QT * b, None, True)
                    first_step(G + 1, QT * b, True)
                G = b * KVH + (KVH - 1)
                group(G, QT * b)
                last_step(G, QT * b, b + 1, False)
                for j in range(QT):
                    x_tile = x_res[:, bass.ds(QT * b + j, 1), :].rearrange("p a d -> p (a d)")
                    dve.wait_ge(wo_added, PRIMED + QT * HPG * (G + 1))
                    tile_statistics(dve, stats, x_tile, QT * b + j, stats_done)


class Chain:

    def __init__(self, engine, semaphore):
        self.engine, self.semaphore, self.count = engine, semaphore, 0

    def link(self, instruction):
        self.count += 1
        instruction.then_inc(self.semaphore, 1)
        self.engine.wait_ge(self.semaphore, self.count)


def wide(x, n):
    return x.unsqueeze(2).to_broadcast([x.shape[0], x.shape[1], n])


def softmax_rows(dve, chain, scores, logits, row, row2, exp_wait, max_done):
    E = logits.shape[2]
    chain.link(dve.reduce_max(row, logits, AX.X))
    dve.tensor_tensor(scores, logits, wide(row, E), ALU.subtract).then_inc(max_done, 1)
    dve.wait_ge(exp_wait, 1)
    chain.link(dve.reduce_sum(row, scores, AX.X))
    chain.link(dve.reciprocal(row2, row))
    chain.link(dve.tensor_tensor(scores, scores, wide(row2, E), ALU.mult))


def top_two(dve, chain, scores, ramp, hit, first, second, rest, row, best, runner):
    E, tiles = scores.shape[2], scores.shape[1]
    ramps = ramp.unsqueeze(1).to_broadcast([P, tiles, E])
    for values, value, one_hot in ((scores, best, first), (rest, runner, second)):
        chain.link(dve.reduce_max(value, values, AX.X))
        chain.link(dve.tensor_tensor(hit, values, wide(value, E), ALU.is_equal))
        chain.link(dve.tensor_tensor(hit, hit, ramps, ALU.mult))
        chain.link(dve.reduce_max(row, hit, AX.X))
        chain.link(dve.tensor_tensor(one_hot, hit, wide(row, E), ALU.is_equal))
        if values is scores:
            chain.link(dve.scalar_tensor_tensor(rest, first, -4.0, scores, ALU.mult, ALU.add))


def gated_experts_block(nc, held, gate_w, gate_b, w1, b1, w2, b2, x_res, xn, stats, ident, ones, batches):
    TILES, D = x_res.shape[1], x_res.shape[2]
    E, _, F = w1.shape
    DC, FC = D // P, F // P
    TPB = TILES // batches
    VISION = int(TPB * P * 0.3)
    EW = E + E % 2
    BANK = 512
    TC = TILES * P // BANK
    TPC = BANK // P
    STEPS = TC * FC
    PIECES = DC + FC
    FUNCTIONS = (ACT.Tanh, ACT.Gelu, ACT.Silu)
    assert E == len(FUNCTIONS) and TPB == 2 and VISION <= P and PIECES == STEPS and D == BANK and F == BANK

    with ExitStack() as ctx:
        sb = lambda n, s, d=F32: ctx.enter_context(nc.sbuf_tensor(f"b_{n}", s, d))
        sem = lambda n: new_semaphore(nc, held, f"b_{n}")
        xt_hi, xt_lo = sb("xt_hi", [P, DC, TILES * P], F32R), sb("xt_lo", [P, DC, TILES * P], F32R)
        w1_raw, w2_raw = sb("w1_raw", [P, DC, F]), sb("w2_raw", [P, FC, D])
        w1_hi = [sb(f"w1_hi{a}", [P, DC, F], F32R) for a in range(2)]
        w1_lo = [sb(f"w1_lo{a}", [P, DC, F], F32R) for a in range(2)]
        w2_hi = [sb(f"w2_hi{a}", [P, FC, D], F32R) for a in range(2)]
        w2_lo = [sb(f"w2_lo{a}", [P, FC, D], F32R) for a in range(2)]
        hidden = [sb(f"hidden{i}", [P, BANK]) for i in range(2)]
        act_hi, act_lo = sb("act_hi", [P, FC, TILES * P], F32R), sb("act_lo", [P, FC, TILES * P], F32R)
        b1_rows, b1_cols = sb("b1_rows", [E * FC, P]), sb("b1_cols", [P, E, FC])
        b2_rows, biased = sb("b2_rows", [P, E, D]), sb("biased", [P, 2, D])
        gate_raw, gate_hi, gate_lo = sb("gate_raw", [P, DC, EW]), sb("gate_hi", [P, DC, EW], F32R), sb("gate_lo", [P, DC, EW], F32R)
        gate_rows = sb("gate_rows", [P, 2, E])
        vision, text = sb("vision", [P, P]), sb("text", [P, P])
        ramp = sb("ramp", [P, E])
        magnitudes, magnitude = sb("magnitudes", [P, D]), sb("magnitude", [P, TILES])
        strength, ratio = sb("strength", [P, batches]), sb("ratio", [P, batches])
        logits, scores = sb("logits", [P, TILES, E]), sb("scores", [P, TILES, E])
        hit, first, second, rest = (sb(n, [P, TILES, E]) for n in ("hit", "first", "second", "rest"))
        row, row2, best, runner = (sb(n, [P, TILES]) for n in ("row", "row2", "best", "runner"))
        chosen = sb("chosen", [1, batches, 2, E])
        part, share = rest, hit

        ps_t = ctx.enter_context(nc.psum_tensor("b_ps_t", [P, 2, BANK], F32))
        ps_h = ctx.enter_context(nc.psum_tensor("b_ps_h", [P, 2, BANK], F32))
        ps_y = ctx.enter_context(nc.psum_tensor("b_ps_y", [P, 2, BANK], F32))
        ps_r = ctx.enter_context(nc.psum_tensor("b_ps_r", [P, BANK], F32))
        ps_c = ctx.enter_context(nc.psum_tensor("b_ps_c", [P, BANK], F32))
        strengths = ps_c[:, 0:2 * batches].rearrange("p (k b) -> p k b", k=2)
        choices = ps_c[:, 0:batches * 2 * E].rearrange("p (b i e) -> p b i e", b=batches, i=2)

        small_loaded, gate_loaded = sem("small_loaded"), sem("gate_loaded")
        w1_loaded, w2_loaded, b2_loaded = sem("w1_loaded"), sem("w2_loaded"), [sem(f"b2_loaded{e}") for e in range(E)]
        masks_set, masks_done, pads_set = sem("masks_set"), sem("masks_done"), sem("pads_set")
        magnitude_done, strength_ps, gate_hi_done, gate_done = sem("magnitude_done"), sem("strength_ps"), sem("gate_hi_done"), sem("gate_done")
        b1_ps, b1_done = sem("b1_ps"), sem("b1_done")
        xt_ps, xt_hi_done, xt_done, logits_ps = sem("xt_ps"), sem("xt_hi_done"), sem("xt_done"), sem("logits_ps")
        logits_t_ps, logits_t_out = sem("logits_t_ps"), sem("logits_t_out")
        centred, exp_done, chosen_done, choices_ps = sem("centred"), sem("exp_done"), sem("chosen_done"), sem("choices_ps")
        w_hi_done, w_done = sem("w_hi_done"), sem("w_done")
        h_ps, hidden_done, act_hi_done, act_done = sem("h_ps"), sem("hidden_done"), sem("act_hi_done"), sem("act_done")
        stats_done = sem("stats_done")
        y_biased = sem("y_biased")
        y_ps, added, router = sem("y_ps"), sem("added"), sem("router")
        block = ctx.enter_context(nc.Block())

        @block.sync
        def _(sp):
            for e in range(E):
                if e:
                    sp.wait_ge(w_done, PIECES * e)
                sp.dma_start(w1_raw[:, :, :], w1[e].rearrange("(c p) f -> p c f", p=P)).then_inc(w1_loaded, 16)
                sp.dma_start(w2_raw[:, :, :], w2[e].rearrange("(c p) d -> p c d", p=P)).then_inc(w2_loaded, 16)
                if e == 0:
                    sp.dma_start(gate_raw[:, :, 0:E], gate_w[0:D, :].rearrange("(c p) e -> p c e", p=P)).then_inc(gate_loaded, 16)
                    sp.dma_start(gate_rows[:, 0, :], gate_w[D, :].partition_broadcast(P)).then_inc(small_loaded, 16)
                    sp.dma_start(gate_rows[:, 1, :], gate_b.partition_broadcast(P)).then_inc(small_loaded, 16)
                    sp.dma_start(b1_rows[:, :], b1.rearrange("e (c p) -> (e c) p", p=P)).then_inc(small_loaded, 16)
                sp.dma_start(b2_rows[:, e, :], b2[e].partition_broadcast(P)).then_inc(b2_loaded[e], 16)

        @block.gpsimd
        def _(pool):
            pool.memset(gate_raw[:, :, E:EW], 0.0).then_inc(pads_set, 1)
            pool.iota(ramp[:, :], pattern=[[-1, E]], base=E, channel_multiplier=0,
                      allow_small_or_imprecise_dtypes=True).then_inc(pads_set, 1)
            pool.memset(vision[:, :], 1.0).then_inc(masks_set, 1)
            pool.memset(text[:, :], 1.0).then_inc(masks_set, 1)
            pool.wait_ge(masks_set, 2)
            pool.affine_select(out=vision[:, :], in_=vision[:, :], compare_op=ALU.is_ge, fill=0.0,
                               base=VISION - 1, pattern=[[0, P]], channel_multiplier=-1).then_inc(masks_done, 1)
            pool.affine_select(out=text[:, :], in_=text[:, :], compare_op=ALU.is_ge, fill=0.0,
                               base=-VISION, pattern=[[0, P]], channel_multiplier=1).then_inc(masks_done, 1)

        @block.tensor
        def _(pe):
            def three(out, w_hi, w_lo, m_hi, m_lo, first, last):
                pe.matmul(out, w_hi, m_hi, start=first, stop=False)
                pe.matmul(out, w_hi, m_lo, start=False, stop=False)
                return pe.matmul(out, w_lo, m_hi, start=False, stop=last)

            for t in range(TILES):
                if t >= 2:
                    pe.wait_ge(xt_done, t - 1)
                for c in range(DC):
                    tr = pe.transpose(ps_t[:, t % 2, c * P:(c + 1) * P], xn[:, t, c * P:(c + 1) * P], ident[:, :])
                tr.then_inc(xt_ps, 1)
            pe.wait_ge(small_loaded, 48)
            pe.transpose(ps_h[:, 0, 0:E * FC], b1_rows[:, :], ident[0:E * FC, 0:E * FC]).then_inc(b1_ps, 1)
            pe.wait_ge(masks_done, 2)
            pe.wait_ge(magnitude_done, TILES)
            pe.matmul(strengths[:, 0, :], vision[:, :], magnitude[:, 0:TILES:TPB], start=True, stop=True)
            pe.matmul(strengths[:, 1, :], text[:, :], magnitude[:, 0:TILES:TPB], start=True, stop=False)
            pe.matmul(strengths[:, 1, :], ones[:, :], magnitude[:, 1:TILES:TPB], start=False, stop=True).then_inc(strength_ps, 1)
            pe.wait_ge(gate_done, 1)
            pe.wait_ge(xt_done, TILES)
            for tc in range(TC):
                for c in range(DC):
                    mm = three(ps_y[0:EW, tc, :], gate_hi[:, c, :], gate_lo[:, c, :], xt_hi[:, c, tc * BANK:(tc + 1) * BANK],
                               xt_lo[:, c, tc * BANK:(tc + 1) * BANK], c == 0, c == DC - 1)
                mm.then_inc(logits_t_ps, 1)
            pe.wait_ge(logits_t_out, TC)
            for t in range(TILES):
                tr = pe.transpose(ps_r[:, t * EW:(t + 1) * EW], hidden[t // TPC][0:EW, t % TPC * P:(t % TPC + 1) * P],
                                  ident[0:EW, 0:EW])
            tr.then_inc(logits_ps, 1)
            for e in range(E):
                a = e % 2
                pe.wait_ge(w_done, PIECES * e + DC)
                for s in range(STEPS):
                    tc, f, n = s // FC, s % FC, STEPS * e + s
                    if n == 0:
                        pe.wait_ge(b1_done, 1)
                    if n >= 2:
                        pe.wait_ge(hidden_done, n - 1)
                    for c in range(DC):
                        mm = three(ps_h[:, n % 2, :], w1_hi[a][:, c, f * P:(f + 1) * P], w1_lo[a][:, c, f * P:(f + 1) * P],
                                   xt_hi[:, c, tc * BANK:(tc + 1) * BANK], xt_lo[:, c, tc * BANK:(tc + 1) * BANK],
                                   c == 0, c == DC - 1)
                    mm.then_inc(h_ps, 1)
                if e == 0:
                    pe.wait_ge(chosen_done, 1)
                    pe.matmul(ps_c[:, 0:batches * 2 * E], ones[0:1, :], chosen[:, :, :, :].rearrange("p b i e -> p (b i e)"),
                              start=True, stop=True).then_inc(choices_ps, 1)
                pe.wait_ge(w_done, PIECES * (e + 1))
                for t in range(TILES):
                    n = TILES * e + t
                    if t % TPC == 0:
                        pe.wait_ge(act_done, STEPS * e + FC * (t // TPC + 1))
                    if n >= 2:
                        pe.wait_ge(y_biased, n - 1)
                    for f in range(FC):
                        mm = three(ps_y[:, n % 2, :], act_hi[:, f, t * P:(t + 1) * P], act_lo[:, f, t * P:(t + 1) * P],
                                   w2_hi[a][:, f, :], w2_lo[a][:, f, :], f == 0, f == FC - 1)
                    mm.then_inc(y_ps, 1)

        def weight_piece(e, i):
            a, c = e % 2, i % DC
            if i < DC:
                return w1_raw[:, c, :], w1_hi[a][:, c, :], w1_lo[a][:, c, :]
            return w2_raw[:, c, :], w2_hi[a][:, c, :], w2_lo[a][:, c, :]

        @block.scalar
        def _(act):
            def split_hi(e, i):
                raw, hi, _ = weight_piece(e, i)
                if i == 0:
                    act.wait_ge(w1_loaded, 16 * (e + 1))
                if i == DC:
                    act.wait_ge(w2_loaded, 16 * (e + 1))
                if e >= 2 and i == 0:
                    act.wait_ge(y_ps, TILES * (e - 1))
                act.activation(hi, raw, ACT.Copy).then_inc(w_hi_done, 1)

            for t in range(TILES):
                if t:
                    act.wait_ge(magnitude_done, t)
                act.activation(magnitudes[:, :], xn[:, t, :], ACT.Abs, accum_out=magnitude[:, t:t + 1]).then_inc(magnitude_done, 1)
                act.wait_ge(xt_ps, t + 1)
                act.activation(xt_hi[:, :, t * P:(t + 1) * P], ps_t[:, t % 2, :].rearrange("p (c n) -> p c n", c=DC),
                               ACT.Copy).then_inc(xt_hi_done, 1)
            act.wait_ge(gate_loaded, 16)
            act.wait_ge(pads_set, 2)
            act.activation(gate_hi[:, :, :], gate_raw[:, :, :], ACT.Copy).then_inc(gate_hi_done, 1)
            act.wait_ge(small_loaded, 48)
            act.wait_ge(b1_ps, 1)
            act.activation(b1_cols[:, :, :], ps_h[:, 0, 0:E * FC].rearrange("p (e c) -> p e c", e=E), ACT.Copy).then_inc(b1_done, 1)
            for i in range(DC):
                split_hi(0, i)
            for tc in range(TC):
                act.wait_ge(logits_t_ps, tc + 1)
                act.activation(hidden[tc][0:EW, :], ps_y[0:EW, tc, :], ACT.Copy).then_inc(logits_t_out, 1)
            for i in range(DC, PIECES):
                split_hi(0, i)
            act.wait_ge(b1_done, 1)
            act.wait_ge(logits_ps, 1)
            for e in range(E):
                for s in range(STEPS):
                    tc, f, n = s // FC, s % FC, STEPS * e + s
                    act.wait_ge(h_ps, n + 1)
                    if n >= 2:
                        act.wait_ge(act_done, n - 1)
                    act.activation(hidden[n % 2][:, :], ps_h[:, n % 2, :], FUNCTIONS[e], bias=b1_cols[:, e, f:f + 1]).then_inc(hidden_done, 1)
                    act.wait_ge(hidden_done, n + 1)
                    act.activation(act_hi[:, f, tc * BANK:(tc + 1) * BANK], hidden[n % 2][:, :], ACT.Copy).then_inc(act_hi_done, 1)
                    if n == 1:
                        act.wait_ge(centred, 1)
                        act.activation(scores[:, :, :], scores[:, :, :], ACT.Exp).then_inc(exp_done, 1)
                    if e + 1 < E:
                        split_hi(e + 1, s)

        @block.vector
        def _(dve):
            chain = Chain(dve, router)

            def split_lo(e, i):
                raw, hi, lo = weight_piece(e, i)
                dve.wait_ge(w_hi_done, PIECES * e + i + 1)
                dve.tensor_tensor(lo, raw, hi.bitcast(F32), ALU.subtract).then_inc(w_done, 1)

            for t in range(TILES):
                dve.wait_ge(xt_hi_done, t + 1)
                dve.tensor_tensor(xt_lo[:, :, t * P:(t + 1) * P], ps_t[:, t % 2, :].rearrange("p (c n) -> p c n", c=DC),
                                  xt_hi[:, :, t * P:(t + 1) * P].bitcast(F32), ALU.subtract).then_inc(xt_done, 1)
            dve.wait_ge(gate_hi_done, 1)
            dve.tensor_tensor(gate_lo[:, :, :], gate_raw[:, :, :], gate_hi[:, :, :].bitcast(F32), ALU.subtract).then_inc(gate_done, 1)
            for i in range(DC):
                split_lo(0, i)
            def route():
                dve.wait_ge(strength_ps, 1)
                chain.link(dve.tensor_scalar(strength[:, :], strengths[:, 0, :], 1.0 / (VISION * D), 1e-8, ALU.mult, ALU.add))
                chain.link(dve.reciprocal(strength[:, :], strength[:, :]))
                chain.link(dve.scalar_tensor_tensor(ratio[:, :], strengths[:, 1, :], 1.0 / ((TPB * P - VISION) * D),
                                                    strength[:, :], ALU.mult, ALU.mult))
                dve.wait_ge(logits_ps, 1)
                dve.wait_ge(small_loaded, 48)
                chain.link(dve.tensor_tensor(logits[:, :, :], ps_r[:, 0:TILES * EW].rearrange("p (t e) -> p t e", t=TILES)[:, :, 0:E],
                                             gate_rows[:, 1, :].unsqueeze(1).to_broadcast([P, TILES, E]), ALU.add))
                for b in range(batches):
                    tiles = slice(TPB * b, TPB * (b + 1))
                    chain.link(dve.scalar_tensor_tensor(logits[:, tiles, :], gate_rows[:, 0, :].unsqueeze(1).to_broadcast([P, TPB, E]),
                                                        ratio[:, b:b + 1], logits[:, tiles, :], ALU.mult, ALU.add))
                softmax_rows(dve, chain, scores[:, :, :], logits[:, :, :], row[:, :], row2[:, :], exp_done, centred)

            def choose():
                top_two(dve, chain, scores[:, :, :], ramp[:, :], hit[:, :, :], first[:, :, :], second[:, :, :], rest[:, :, :],
                        row[:, :], best[:, :], runner[:, :])
                chain.link(dve.tensor_tensor(row[:, :], best[:, :], runner[:, :], ALU.add))
                chain.link(dve.tensor_scalar(row[:, :], row[:, :], 1e-8, None, ALU.add))
                chain.link(dve.reciprocal(row[:, :], row[:, :]))
                chain.link(dve.tensor_tensor(best[:, :], best[:, :], row[:, :], ALU.mult))
                chain.link(dve.tensor_tensor(runner[:, :], runner[:, :], row[:, :], ALU.mult))
                dve.tensor_copy(chosen[:, :, 0, :], first[0:1, 0:TILES:TPB, :])
                dve.tensor_copy(chosen[:, :, 1, :], second[0:1, 0:TILES:TPB, :]).then_inc(chosen_done, 1)

            for i in range(DC, PIECES):
                split_lo(0, i)

            def shares():
                dve.wait_ge(choices_ps, 1)
                for b in range(batches):
                    tiles = slice(TPB * b, TPB * (b + 1))
                    pick = lambda i: choices[:, b, i, :].unsqueeze(1).to_broadcast([P, TPB, E])
                    chain.link(dve.tensor_tensor(part[:, tiles, :], pick(0), wide(best[:, tiles], E), ALU.mult))
                    chain.link(dve.tensor_tensor(share[:, tiles, :], pick(1), wide(runner[:, tiles], E), ALU.mult))
                    chain.link(dve.tensor_tensor(share[:, tiles, :], share[:, tiles, :], part[:, tiles, :], ALU.add))

            for e in range(E):
                for s in range(STEPS):
                    tc, f, n = s // FC, s % FC, STEPS * e + s
                    dve.wait_ge(act_hi_done, n + 1)
                    dve.tensor_tensor(act_lo[:, f, tc * BANK:(tc + 1) * BANK], hidden[n % 2][:, :],
                                      act_hi[:, f, tc * BANK:(tc + 1) * BANK].bitcast(F32), ALU.subtract).then_inc(act_done, 1)
                    if n == 1:
                        route()
                    if n == 4:
                        choose()
                    if e + 1 < E:
                        split_lo(e + 1, s)
                if e == 0:
                    shares()
                for t in range(TILES):
                    n = TILES * e + t
                    dve.wait_ge(y_ps, n + 1)
                    if t == 0:
                        dve.wait_ge(b2_loaded[e], 16)
                    dve.tensor_tensor(biased[:, n % 2, :], ps_y[:, n % 2, :], b2_rows[:, e, :], ALU.add).then_inc(y_biased, 1)
                    dve.wait_ge(y_biased, n + 1)
                    if e:
                        dve.wait_ge(added, TILES * (e - 1) + t + 1)
                    dve.scalar_tensor_tensor(x_res[:, t, :], biased[:, n % 2, :], share[:, t, e:e + 1], x_res[:, t, :],
                                             ALU.mult, ALU.add).then_inc(added, 1)
                    if e == E - 1:
                        dve.wait_ge(added, n + 1)
                        tile_statistics(dve, stats, x_res[:, t, :], t, stats_done)


def normed_attention_block(nc, held, ctx_in, wq, bq, wk, bk, fn_w, qn_w, kn_w, x_res, xn, stats, ident, ones):
    B, CTX, D = ctx_in.shape
    TILES = x_res.shape[1]
    QT = TILES // B
    TOK = QT * P
    DC = D // P
    KT = -(-CTX // P)
    LAST = CTX - (KT - 1) * P
    WIDTH = CTX + CTX % 2
    BANK = 512
    CHUNKS = [(c, min(BANK, WIDTH - c)) for c in range(0, WIDTH, BANK)]
    HALVES = [(0, 2 * BANK), (2 * BANK, CTX)]
    STEPS = KT // 2
    TILES_OF = [[2 * s, 2 * s + 1] + ([KT - 1] if s == STEPS - 1 else []) for s in range(STEPS)]
    COLS = [(2 * P * s, 2 * P if s < STEPS - 1 else WIDTH - 2 * P * s) for s in range(STEPS)]
    RING = 4
    GROUP = BANK // P
    GROUPS = -(-KT // GROUP)
    EPS = 1e-6
    SCALE = 1.0 / math.sqrt(D)
    rows_of = lambda k: LAST if k == KT - 1 else P
    step_of = lambda t: min(t // 2, STEPS - 1)
    widths = [max(n for s, (_, n) in enumerate(COLS) if s % 2 == a) for a in range(2)]
    assert len(CHUNKS) == 4 and D == BANK and QT == 2 and GROUPS == 4 and LAST < P and KT % 2 == 1 and STEPS % 2 == 0

    with ExitStack() as ctx:
        sb = lambda n, s, d=F32: ctx.enter_context(nc.sbuf_tensor(f"c_{n}", s, d))
        sem = lambda n: new_semaphore(nc, held, f"c_{n}")
        raw = sb("raw", [P, RING, D])
        w_hi, w_lo = sb("w_hi", [P, DC, D], F32R), sb("w_lo", [P, DC, D], F32R)
        f_hi, f_lo = sb("f_hi", [P, KT, D], F32R), sb("f_lo", [P, KT, D], F32R)
        k_hi, k_lo = sb("k_hi", [P, DC, WIDTH], F32R), sb("k_lo", [P, DC, WIDTH], F32R)
        t_hi = [sb(f"t_hi{a}", [P, DC, widths[a]], F32R) for a in range(2)]
        t_lo = [sb(f"t_lo{a}", [P, DC, widths[a]], F32R) for a in range(2)]
        q_hi, q_lo = sb("q_hi", [P, DC, TOK], F32R), sb("q_lo", [P, DC, TOK], F32R)
        shared = sb("shared", [P, 2 * WIDTH])
        probs = [shared[:, j * WIDTH:(j + 1) * WIDTH] for j in range(QT)]
        squared = [shared[:, a * DC * widths[0]:a * DC * widths[0] + DC * widths[a]].rearrange("p (c n) -> p c n", c=DC) for a in range(2)]
        scratch = shared[:, DC * sum(widths):DC * sum(widths) + D]
        key_inv = sb("key_inv", [P, WIDTH])
        wk_raw = [key_inv[:, t * D:(t + 1) * D] for t in range(DC - 1)] + [scratch]
        fn_row = sb("fn_row", [P, D])
        columns = sb("columns", [P, 5, DC])
        vectors = sb("vectors", [5 * DC, P])
        qk_w, eps_col = sb("qk_w", [P, DC]), sb("eps_col", [P, 1])
        squares, inverse = sb("squares", [P, KT]), sb("inverse", [P, KT])
        table_seed = sb("table_seed", [P, 1])
        q_inv, q_inv_now = sb("q_inv", [P, TILES]), sb("q_inv_now", [P, QT])
        half_max, neg_max = sb("half_max", [P, 2]), sb("neg_max", [P, QT])
        half_sum, row_sum, row_inv = sb("half_sum", [P, QT, 2]), sb("row_sum", [P, QT]), sb("row_inv", [P, QT])
        BQ, BK, FN, QN, KN = range(5)
        queries = xn[:, :, :].rearrange("p t d -> p (t d)").rearrange("p (b n) -> p b n", b=B)

        ps_s = ctx.enter_context(nc.psum_tensor("c_ps_s", [P, 4, BANK], F32))
        ps_t = ctx.enter_context(nc.psum_tensor("c_ps_t", [P, 2, BANK], F32))
        ps_p = ctx.enter_context(nc.psum_tensor("c_ps_p", [P, 2, BANK], F32))
        s_flat = ps_s[:, :, :].rearrange("p c n -> p (c n)")

        wq_loaded, wk_loaded, rows_loaded, set_up, qk_w_done = sem("wq_loaded"), sem("wk_loaded"), sem("rows_loaded"), sem("set_up"), sem("qk_w_done")
        columns_ps, columns_done = sem("columns_ps"), sem("columns_done")
        ctx_loaded = [sem(f"ctx_loaded{i}") for i in range(RING)]
        w_ps, w_hi_done, w_done = sem("w_ps"), sem("w_hi_done"), sem("w_done")
        xt_ps, xt_hi_done, xt_done = sem("xt_ps"), sem("xt_hi_done"), sem("xt_done")
        qp_ps, q_squared, q_kept, qs_ps, q_root, q_inv_done = (sem(n) for n in (
            "qp_ps", "q_squared", "q_kept", "qs_ps", "q_root", "q_inv_done"))
        c_squared, c_root, c_inv, f_scaled, f_hi_done, f_done = (sem(n) for n in (
            "c_squared", "c_root", "c_inv", "f_scaled", "f_hi_done", "f_done"))
        ft_ps, ft_hi_done, ft_done = sem("ft_ps"), sem("ft_hi_done"), sem("ft_done")
        kp_ps, k_squared, k_hi_done, k_done = sem("kp_ps"), sem("k_squared"), sem("k_hi_done"), sem("k_done")
        k_added, k_summed, ks_ps, k_root, k_inv = (sem(n) for n in ("k_added", "k_summed", "ks_ps", "k_root", "k_inv"))
        q_hi_done, q_done, q_inv_copied = sem("q_hi_done"), sem("q_done"), sem("q_inv_copied")
        s_ps, s_scaled, max_done, neg_max_done = sem("s_ps"), sem("s_scaled"), sem("max_done"), sem("neg_max_done")
        probs_done, sum_done, inv_done = sem("probs_done"), sem("sum_done"), sem("inv_done")
        stats_done = sem("stats_done")
        pt_ps, pt_hi_done, pt_done = sem("pt_ps"), sem("pt_hi_done"), sem("pt_done")
        pv_ps, o_ps, o_scaled, added = sem("pv_ps"), sem("o_ps"), sem("o_scaled"), sem("added")
        def load_weights(sp):
            sp.dma_start(raw[:, 0:DC, :], wq.rearrange("(t p) d -> p t d", p=P)).then_inc(wq_loaded, 16)
            for i, column in enumerate((bq, bk, fn_w, qn_w, kn_w)):
                sp.dma_start(vectors[DC * i:DC * (i + 1), :], column.rearrange("(c p) -> c p", p=P)).then_inc(rows_loaded, 16)
            for t in range(DC):
                sp.dma_start(wk_raw[t], wk[t * P:(t + 1) * P, :]).then_inc(wk_loaded, 16)
            sp.dma_start(fn_row[:, :], fn_w.partition_broadcast(P)).then_inc(rows_loaded, 16)

        prime(nc, (o_ps, pt_done, o_scaled, s_scaled, s_ps))
        norm_block(nc, held, x_res, xn, stats, 1e-5, "norm2", prefetch=load_weights)
        block = ctx.enter_context(nc.Block())
        by_chunk = lambda bank, n=P: bank.rearrange("p (c n) -> p c n", c=DC)[:, :, 0:n]

        @block.sync
        def _(sp):
            def load_tile(b, t):
                n = rows_of(t)
                sp.dma_start(raw[0:n, t % RING, :], ctx_in[b, t * P:t * P + n, :]).then_inc(ctx_loaded[t % RING], 16)

            sp.wait_ge(w_ps, DC)
            for t in range(RING):
                load_tile(0, t)
            with sp.Fori(0, B) as b:
                for t in range(RING, KT):
                    sp.wait_ge(ft_ps, KT * b + t - RING + 1)
                    sp.wait_ge(f_done, KT * b + t - RING + 1)
                    load_tile(b, t)
                sp.wait_ge(ft_ps, KT * (b + 1))
                sp.wait_ge(f_done, KT * (b + 1))
                for t in range(RING):
                    load_tile((b + 1) % B, t)

        @block.gpsimd
        def _(pool):
            pool.memset(squares[:, :], 1.0).then_inc(set_up, 1)
            pool.memset(eps_col[:, :], EPS).then_inc(set_up, 1)
            pool.memset(t_hi[1][:, :, widths[1] - 1:widths[1]].bitcast(F32), 0.0).then_inc(set_up, 1)
            pool.memset(t_lo[1][:, :, widths[1] - 1:widths[1]].bitcast(F32), 0.0).then_inc(set_up, 1)
            with pool.Fori(0, B) as b:
                for t in range(KT):
                    n = rows_of(t)
                    pool.wait_ge(f_scaled, KT * b + t + 1)
                    if t == 0:
                        pool.wait_ge(o_ps, PRIMED + QT * b)
                    pool.tensor_tensor(f_hi[0:n, t, :], raw[0:n, t % RING, :], ones[0:n, 0:1].to_broadcast([n, D]),
                                       ALU.mult).then_inc(f_hi_done, 1)
                    pool.wait_ge(f_hi_done, KT * b + t + 1)
                    pool.tensor_tensor(f_lo[0:n, t, :], raw[0:n, t % RING, :], f_hi[0:n, t, :].bitcast(F32),
                                       ALU.subtract).then_inc(f_done, 1)

        @block.tensor
        def _(pe):
            def three(out, a_hi, a_lo, m_hi, m_lo, first, last):
                pe.matmul(out, a_hi, m_hi, start=first, stop=False)
                pe.matmul(out, a_hi, m_lo, start=False, stop=False)
                return pe.matmul(out, a_lo, m_hi, start=False, stop=last)

            def transpose_weights(which, tiles):
                pe.wait_ge(*((wk_loaded, 16 * DC) if which else (wq_loaded, 16)))
                for c in range(DC):
                    n = DC * which + c
                    if n >= 2:
                        pe.wait_ge(w_done, n - 1)
                    if n == DC:
                        pe.wait_ge(xt_done, TILES)
                    for t in range(DC):
                        tr = pe.transpose(ps_t[:, n % 2, t * P:(t + 1) * P], tiles[t][:, c * P:(c + 1) * P], ident[:, :])
                    tr.then_inc(w_ps, 1)

            def project(f, a, n):
                for c in range(DC):
                    mm = three(ps_s[:, f, 0:n], w_hi[:, c, f * P:(f + 1) * P], w_lo[:, c, f * P:(f + 1) * P],
                               t_hi[a][:, c, 0:n], t_lo[a][:, c, 0:n], c == 0, c == DC - 1)
                return mm

            def transpose_x(i):
                for t in range(QT * i, QT * (i + 1)):
                    if t >= 2:
                        pe.wait_ge(xt_done, t - 1)
                    else:
                        pe.wait_ge(w_done, DC)
                    for c in range(DC):
                        tr = pe.transpose(ps_t[:, t % 2, c * P:(c + 1) * P], xn[:, t, c * P:(c + 1) * P], ident[:, :])
                    tr.then_inc(xt_ps, 1)

            def sum_query_squares(i):
                pe.wait_ge(q_squared, DC * (i + 1))
                for j in range(QT):
                    for f in range(DC):
                        mm = pe.matmul(ps_p[:, 0, QT * i + j:QT * i + j + 1], squared[i % 2][:, f, j * P:(j + 1) * P], ones[:, 0:1],
                                       start=f == 0, stop=f == DC - 1)
                mm.then_inc(qs_ps, 1)

            transpose_weights(0, [raw[:, t, :] for t in range(DC)])
            pe.wait_ge(rows_loaded, 96)
            pe.transpose(ps_p[:, 1, 0:5 * DC], vectors[:, :], ident[0:5 * DC, 0:5 * DC]).then_inc(columns_ps, 1)
            transpose_x(0)
            for i in range(B):
                if i + 1 < B:
                    transpose_x(i + 1)
                pe.wait_ge(xt_done, QT * (i + 1))
                for f in range(DC):
                    if i:
                        pe.wait_ge(q_kept, DC * (i - 1) + f + 1)
                    project(f, i % 2, TOK).then_inc(qp_ps, 1)
                if i:
                    sum_query_squares(i - 1)
            sum_query_squares(B - 1)
            transpose_weights(1, wk_raw)
            pe.wait_ge(w_done, 2 * DC)
            pe.wait_ge(set_up, 4)
            pe.wait_ge(q_kept, DC * B)
            pe.wait_ge(q_root, 1)
            with pe.Fori(0, B) as b:
                def transpose_features(s, third=False):
                    for t in TILES_OF[s][2:] if third else TILES_OF[s][:2]:
                        n = rows_of(t)
                        pe.wait_ge(f_scaled, KT * b + t + 1)
                        if t >= 2:
                            pe.wait_ge(ft_done, KT * b + t - 1)
                        else:
                            pe.wait_ge(pt_done, PRIMED + GROUPS * QT * b)
                        for c in range(DC):
                            tr = pe.transpose(ps_t[:, t % 2, c * P:c * P + n], raw[0:n, t % RING, c * P:(c + 1) * P], ident[0:n, 0:n])
                        tr.then_inc(ft_ps, 1)

                def sum_key_squares(s):
                    n = COLS[s][1]
                    pe.wait_ge(k_summed, STEPS * b + s + 1)
                    if s >= 2:
                        pe.wait_ge(k_root, STEPS * b + s - 1)
                    else:
                        pe.wait_ge(o_scaled, PRIMED + QT * b)
                    pe.matmul(ps_p[:, s % 2, 0:n], ones[:, :], squared[s % 2][:, 0, :][:, 0:n], start=True, stop=True).then_inc(ks_ps, 1)

                transpose_features(0)
                for s in range(STEPS):
                    if s + 1 < STEPS:
                        transpose_features(s + 1)
                    pe.wait_ge(ft_done, KT * b + TILES_OF[s][-1] + 1)
                    for f in range(DC):
                        if s:
                            pe.wait_ge(k_done, DC * (STEPS * b + s - 1) + f + 1)
                        elif f == 0:
                            pe.wait_ge(s_scaled, PRIMED + 2 * QT * b)
                        project(f, s % 2, COLS[s][1]).then_inc(kp_ps, 1)
                        if s and f == 2:
                            sum_key_squares(s - 1)
                        if f == 1 and s + 1 < STEPS:
                            transpose_features(s + 1, third=True)

                def scores(j):
                    for half in range(2):
                        if j:
                            pe.wait_ge(s_scaled, PRIMED + 2 * QT * b + half + 1)
                        for ch in (2 * half, 2 * half + 1):
                            c0, n = CHUNKS[ch]
                            if j == 0:
                                last = max(s for s in range(STEPS) if COLS[s][0] < c0 + n)
                                pe.wait_ge(k_done, DC * (STEPS * b + STEPS - 1) + (ch + 1 if last < STEPS - 1 else DC))
                            for c in range(DC):
                                mm = three(ps_s[:, ch, 0:n], q_hi[:, c, j * P:(j + 1) * P], q_lo[:, c, j * P:(j + 1) * P],
                                           k_hi[:, c, c0:c0 + n], k_lo[:, c, c0:c0 + n], c == 0, c == DC - 1)
                            if j == 0 and ch == 0:
                                sum_key_squares(STEPS - 1)
                        mm.then_inc(s_ps, 1)
                        if j == 1 and half == 0:
                            transpose_probs(0, 0)
                            transpose_probs(0, 1)

                def transpose_probs(j, g):
                    n = GROUPS * j + g
                    if g == 0:
                        pe.wait_ge(probs_done, 2 * QT * b + 2 * j + 1)
                    if g == GROUPS // 2:
                        pe.wait_ge(probs_done, 2 * QT * b + 2 * j + 2)
                    if n >= 2:
                        pe.wait_ge(pt_done, PRIMED + GROUPS * QT * b + n - 1)
                    for k in range(GROUP * g, min(GROUP * (g + 1), KT)):
                        r = rows_of(k)
                        tr = pe.transpose(ps_t[0:r, n % 2, (k % GROUP) * P:(k % GROUP + 1) * P], probs[j][:, k * P:k * P + r], ident[:, :])
                    tr.then_inc(pt_ps, 1)

                def weigh(j, g):
                    n = GROUPS * j + g
                    pe.wait_ge(pt_done, PRIMED + GROUPS * QT * b + n + 1)
                    for k in range(GROUP * g, min(GROUP * (g + 1), KT)):
                        r = rows_of(k)
                        mm = three(ps_p[:, j, :], t_hi[n % 2][0:r, k % GROUP, 0:P], t_lo[n % 2][0:r, k % GROUP, 0:P],
                                   f_hi[0:r, k, :], f_lo[0:r, k, :], k == 0, k == KT - 1)
                    if g == GROUPS - 1:
                        mm.then_inc(o_ps, 1)
                    else:
                        mm.then_inc(pv_ps, 1)

                pe.wait_ge(q_done, b + 1)
                scores(0)
                scores(1)
                pe.wait_ge(f_done, KT * (b + 1))
                pe.wait_ge(k_root, STEPS * (b + 1))
                steps = [(j, g) for j in range(QT) for g in range(GROUPS)]
                for n, (j, g) in enumerate(steps):
                    if 1 < n + 1 < len(steps):
                        transpose_probs(*steps[n + 1])
                    weigh(j, g)

        @block.scalar
        def _(act):
            def weights_hi(n):
                act.wait_ge(w_ps, n + 1)
                if n == DC:
                    act.wait_ge(qp_ps, DC * B)
                act.activation(w_hi[:, n % DC, :], ps_t[:, n % 2, :], ACT.Copy,
                               scale=1.0 if n < DC else columns[:, FN, n % DC:n % DC + 1]).then_inc(w_hi_done, 1)

            for c in range(DC):
                weights_hi(c)
            act.wait_ge(columns_done, 1)
            act.wait_ge(set_up, 4)

            def inputs_hi(i):
                for t in range(QT * i, QT * (i + 1)):
                    act.wait_ge(xt_ps, t + 1)
                    if i >= 2:
                        act.wait_ge(qp_ps, DC * (i - 1))
                    act.activation(t_hi[i % 2][:, :, t % 2 * P:(t % 2 + 1) * P], by_chunk(ps_t[:, t % 2, :]),
                                   ACT.Copy).then_inc(xt_hi_done, 1)

            inputs_hi(0)
            for i in range(B):
                if i + 1 < B:
                    inputs_hi(i + 1)
                for f in range(DC):
                    act.wait_ge(qp_ps, DC * i + f + 1)
                    if i >= 2:
                        act.wait_ge(qs_ps, i - 1)
                    act.activation(squared[i % 2][:, f, 0:TOK], ps_s[:, f, 0:TOK], ACT.Square,
                                   bias=columns[:, BQ, f:f + 1]).then_inc(q_squared, 1)
            act.wait_ge(qs_ps, B)
            act.activation(q_inv[:, :], ps_p[:, 0, 0:TILES], ACT.Sqrt, bias=eps_col[:, :], scale=1.0 / D).then_inc(q_root, 1)

            def root_of_tiles(b, s, place, scratch):
                for t in TILES_OF[s]:
                    n = rows_of(t)
                    per_batch = [q for q in range(KT) if q % RING == t % RING]
                    act.wait_ge(ctx_loaded[t % RING], 16 * (len(per_batch) * place + per_batch.index(t) + 1))
                    act.wait_ge(c_squared, KT * place + t)
                    act.activation(scratch[0:n, :], raw[0:n, t % RING, :], ACT.Square,
                                   accum_out=squares[0:n, t:t + 1]).then_inc(c_squared, 1)
                t0, t1 = TILES_OF[s][0], TILES_OF[s][-1] + 1
                act.wait_ge(c_squared, KT * place + t1)
                act.activation(inverse[:, t0:t1], squares[:, t0:t1], ACT.Sqrt, bias=eps_col[:, :], scale=1.0 / D).then_inc(c_root, 1)

            root_of_tiles(0, 0, 0, shared[:, 0:D])
            root_of_tiles(0, 1, 0, shared[:, 0:D])
            for c in range(DC):
                weights_hi(DC + c)
            with act.Fori(0, B) as b:
                def features_hi(s, third=False):
                    for t in TILES_OF[s][2:] if third else TILES_OF[s][:2]:
                        n = rows_of(t)
                        act.wait_ge(ft_ps, KT * b + t + 1)
                        if s >= 2:
                            act.wait_ge(kp_ps, DC * (STEPS * b + s - 1))
                        else:
                            act.wait_ge(o_ps, PRIMED + QT * b)
                        at = t * P - COLS[s][0]
                        act.activation(t_hi[s % 2][:, :, at:at + n], by_chunk(ps_t[:, t % 2, :], n), ACT.Copy).then_inc(ft_hi_done, 1)

                def key_roots(s):
                    c0, n = COLS[s]
                    act.wait_ge(ks_ps, STEPS * b + s + 1)
                    act.activation(key_inv[:, c0:c0 + n], ps_p[:, s % 2, 0:n], ACT.Sqrt, bias=eps_col[:, :], scale=1.0 / D
                                   ).then_inc(k_root, 1)

                features_hi(0)
                for s in range(STEPS):
                    c0, w = COLS[s]
                    if s + 1 < STEPS:
                        features_hi(s + 1)
                    if s == 0:
                        act.wait_ge(s_ps, PRIMED + 2 * QT * b)
                        act.activation(q_hi[:, :, :].rearrange("p c n -> p (c n)"),
                                       queries[:, bass.ds(b, 1), :].rearrange("p a n -> p (a n)"), ACT.Copy).then_inc(q_hi_done, 1)
                    for f in range(DC):
                        act.wait_ge(kp_ps, DC * (STEPS * b + s) + f + 1)
                        if s >= 2:
                            act.wait_ge(ks_ps, STEPS * b + s - 1)
                        act.activation(k_hi[:, f, c0:c0 + w], ps_s[:, f, 0:w], ACT.Identity, bias=columns[:, BK, f:f + 1]
                                       ).then_inc(k_hi_done, 1)
                        act.activation(squared[s % 2][:, f, 0:w], ps_s[:, f, 0:w], ACT.Square, bias=columns[:, BK, f:f + 1]
                                       ).then_inc(k_squared, 1)
                        if f == 0 and s + 2 < STEPS:
                            root_of_tiles(b, s + 2, b, scratch)
                        if f == 1 and s + 1 < STEPS:
                            features_hi(s + 1, third=True)
                        if f == 3 and s:
                            key_roots(s - 1)
                key_roots(STEPS - 1)
                root_of_tiles(b + 1, 0, b + 1, scratch)
                root_of_tiles(b + 1, 1, b + 1, scratch)

                def probs_hi(j, g):
                    n = GROUPS * j + g
                    m = min(GROUP, KT - GROUP * g)
                    r = P if m > 1 else LAST
                    act.wait_ge(pt_ps, GROUPS * QT * b + n + 1)
                    if n >= 2:
                        if (n - 2) % GROUPS == GROUPS - 1:
                            act.wait_ge(o_ps, PRIMED + QT * b + (n - 2) // GROUPS + 1)
                        else:
                            act.wait_ge(pv_ps, (GROUPS - 1) * (QT * b + (n - 2) // GROUPS) + (n - 2) % GROUPS + 1)
                    act.activation(t_hi[n % 2][0:r, 0:m, 0:P], by_chunk(ps_t[:, n % 2, :])[0:r, 0:m, :], ACT.Copy).then_inc(pt_hi_done, 1)

                for j in range(QT):
                    act.wait_ge(neg_max_done, QT * b + j + 1)
                    for half, (lo, hi) in enumerate(HALVES):
                        act.activation(probs[j][:, lo:hi], probs[j][:, lo:hi], ACT.Exp, bias=neg_max[:, j:j + 1], scale=SCALE,
                                       accum_out=half_sum[:, j, half:half + 1]).then_inc(probs_done, 1)
                    if j == 0:
                        probs_hi(0, 0)
                        probs_hi(0, 1)
                act.activation(table_seed[:, :], eps_col[:, :], ACT.Sqrt)
                for j in range(QT):
                    for g in range(GROUPS):
                        if GROUPS * j + g >= 2:
                            probs_hi(j, g)

        @block.vector
        def _(dve):
            def weights_lo(n):
                dve.wait_ge(w_hi_done, n + 1)
                if n < DC:
                    dve.tensor_tensor(w_lo[:, n, :], ps_t[:, n % 2, :], w_hi[:, n, :].bitcast(F32), ALU.subtract).then_inc(w_done, 1)
                else:
                    dve.scalar_tensor_tensor(w_lo[:, n % DC, :], ps_t[:, n % 2, :], columns[:, FN, n % DC:n % DC + 1],
                                             w_hi[:, n % DC, :].bitcast(F32), ALU.mult, ALU.subtract).then_inc(w_done, 1)

            for c in range(DC):
                weights_lo(c)
            dve.wait_ge(columns_ps, 1)
            dve.tensor_copy(columns[:, :, :].rearrange("p i c -> p (i c)"), ps_p[:, 1, 0:5 * DC]).then_inc(columns_done, 1)
            dve.wait_ge(columns_done, 1)
            dve.tensor_tensor(qk_w[:, :], columns[:, QN, :], columns[:, KN, :], ALU.mult).then_inc(qk_w_done, 1)

            def inputs_lo(i):
                for t in range(QT * i, QT * (i + 1)):
                    dve.wait_ge(xt_hi_done, t + 1)
                    at = t % 2 * P
                    dve.tensor_tensor(t_lo[i % 2][:, :, at:at + P], by_chunk(ps_t[:, t % 2, :]),
                                      t_hi[i % 2][:, :, at:at + P].bitcast(F32), ALU.subtract).then_inc(xt_done, 1)

            inputs_lo(0)
            dve.wait_ge(qk_w_done, 1)
            for i in range(B):
                if i + 1 < B:
                    inputs_lo(i + 1)
                for f in range(DC):
                    dve.wait_ge(q_squared, DC * i + f + 1)
                    dve.tensor_scalar(queries[:, i, f * TOK:(f + 1) * TOK], ps_s[:, f, 0:TOK], columns[:, BQ, f:f + 1],
                                      qk_w[:, f:f + 1], ALU.add, ALU.mult).then_inc(q_kept, 1)
            dve.wait_ge(q_root, 1)
            dve.reciprocal(q_inv[:, :], q_inv[:, :]).then_inc(q_inv_done, 1)

            def scale_tiles(s, place):
                dve.wait_ge(c_root, STEPS * place + s + 1)
                t0, t1 = TILES_OF[s][0], TILES_OF[s][-1] + 1
                dve.reciprocal(inverse[:, t0:t1], inverse[:, t0:t1]).then_inc(c_inv, 1)
                dve.wait_ge(c_inv, STEPS * place + s + 1)
                for t in TILES_OF[s]:
                    n = rows_of(t)
                    dve.tensor_scalar(raw[0:n, t % RING, :], raw[0:n, t % RING, :], inverse[0:n, t:t + 1], None,
                                      ALU.mult).then_inc(f_scaled, 1)

            scale_tiles(0, 0)
            scale_tiles(1, 0)
            for c in range(DC):
                weights_lo(DC + c)
            dve.wait_ge(q_inv_done, 1)
            with dve.Fori(0, B) as b:
                def features_lo(s, third=False):
                    for t in TILES_OF[s][2:] if third else TILES_OF[s][:2]:
                        n = rows_of(t)
                        at = t * P - COLS[s][0]
                        dve.wait_ge(ft_hi_done, KT * b + t + 1)
                        dve.tensor_tensor(t_lo[s % 2][:, :, at:at + n], by_chunk(ps_t[:, t % 2, :], n),
                                          t_hi[s % 2][:, :, at:at + n].bitcast(F32), ALU.subtract).then_inc(ft_done, 1)

                def output(b, j):
                    x_tile = x_res[:, bass.ds(QT * b + j, 1), :].rearrange("p a d -> p (a d)")
                    dve.wait_ge(o_ps, PRIMED + QT * b + j + 1)
                    dve.scalar_tensor_tensor(probs[j][:, 0:D], ps_p[:, j, :], row_inv[:, j:j + 1], fn_row[:, :], ALU.mult,
                                             ALU.mult).then_inc(o_scaled, 1)
                    dve.wait_ge(o_scaled, PRIMED + QT * b + j + 1)
                    dve.tensor_tensor(x_tile, probs[j][:, 0:D], x_tile, ALU.add).then_inc(added, 1)
                    dve.wait_ge(added, QT * b + j + 1)
                    tile_statistics(dve, stats, x_tile, QT * b + j, stats_done)

                def key_inverses(s):
                    c0, n = COLS[s]
                    dve.wait_ge(k_root, STEPS * b + s + 1)
                    dve.reciprocal(key_inv[:, c0:c0 + n], key_inv[:, c0:c0 + n]).then_inc(k_inv, 1)

                features_lo(0)
                for s in range(STEPS):
                    c0, w = COLS[s]
                    if s + 1 < STEPS:
                        features_lo(s + 1)
                    if s == 0:
                        dve.wait_ge(q_hi_done, b + 1)
                        dve.tensor_tensor(q_lo[:, :, :].rearrange("p c n -> p (c n)"),
                                          queries[:, bass.ds(b, 1), :].rearrange("p a n -> p (a n)"),
                                          q_hi[:, :, :].rearrange("p c n -> p (c n)").bitcast(F32), ALU.subtract).then_inc(q_done, 1)
                        dve.tensor_copy(q_inv_now[:, :], q_inv[:, bass.ds(QT * b, QT)]).then_inc(q_inv_copied, 1)
                    for f in range(DC):
                        dve.wait_ge(k_squared, DC * (STEPS * b + s) + f + 1)
                        dve.scalar_tensor_tensor(k_lo[:, f, c0:c0 + w], ps_s[:, f, 0:w], columns[:, BK, f:f + 1],
                                                 k_hi[:, f, c0:c0 + w].bitcast(F32), ALU.add, ALU.subtract).then_inc(k_done, 1)
                        if f == 1 and s + 2 < STEPS:
                            scale_tiles(s + 2, b)
                        if f == 1 and s + 1 < STEPS:
                            features_lo(s + 1, third=True)
                    sq = squared[s % 2][:, :, 0:w]
                    dve.tensor_tensor(sq[:, 0:2, :], sq[:, 0:2, :], sq[:, 2:4, :], ALU.add).then_inc(k_added, 1)
                    dve.wait_ge(k_added, STEPS * b + s + 1)
                    dve.tensor_tensor(sq[:, 0, :], sq[:, 0, :], sq[:, 1, :], ALU.add).then_inc(k_summed, 1)
                    if s:
                        key_inverses(s - 1)
                key_inverses(STEPS - 1)
                dve.wait_ge(q_inv_copied, b + 1)
                dve.wait_ge(k_inv, STEPS * (b + 1))
                def probs_lo(j, g):
                    n = GROUPS * j + g
                    m = min(GROUP, KT - GROUP * g)
                    r = P if m > 1 else LAST
                    dve.wait_ge(pt_hi_done, GROUPS * QT * b + n + 1)
                    dve.tensor_tensor(t_lo[n % 2][0:r, 0:m, 0:P], by_chunk(ps_t[:, n % 2, :])[0:r, 0:m, :],
                                      t_hi[n % 2][0:r, 0:m, 0:P].bitcast(F32), ALU.subtract).then_inc(pt_done, 1)

                for j in range(QT):
                    for half, (lo, hi) in enumerate(HALVES):
                        if j == 1 and half == 1:
                            probs_lo(0, 0)
                            probs_lo(0, 1)
                        dve.wait_ge(s_ps, PRIMED + 2 * QT * b + 2 * j + half + 1)
                        dve.scalar_tensor_tensor(probs[j][:, lo:hi], s_flat[:, lo:hi], q_inv_now[:, j:j + 1], key_inv[:, lo:hi],
                                                 ALU.mult, ALU.mult).then_inc(s_scaled, 1)
                        dve.wait_ge(s_scaled, PRIMED + 2 * QT * b + 2 * j + half + 1)
                        dve.reduce_max(half_max[:, half:half + 1], probs[j][:, lo:hi], AX.X).then_inc(max_done, 1)
                    dve.wait_ge(max_done, 2 * QT * b + 2 * j + 2)
                    dve.tensor_scalar(neg_max[:, j:j + 1], half_max[:, 0:1], half_max[:, 1:2], -SCALE, ALU.max,
                                      ALU.mult).then_inc(neg_max_done, 1)
                    if j == 0:
                        scale_tiles(0, b + 1)
                        scale_tiles(1, b + 1)
                for j in range(QT):
                    for g in range(GROUPS):
                        if GROUPS * j + g >= 2:
                            probs_lo(j, g)
                        if GROUPS * j + g == GROUPS:
                            output(b, 0)
                    if j == 0:
                        dve.wait_ge(probs_done, 2 * QT * (b + 1))
                        dve.tensor_tensor(row_sum[:, :], half_sum[:, :, 0], half_sum[:, :, 1], ALU.add).then_inc(sum_done, 1)
                        dve.wait_ge(sum_done, b + 1)
                        dve.reciprocal(row_inv[:, :], row_sum[:, :]).then_inc(inv_done, 1)
                        dve.wait_ge(inv_done, b + 1)
                output(b, 1)


def routed_experts_block(nc, held, gate_w, w_gate_up, w_down, shared_gate_up, shared_down, x_res, xn, ident, ones, out):
    TILES, D = x_res.shape[1], x_res.shape[2]
    E, I2, _ = w_gate_up.shape
    I = I2 // 2
    SHARED = shared_down.shape[1] // I
    N = E + SHARED
    DC = D // P
    BANK = 512
    TC = TILES * P // BANK
    TPC = BANK // P
    JOBS = 3
    assert TILES == 8 and I == P and D == BANK and TC == 2 and E % 2 == 0 and SHARED % 2 == 0

    with ExitStack() as ctx:
        sb = lambda n, s, d=F32: ctx.enter_context(nc.sbuf_tensor(f"d_{n}", s, d))
        sem = lambda n: new_semaphore(nc, held, f"d_{n}")
        xt_hi, xt_lo = sb("xt_hi", [P, DC, TILES * P], F32R), sb("xt_lo", [P, DC, TILES * P], F32R)
        up_raw = [sb(f"up_raw{a}", [P, 2, D]) for a in range(2)]
        down_raw = [sb(f"down_raw{a}", [P, DC, I]) for a in range(2)]
        up_hi = [sb(f"up_hi{a}", [P, 2, DC, I], F32R) for a in range(2)]
        up_lo = [sb(f"up_lo{a}", [P, 2, DC, I], F32R) for a in range(2)]
        down_hi = [sb(f"down_hi{a}", [P, D], F32R) for a in range(2)]
        down_lo = [sb(f"down_lo{a}", [P, D], F32R) for a in range(2)]
        gated = [sb(f"gated{i}", [P, BANK]) for i in range(TC)]
        act_hi, act_lo = sb("act_hi", [P, TC, BANK], F32R), sb("act_lo", [P, TC, BANK], F32R)
        gate_raw, gate_hi, gate_lo = sb("gate_raw", [E, D]), sb("gate_hi", [P, DC, E], F32R), sb("gate_lo", [P, DC, E], F32R)
        ramp = sb("ramp", [P, E])
        logits, scores = sb("logits", [P, TILES, E]), sb("scores", [P, TILES, E])
        hit, first, second, rest = (sb(n, [P, TILES, E]) for n in ("hit", "first", "second", "rest"))
        row, row2, best, runner = (sb(n, [P, TILES]) for n in ("row", "row2", "best", "runner"))
        share = sb("share", [P, TILES, N])

        ps_t = ctx.enter_context(nc.psum_tensor("d_ps_t", [P, 2, BANK], F32))
        ps_h = ctx.enter_context(nc.psum_tensor("d_ps_h", [P, TC, 2, BANK], F32))
        ps_y = ctx.enter_context(nc.psum_tensor("d_ps_y", [P, 2, BANK], F32))

        gate_loaded, pads_set, gate_ps, gate_hi_done, gate_done = (sem(n) for n in (
            "gate_loaded", "pads_set", "gate_ps", "gate_hi_done", "gate_done"))
        logits_t_ps, logits_t_out = sem("logits_t_ps"), sem("logits_t_out")
        xt_ps, xt_hi_done, xt_done, logits_ps = sem("xt_ps"), sem("xt_hi_done"), sem("xt_done"), sem("logits_ps")
        logits_out, centred, exp_done, share_done, router = (sem(n) for n in ("logits_out", "centred", "exp_done", "share_done", "router"))
        raw_loaded = [sem(f"raw_loaded{a}") for a in range(2)]
        w_ps, w_hi_done, w_done = sem("w_ps"), sem("w_hi_done"), sem("w_done")
        h_ps, silu_done, gated_done, act_hi_done, act_done = (sem(n) for n in ("h_ps", "silu_done", "gated_done", "act_hi_done", "act_done"))
        y_ps, added, stored = sem("y_ps"), sem("added"), sem("stored")
        block = ctx.enter_context(nc.Block())
        by_chunk = lambda bank: bank.rearrange("p (c n) -> p c n", c=DC)
        tile_rows = out.rearrange("b (t p) d -> (b t) p d", p=P)

        @block.sync
        def _(sp):
            def load(a, transposed, up, down):
                sp.wait_ge(w_ps, transposed)
                sp.dma_start(up_raw[a][:, :, :], up).then_inc(raw_loaded[a], 16)
                sp.dma_start(down_raw[a][:, :, :], down).then_inc(raw_loaded[a], 16)

            def routed(e):
                return (w_gate_up[bass.ds(e, 1), :, :].rearrange("a (k p) h -> p (a k) h", p=P),
                        w_down[bass.ds(e, 1), :, :].rearrange("a (c p) i -> p (a c) i", p=P))

            def shared(s):
                return (shared_gate_up.rearrange("(k r) h -> r k h", k=2)[bass.ds(s * I, I), :, :],
                        shared_down[:, bass.ds(s * I, I)].rearrange("(c p) i -> p c i", p=P))

            sp.dma_start(gate_raw[:, :], gate_w).then_inc(gate_loaded, 16)
            load(0, 0, *routed(0))
            load(1, 0, *routed(1))
            with sp.Fori(1, E // 2) as i:
                for a in range(2):
                    load(a, JOBS * (2 * i + a - 1), *routed(2 * i + a))
            with sp.Fori(0, SHARED // 2) as i:
                for a in range(2):
                    load(a, JOBS * (E + 2 * i + a - 1), *shared(2 * i + a))
            for t in range(TILES):
                sp.wait_ge(added, TILES * (N - 1) + t + 1)
                sp.dma_start(tile_rows[t], x_res[:, t, :]).then_inc(stored, 16)
            sp.wait_ge(stored, 16 * TILES)

        @block.gpsimd
        def _(pool):
            pool.iota(ramp[:, :], pattern=[[-1, E]], base=E, channel_multiplier=0,
                      allow_small_or_imprecise_dtypes=True).then_inc(pads_set, 1)
            pool.memset(share[:, :, E:N], 1.0).then_inc(pads_set, 1)

        @block.tensor
        def _(pe):
            def three(o, w_hi, w_lo, m_hi, m_lo, start, stop):
                pe.matmul(o, w_hi, m_hi, start=start, stop=False)
                pe.matmul(o, w_hi, m_lo, start=False, stop=False)
                return pe.matmul(o, w_lo, m_hi, start=False, stop=stop)

            def transpose_weights(n, a, pair, job, first=False):
                if job == 0:
                    pe.wait_ge(raw_loaded[a], 32 * pair + 32)
                bank = (JOBS * a + job) % 2
                if not (first and job < 2):
                    pe.wait_ge(w_done, JOBS * n + job - 1)
                for c in range(DC):
                    src = down_raw[a][:, c, :] if job == 2 else up_raw[a][:, job, c * P:(c + 1) * P]
                    tr = pe.transpose(ps_t[:, bank, c * P:(c + 1) * P], src, ident[:, :])
                tr.then_inc(w_ps, 1)

            def up(n, last, a, tc, quarter):
                k, half = quarter // 2, quarter % 2
                if quarter == 0:
                    pe.wait_ge(w_done, JOBS * n + 2)
                    if last is not None:
                        pe.wait_ge(gated_done, TC * last + tc + 1)
                for c in range(half * DC // 2, (half + 1) * DC // 2):
                    mm = three(ps_h[:, tc, k, :], up_hi[a][:, k, c, :], up_lo[a][:, k, c, :],
                               xt_hi[:, c, tc * BANK:(tc + 1) * BANK], xt_lo[:, c, tc * BANK:(tc + 1) * BANK],
                               c == 0, c == DC - 1)
                if quarter == 3:
                    mm.then_inc(h_ps, 1)

            def down(n, last, a, t):
                tc, p0 = t // TPC, t % TPC * P
                if t == 0:
                    pe.wait_ge(w_done, JOBS * n + JOBS)
                if t % TPC == 0:
                    pe.wait_ge(act_done, TC * n + tc + 1)
                if t >= 2:
                    pe.wait_ge(added, TILES * n + t - 1)
                elif last is not None:
                    pe.wait_ge(added, TILES * last + TILES + t - 1)
                three(ps_y[:, t % 2, :], act_hi[:, tc, p0:p0 + P], act_lo[:, tc, p0:p0 + P], down_hi[a][:, :],
                      down_lo[a][:, :], True, True).then_inc(y_ps, 1)

            def expert(last, n, a, pair, following=True):
                for slot in range(TC * 4):
                    up(n, last, a, slot // 4, slot % 4)
                    if slot >= 6:
                        down(n, last, a, slot - 6)
                    elif last is not None:
                        down(last, None, 1 - a, slot + 2)
                    if slot in (0, 2, 6) and following:
                        transpose_weights(n + 1, 1 - a, pair, (0, 2, 6).index(slot))

            for t in range(TILES):
                if t >= 2:
                    pe.wait_ge(xt_done, t - 1)
                for c in range(DC):
                    tr = pe.transpose(ps_t[:, t % 2, c * P:(c + 1) * P], xn[:, t, c * P:(c + 1) * P], ident[:, :])
                tr.then_inc(xt_ps, 1)
            pe.wait_ge(gate_loaded, 16)
            for c in range(DC):
                tr = pe.transpose(ps_h[:, 0, 0, c * E:(c + 1) * E], gate_raw[:, c * P:(c + 1) * P], ident[0:E, 0:E])
            tr.then_inc(gate_ps, 1)
            pe.wait_ge(xt_done, TILES)
            for job in range(JOBS):
                transpose_weights(0, 0, 0, job, first=True)
            pe.wait_ge(gate_done, 1)
            for tc in range(TC):
                for c in range(DC):
                    mm = three(ps_y[0:E, tc, :], gate_hi[:, c, :], gate_lo[:, c, :], xt_hi[:, c, tc * BANK:(tc + 1) * BANK],
                               xt_lo[:, c, tc * BANK:(tc + 1) * BANK], c == 0, c == DC - 1)
                mm.then_inc(logits_t_ps, 1)
            pe.wait_ge(logits_t_out, TC)
            for t in range(TILES):
                tr = pe.transpose(ps_y[:, 0, t * E:(t + 1) * E], gated[t // TPC][0:E, t % TPC * P:(t % TPC + 1) * P], ident[0:E, 0:E])
            tr.then_inc(logits_ps, 1)
            pe.wait_ge(logits_out, 1)
            expert(None, 0, 0, 0)
            with pe.Fori(0, N // 2 - 1) as i:
                expert(2 * i, 2 * i + 1, 1, i + 1)
                expert(2 * i + 1, 2 * i + 2, 0, i + 1)
            expert(N - 2, N - 1, 1, None, following=False)
            for t in range(2, TILES):
                down(N - 1, None, 1, t)

        @block.scalar
        def _(act):
            def weights_hi(n, a, job):
                bank = ps_t[:, (JOBS * a + job) % 2, :]
                act.wait_ge(w_ps, JOBS * n + job + 1)
                if job == 2:
                    act.activation(down_hi[a][:, :], bank, ACT.Copy).then_inc(w_hi_done, 1)
                else:
                    act.activation(up_hi[a][:, job, :, :], by_chunk(bank), ACT.Copy).then_inc(w_hi_done, 1)

            def hidden(n, last, tc):
                act.wait_ge(h_ps, TC * n + tc + 1)
                if tc == 1:
                    act.wait_ge(act_done, TC * n + 1)
                elif last is not None:
                    act.wait_ge(act_done, TC * last + 1)
                act.activation(gated[tc][:, :], ps_h[:, tc, 0, :], ACT.Silu).then_inc(silu_done, 1)
                act.wait_ge(gated_done, TC * n + tc + 1)
                if tc == 1:
                    act.wait_ge(y_ps, TILES * n + 1)
                elif last is not None:
                    act.wait_ge(y_ps, TILES * last + TPC)
                act.activation(act_hi[:, tc, :], gated[tc][:, :], ACT.Copy).then_inc(act_hi_done, 1)

            def expert(last, n, a, following=True):
                if last is not None:
                    hidden(last, None, 1)
                if following:
                    weights_hi(n + 1, 1 - a, 0)
                    weights_hi(n + 1, 1 - a, 1)
                hidden(n, last, 0)
                if following:
                    weights_hi(n + 1, 1 - a, 2)

            for t in range(TILES):
                act.wait_ge(xt_ps, t + 1)
                act.activation(xt_hi[:, :, t * P:(t + 1) * P], by_chunk(ps_t[:, t % 2, :]), ACT.Copy).then_inc(xt_hi_done, 1)
            act.wait_ge(gate_ps, 1)
            act.activation(gate_hi[:, :, :], ps_h[:, 0, 0, 0:DC * E].rearrange("p (c e) -> p c e", c=DC), ACT.Copy).then_inc(gate_hi_done, 1)
            for job in range(JOBS):
                weights_hi(0, 0, job)
            for tc in range(TC):
                act.wait_ge(logits_t_ps, tc + 1)
                act.activation(gated[tc][0:E, :], ps_y[0:E, tc, :], ACT.Copy).then_inc(logits_t_out, 1)
            act.wait_ge(centred, 1)
            act.activation(scores[:, :, :], scores[:, :, :], ACT.Exp).then_inc(exp_done, 1)
            act.wait_ge(logits_ps, 1)
            expert(None, 0, 0)
            with act.Fori(0, N // 2 - 1) as i:
                expert(2 * i, 2 * i + 1, 1)
                expert(2 * i + 1, 2 * i + 2, 0)
            expert(N - 2, N - 1, 1, following=False)
            hidden(N - 1, None, 1)

        @block.vector
        def _(dve):
            chain = Chain(dve, router)

            def weights_lo(n, a, job):
                bank = ps_t[:, (JOBS * a + job) % 2, :]
                dve.wait_ge(w_hi_done, JOBS * n + job + 1)
                if job == 2:
                    dve.tensor_tensor(down_lo[a][:, :], bank, down_hi[a][:, :].bitcast(F32), ALU.subtract).then_inc(w_done, 1)
                else:
                    dve.tensor_tensor(up_lo[a][:, job, :, :], by_chunk(bank), up_hi[a][:, job, :, :].bitcast(F32),
                                      ALU.subtract).then_inc(w_done, 1)

            def product(n, tc):
                dve.wait_ge(silu_done, TC * n + tc + 1)
                dve.tensor_tensor(gated[tc][:, :], ps_h[:, tc, 1, :], gated[tc][:, :], ALU.mult).then_inc(gated_done, 1)

            def product_lo(n, tc):
                dve.wait_ge(act_hi_done, TC * n + tc + 1)
                dve.tensor_tensor(act_lo[:, tc, :], gated[tc][:, :], act_hi[:, tc, :].bitcast(F32), ALU.subtract).then_inc(act_done, 1)

            def add(n, last, t):
                dve.wait_ge(y_ps, TILES * n + t + 1)
                if t >= 2:
                    dve.wait_ge(added, TILES * n + 1)
                elif last is not None:
                    dve.wait_ge(added, TILES * last + t + 1)
                weight = share[:, t, n:n + 1] if isinstance(n, int) else share[:, t, bass.ds(n, 1)]
                dve.scalar_tensor_tensor(x_res[:, t, :], ps_y[:, t % 2, :], weight, x_res[:, t, :],
                                         ALU.mult, ALU.add).then_inc(added, 1)

            def expert(last, n, a, following=True):
                if last is not None:
                    product(last, 1)
                    add(last, None, 2)
                    product_lo(last, 1)
                if following:
                    weights_lo(n + 1, 1 - a, 0)
                if last is not None:
                    add(last, None, 3)
                    add(last, None, 4)
                if following:
                    weights_lo(n + 1, 1 - a, 1)
                product(n, 0)
                if last is not None:
                    add(last, None, 5)
                product_lo(n, 0)
                if last is not None:
                    add(last, None, 6)
                    add(last, None, 7)
                add(n, last, 0)
                if following:
                    weights_lo(n + 1, 1 - a, 2)
                add(n, last, 1)

            for t in range(TILES):
                dve.wait_ge(xt_hi_done, t + 1)
                dve.tensor_tensor(xt_lo[:, :, t * P:(t + 1) * P], by_chunk(ps_t[:, t % 2, :]),
                                  xt_hi[:, :, t * P:(t + 1) * P].bitcast(F32), ALU.subtract).then_inc(xt_done, 1)
            dve.wait_ge(gate_hi_done, 1)
            dve.tensor_tensor(gate_lo[:, :, :], ps_h[:, 0, 0, 0:DC * E].rearrange("p (c e) -> p c e", c=DC),
                              gate_hi[:, :, :].bitcast(F32), ALU.subtract).then_inc(gate_done, 1)
            for job in range(JOBS):
                weights_lo(0, 0, job)
            dve.wait_ge(logits_ps, 1)
            dve.tensor_copy(logits[:, :, :], ps_y[:, 0, 0:TILES * E].rearrange("p (t e) -> p t e", t=TILES)).then_inc(logits_out, 1)
            dve.wait_ge(logits_out, 1)
            softmax_rows(dve, chain, scores[:, :, :], logits[:, :, :], row[:, :], row2[:, :], exp_done, centred)
            dve.wait_ge(pads_set, 2)
            top_two(dve, chain, scores[:, :, :], ramp[:, :], hit[:, :, :], first[:, :, :], second[:, :, :], rest[:, :, :],
                    row[:, :], best[:, :], runner[:, :])
            chain.link(dve.tensor_tensor(row[:, :], best[:, :], runner[:, :], ALU.add))
            chain.link(dve.reciprocal(row[:, :], row[:, :]))
            chain.link(dve.tensor_tensor(best[:, :], best[:, :], row[:, :], ALU.mult))
            chain.link(dve.tensor_tensor(runner[:, :], runner[:, :], row[:, :], ALU.mult))
            chain.link(dve.tensor_tensor(first[:, :, :], first[:, :, :], wide(best[:, :], E), ALU.mult))
            chain.link(dve.tensor_tensor(second[:, :, :], second[:, :, :], wide(runner[:, :], E), ALU.mult))
            chain.link(dve.tensor_tensor(share[:, :, 0:E], first[:, :, :], second[:, :, :], ALU.add))
            expert(None, 0, 0)
            with dve.Fori(0, N // 2 - 1) as i:
                expert(2 * i, 2 * i + 1, 1)
                expert(2 * i + 1, 2 * i + 2, 0)
            expert(N - 2, N - 1, 1, following=False)
            product(N - 1, 1)
            add(N - 1, None, 2)
            product_lo(N - 1, 1)
            for t in range(3, TILES):
                add(N - 1, None, t)


def layers(nc, x, ctx_4096, L0_xattn_Wq, L0_xattn_Wk, L0_xattn_Wv, L0_xattn_Wo, L0_ffn_gate_w, L0_ffn_gate_b, L0_ffn_w1,
           L0_ffn_b1, L0_ffn_w2, L0_ffn_b2, L1_xattn_Wq_w, L1_xattn_Wq_b, L1_xattn_Wk_w, L1_xattn_Wk_b, L1_xattn_fn_w,
           L1_xattn_qn_w, L1_xattn_kn_w, L1_ffn_gate_w, L1_ffn_w_gate_up, L1_ffn_w_down, L1_ffn_shared_w_gate_up,
           L1_ffn_shared_w_down, out):
    B, S, D = x.shape
    held = []
    with ExitStack() as ctx:
        sb = lambda n, s: ctx.enter_context(nc.sbuf_tensor(n, s, F32))
        x_res, xn = sb("x_res", [P, B * S // P, D]), sb("xn", [P, B * S // P, D])
        stats = sb("stats", [P, B * S // P, 6])
        ident, ones = sb("ident", [P, P]), sb("ones", [P, P])
        grouped_attention_block(nc, held, x, ctx_4096, L0_xattn_Wq, L0_xattn_Wk, L0_xattn_Wv, L0_xattn_Wo, x_res, xn, stats, ident, ones)
        release(nc, held)
        norm_block(nc, held, x_res, xn, stats, 1e-5, "norm1")
        gated_experts_block(nc, held, L0_ffn_gate_w, L0_ffn_gate_b, L0_ffn_w1, L0_ffn_b1, L0_ffn_w2, L0_ffn_b2, x_res, xn, stats, ident,
                            ones, B)
        release(nc, held)
        normed_attention_block(nc, held, ctx_4096, L1_xattn_Wq_w, L1_xattn_Wq_b, L1_xattn_Wk_w, L1_xattn_Wk_b, L1_xattn_fn_w,
                               L1_xattn_qn_w, L1_xattn_kn_w, x_res, xn, stats, ident, ones)
        release(nc, held)
        norm_block(nc, held, x_res, xn, stats, 1e-5, "norm3")
        routed_experts_block(nc, held, L1_ffn_gate_w, L1_ffn_w_gate_up, L1_ffn_w_down, L1_ffn_shared_w_gate_up,
                             L1_ffn_shared_w_down, x_res, xn, ident, ones, out)


_INS = ["x", "ctx_4096", "L0_xattn_Wq", "L0_xattn_Wk", "L0_xattn_Wv", "L0_xattn_Wo", "L0_ffn_gate_w", "L0_ffn_gate_b",
        "L0_ffn_w1", "L0_ffn_b1", "L0_ffn_w2", "L0_ffn_b2", "L1_xattn_Wq_w", "L1_xattn_Wq_b", "L1_xattn_Wk_w",
        "L1_xattn_Wk_b", "L1_xattn_fn_w", "L1_xattn_qn_w", "L1_xattn_kn_w", "L1_ffn_gate_w", "L1_ffn_w_gate_up",
        "L1_ffn_w_down", "L1_ffn_shared_w_gate_up", "L1_ffn_shared_w_down"]


def kernel(**inputs):
    import concourse.bacc as _bacc
    import numpy as _np
    from concourse.bass_utils import run_bass_kernel_spmd as _run

    nc = _bacc.Bacc("TRN2", target_bir_lowering=False, num_devices=1)
    arrays, args = {}, []
    for name in _INS:
        a = _np.ascontiguousarray(inputs[name])
        arrays[f"in_{name}"] = a
        args.append(nc.dram_tensor(f"in_{name}", a.shape, mybir.dt.from_np(a.dtype), kind="ExternalInput").ap())
    out = nc.dram_tensor("out_x", inputs["x"].shape, F32, kind="ExternalOutput").ap()
    layers(nc, *args, out)
    return _run(nc, [arrays], core_ids=[0]).results[0]["out_x"]
```
